# Optimizing a Trainium2 kernel written in Bass

```python
import numpy as np
import jax
import jax.numpy as jnp

def _softmax(x, axis=-1):
    return jax.nn.softmax(x, axis=axis)

def _gelu(x):
    return jax.nn.gelu(x, approximate=True)

def _silu(x):
    return jax.nn.silu(x)

def _sigmoid(x):
    return jax.nn.sigmoid(x)

def _layernorm(x, axis=-1, eps=1e-05):
    m = jnp.mean(x, axis=axis, keepdims=True)
    v = jnp.var(x, axis=axis, keepdims=True)
    return (x - m) / jnp.sqrt(v + eps)

def _scatter_add(tgt, idx, src, axis=0):
    return tgt.at[idx].add(src)

def _segment_sum(src, seg, n):
    return jax.ops.segment_sum(src, seg, n)
kernel_name = 'mk_sandwich_d1_jaxref_r8_9ef7e9'

def setup_inputs(seed: int=0):
    np.random.seed(seed)
    _w = jnp.asarray

    def _L0_attn_setup():
        import jax, jax.numpy as jnp
        import numpy as np
        B, N, H = (4, 512, 128)
        NUM_HEADS = 16
        HEAD_DIM = H // NUM_HEADS
        EPS = 1e-05

        def _layernorm(x, g, b):
            mu = jnp.mean(x, axis=-1, keepdims=True)
            var = jnp.mean(jnp.square(x - mu), axis=-1, keepdims=True)
            return (x - mu) * jax.lax.rsqrt(var + EPS) * g + b
        key = jax.random.key(seed)
        ks = jax.random.split(key, 12)
        s = 0.02
        return {'x': jax.random.normal(ks[0], (B, N, H), dtype=jnp.float32), 'w_qkv': jax.random.normal(ks[1], (3 * H, H), dtype=jnp.float32) * s, 'b_qkv': jax.random.normal(ks[2], (3 * H,), dtype=jnp.float32) * s, 'w_g1': jax.random.normal(ks[3], (HEAD_DIM, H), dtype=jnp.float32) * s, 'b_g1': jax.random.normal(ks[4], (HEAD_DIM,), dtype=jnp.float32) * s, 'w_g2': jax.random.normal(ks[5], (H, HEAD_DIM), dtype=jnp.float32) * s, 'b_g2': jax.random.normal(ks[6], (H,), dtype=jnp.float32) * s, 'w_out': jax.random.normal(ks[7], (H, H), dtype=jnp.float32) * s, 'b_out': jax.random.normal(ks[8], (H,), dtype=jnp.float32) * s, 'ln_g': jnp.ones((H,), dtype=jnp.float32), 'ln_b': jnp.zeros((H,), dtype=jnp.float32)}
    _L0_attn_in = _L0_attn_setup()

    def _L0_ffn_setup():
        import jax, jax.numpy as jnp
        import numpy as np
        B, S, H = (4, 256, 128)
        E, K = (8, 2)
        I_R, I_S = (4 * H, 8 * H)
        CAP_FACTOR = 1.25
        SCALE = 1.0
        key = jax.random.key(seed)
        ks = jax.random.split(key, 9)
        std = 0.02
        return {'x': jax.random.normal(ks[0], (B, S, H), jnp.float32), 'router_w': std * jax.random.normal(ks[1], (E, H), jnp.float32), 'rg': std * jax.random.normal(ks[2], (E, H, I_R), jnp.float32), 'ru': std * jax.random.normal(ks[3], (E, H, I_R), jnp.float32), 'rd': std * jax.random.normal(ks[4], (E, I_R, H), jnp.float32), 'sg': std * jax.random.normal(ks[5], (H, I_S), jnp.float32), 'su': std * jax.random.normal(ks[6], (H, I_S), jnp.float32), 'sd': std * jax.random.normal(ks[7], (I_S, H), jnp.float32)}
    _L0_ffn_in = _L0_ffn_setup()
    _d = {'L0_attn_x': _L0_attn_in['x'], 'L0_attn_w_qkv': _L0_attn_in['w_qkv'], 'L0_attn_b_qkv': _L0_attn_in['b_qkv'], 'L0_attn_w_g1': _L0_attn_in['w_g1'], 'L0_attn_b_g1': _L0_attn_in['b_g1'], 'L0_attn_w_g2': _L0_attn_in['w_g2'], 'L0_attn_b_g2': _L0_attn_in['b_g2'], 'L0_attn_w_out': _L0_attn_in['w_out'], 'L0_attn_b_out': _L0_attn_in['b_out'], 'L0_attn_ln_g': _L0_attn_in['ln_g'], 'L0_attn_ln_b': _L0_attn_in['ln_b'], 'L0_ffn_router_w': _L0_ffn_in['router_w'], 'L0_ffn_rg': _L0_ffn_in['rg'], 'L0_ffn_ru': _L0_ffn_in['ru'], 'L0_ffn_rd': _L0_ffn_in['rd'], 'L0_ffn_sg': _L0_ffn_in['sg'], 'L0_ffn_su': _L0_ffn_in['su'], 'L0_ffn_sd': _L0_ffn_in['sd']}
    _x0 = _d['L0_attn_x']
    _d['L0_attn_x'] = jax.random.normal(jax.random.fold_in(jax.random.key(seed), 1), (16, 512, 128), dtype=_x0.dtype)
    del _x0
    return _d

def reference(L0_attn_x, L0_attn_w_qkv, L0_attn_b_qkv, L0_attn_w_g1, L0_attn_b_g1, L0_attn_w_g2, L0_attn_b_g2, L0_attn_w_out, L0_attn_b_out, L0_attn_ln_g, L0_attn_ln_b, L0_ffn_router_w, L0_ffn_rg, L0_ffn_ru, L0_ffn_rd, L0_ffn_sg, L0_ffn_su, L0_ffn_sd):

    def _L0_attn_ref(x, w_qkv, b_qkv, w_g1, b_g1, w_g2, b_g2, w_out, b_out, ln_g, ln_b):
        import jax, jax.numpy as jnp
        import numpy as np
        B, N, H = (4, 512, 128)
        NUM_HEADS = 16
        HEAD_DIM = H // NUM_HEADS
        EPS = 1e-05

        def _layernorm(x, g, b):
            mu = jnp.mean(x, axis=-1, keepdims=True)
            var = jnp.mean(jnp.square(x - mu), axis=-1, keepdims=True)
            return (x - mu) * jax.lax.rsqrt(var + EPS) * g + b
        b, n, hdim = x.shape
        qkv = jnp.einsum('bnh,oh->bno', x, w_qkv) + b_qkv
        q, k, v = jnp.split(qkv, 3, axis=-1)

        def split_heads(t):
            return t.reshape(b, n, NUM_HEADS, HEAD_DIM).transpose(0, 2, 1, 3)
        q, k, v = (split_heads(q), split_heads(k), split_heads(v))
        q = jax.nn.silu(q)
        k = jax.nn.softmax(k, axis=-2)
        if n <= HEAD_DIM:
            attn = jnp.einsum('bhnd,bhmd->bhnm', q, k)
            out = jnp.einsum('bhnm,bhmd->bhnd', attn, v)
        else:
            kv = jnp.einsum('bhnd,bhne->bhde', k, v)
            out = jnp.einsum('bhnd,bhde->bhne', q, kv)
        out = out.transpose(0, 2, 1, 3).reshape(b, n, hdim)
        out = _layernorm(out, ln_g, ln_b)
        gate_hidden = jnp.einsum('bnh,dh->bnd', x, w_g1) + b_g1
        gate = jax.nn.sigmoid(jnp.einsum('bnd,hd->bnh', gate_hidden, w_g2) + b_g2)
        out = out * gate
        out = jnp.einsum('bnh,oh->bno', out, w_out) + b_out
        return out

    def _L0_ffn_ref(x, router_w, rg, ru, rd, sg, su, sd):
        import jax, jax.numpy as jnp
        import numpy as np
        B, S, H = (4, 256, 128)
        E, K = (8, 2)
        I_R, I_S = (4 * H, 8 * H)
        CAP_FACTOR = 1.25
        SCALE = 1.0
        b, s, h = x.shape
        T = b * s
        capacity = max(int(CAP_FACTOR * T / E), 1)
        xf = x.reshape(T, h)
        eps = jnp.finfo(x.dtype).eps
        xn = xf * jax.lax.rsqrt(jnp.mean(xf * xf, axis=-1, keepdims=True) + eps)
        logits = xn @ router_w.T
        probs = jax.nn.softmax(logits, axis=-1)
        topk_p, topk_i = jax.lax.top_k(probs, K)
        rw = topk_p / jnp.sum(topk_p, axis=-1, keepdims=True)
        one_hot = jax.nn.one_hot(topk_i, E, dtype=x.dtype)
        mask = one_hot.sum(1)
        wdense = (one_hot * rw[..., None]).sum(1)
        sel = mask.T.astype(bool)
        order = jnp.argsort(~sel, axis=1, stable=True)
        dispatch = order[:, :capacity]
        count = sel.sum(axis=1)
        valid = (jnp.arange(capacity)[None, :] < count[:, None]).astype(x.dtype)
        xg = xf[dispatch]
        gate = jax.nn.silu(jnp.einsum('ech,ehi->eci', xg, rg))
        up = jnp.einsum('ech,ehi->eci', xg, ru)
        eout = jnp.einsum('eci,eih->ech', gate * up, rd)
        w = jnp.take_along_axis(wdense.T, dispatch, axis=1)
        contrib = eout * (w * valid)[..., None]
        routed = jnp.zeros_like(xf).at[dispatch.reshape(-1)].add(contrib.reshape(-1, h))
        shared = jax.nn.silu(x @ sg) * (x @ su) @ sd
        return shared + SCALE * routed.reshape(b, s, h)
    x = L0_attn_x
    x = x + _layernorm(_L0_attn_ref(_layernorm(x, axis=-1), L0_attn_w_qkv, L0_attn_b_qkv, L0_attn_w_g1, L0_attn_b_g1, L0_attn_w_g2, L0_attn_b_g2, L0_attn_w_out, L0_attn_b_out, L0_attn_ln_g, L0_attn_ln_b), axis=-1)
    x = x + _layernorm(_L0_ffn_ref(_layernorm(x, axis=-1), L0_ffn_router_w, L0_ffn_rg, L0_ffn_ru, L0_ffn_rd, L0_ffn_sg, L0_ffn_su, L0_ffn_sd), axis=-1)
    return x

_drawn_inputs = setup_inputs


def setup_inputs(seed=0):
    import zlib

    import numpy as np

    out = dict(_drawn_inputs(seed))
    spreads = {'L0_attn_ln_g': (1.0, 0.2), 'L0_attn_ln_b': (0.0, 0.1)}
    factors = {'L0_attn_w_g1': 3.886, 'L0_attn_b_g1': 8.0, 'L0_attn_w_g2': 3.724, 'L0_attn_b_g2': 2.945}
    for name, (base, spread) in spreads.items():
        noise = np.random.default_rng([zlib.crc32(name.encode()), seed]).standard_normal(out[name].shape)
        drawn = base * np.exp(spread * noise) if base else spread * noise
        out[name] = jnp.asarray(drawn.astype(out[name].dtype))
    for name, factor in factors.items():
        out[name] = (out[name] * factor).astype(out[name].dtype)
    return out
```

```python
from contextlib import ExitStack

import concourse.bass as bass
from concourse import mybir

ALU = mybir.AluOpType
ACT = mybir.ActivationFunctionType
AX = mybir.AxisListType
F32 = mybir.dt.float32
F32R = mybir.dt.float32r
BF16 = mybir.dt.bfloat16
U32 = mybir.dt.uint32
ts = bass.ts
ds = bass.ds

P = 128
H = 128
LN_EPS = 1e-5
RMS_EPS = 1.1920929e-07
HEAD_DIM = 8


def build(nc, x, w_qkv_t, b_qkv, b_qkv_t, w_g1, b_g1, w_g2_t, b_g2, w_out_t, b_out, ln_g, ln_b,
          router_t, rg, ru, rd, sg, su, sd, out):
    B, N, _ = x.shape
    J = N // P
    E = rg.shape[0]
    IR = rg.shape[2]
    IS = sg.shape[1]
    CR = IR // P
    CS = IS // P
    CAP = max(int(1.25 * B * N / E), 1)
    SLOTS = E * CAP
    BLOCKS = [(a, min(N, CAP - a)) for a in range(0, CAP, N)]
    NBLK = len(BLOCKS)
    K = 2

    slot_x = nc.dram_tensor("slot_x", [SLOTS, H], F32, kind="Internal").ap()
    slot_y = nc.dram_tensor("slot_y", [SLOTS + 1, H], F32, kind="Internal").ap()

    with ExitStack() as ctx:
        def sb(name, shape, dt=F32):
            return ctx.enter_context(nc.sbuf_tensor(name, shape, dt))

        def sem(name):
            return ctx.enter_context(nc.semaphore(name))

        bank = [ctx.enter_context(nc.psum_tensor(f"bank{i}", [P, 512], F32)) for i in range(8)]

        passed = sem("passed")

        def alone(eng):
            eng.sem_inc(passed, 1)

        res = sb("res", [P, B * N])
        xf_hi = sb("xf_hi", [P, B * N], F32R)
        xf_lo = sb("xf_lo", [P, B * N], F32R)
        slots = sb("slots", [P, B * K * J], U32)
        wts = sb("wts", [P, B * K * J])
        ident = sb("ident", [P, P])
        mhalf = sb("mhalf", [P, 8])

        with ExitStack() as c1:
            def sb1(name, shape, dt=F32):
                return c1.enter_context(nc.sbuf_tensor(name, shape, dt))

            wqkv = sb1("wqkv", [P, 3 * H])
            wo = sb1("wo", [P, H])
            wo_half = sb1("wo_half", [P, H])
            g1 = sb1("g1", [8, H])
            g2 = sb1("g2", [8, H])
            wg = sb1("wg", [P, H])
            bqkv = sb1("bqkv", [P, 3])
            bg1 = sb1("bg1", [8, 1])
            bg2 = sb1("bg2", [P, 1])
            bg_half = sb1("bg_half", [P, 1])
            lng = sb1("lng", [P, 1])
            lnb = sb1("lnb", [P, 1])
            bv_row = sb1("bv_row", [P, H])
            bo_row = sb1("bo_row", [1, H])
            ones_row = sb1("ones_row", [1, P])
            wr = sb1("wr", [P, E])
            wr_hi = sb1("wr_hi", [P, E], F32R)
            wr_lo = sb1("wr_lo", [P, E], F32R)
            head_mask = sb1("head_mask", [P, H])
            zeros = sb1("zeros", [P, 1280])
            identb = sb1("identb", [P, P], BF16)
            before = sb1("before", [P, P], BF16)
            onesb = sb1("onesb", [P, P], BF16)
            expert_id = sb1("expert_id", [P, J * E])
            expert_base = sb1("expert_base", [P, J * E])
            st = sb1("st", [P, J * 6])
            mv = sb1("mv", [P, J * 2])
            ve = sb1("ve", [P, J])
            rstd = sb1("rstd", [P, J])
            st2 = sb1("st2", [P, J * 6])
            mv2 = sb1("mv2", [P, J * 2])
            ve2 = sb1("ve2", [P, J])
            rstd2 = sb1("rstd2", [P, J])
            ms = sb1("ms", [P, J])
            rms = sb1("rms", [P, J])
            xn = sb1("xn", [P, N])
            xn_t = sb1("xn_t", [P, N])
            q_t = sb1("q_t", [P, N])
            ek_t = sb1("ek_t", [P, N])
            ek = sb1("ek", [P, N])
            tg = sb1("tg", [P, N])
            kmax = sb1("kmax", [P, 1])
            kbias = sb1("kbias", [P, 1])
            ksum = sb1("ksum", [P, 1])
            rksum = sb1("rksum", [P, 1])
            a_t = sb1("a_t", [P, H])
            kv = sb1("kv", [P, H])
            kvm = sb1("kvm", [P, H])
            on = sb1("on", [P, N])
            oa = sb1("oa", [P, N])
            u = sb1("u", [P, N])
            yn = sb1("yn", [P, N])
            xf = sb1("xf", [P, N])
            lgt = sb1("lgt", [E, N])
            lg = sb1("lg", [P, J * E])
            top = sb1("top", [P, J * 8])
            topi = sb1("topi", [P, J * 8], U32)
            oh = sb1("oh", [P, K * J * E], BF16)
            mask = sb1("mask", [P, J * E], BF16)
            taken = sb1("taken", [P, E], F32)
            takenb = sb1("takenb", [P, E], BF16)
            newly = sb1("newly", [P, E], F32)
            rank = sb1("rank", [P, J * E])
            fits = sb1("fits", [P, J * E])
            place = sb1("place", [P, J * E])
            placed = sb1("placed", [P, J * E])
            picked = sb1("picked", [P, K * J * E])
            slotf = sb1("slotf", [P, K * J])
            slot_now = sb1("slot_now", [P, K * J], U32)
            dl = sb1("dl", [P, J])
            dls = sb1("dls", [P, J])
            tw = sb1("tw", [P, J])

            names = ("consts ident weights zeros_ready filled setup_dve wg_ready wg_psum wg_copied bg_ready "
                     "x_even x_odd stats1 mv1 rstd1 eps1 xn xnT_ps xnT q_ps k_ps g_ps kmax kbias exp silu tanh "
                     "ekT_ps ek aT_ps aT kv_ps kvn rksum kvm out_ps st2 mv2 eps2 rstd2 on onT_ps oa u y_ps "
                     "st3 mv3 eps3 rstd3 yn res st4 mv4 eps4 rstd4 ms rms xf xfT_ps xf_hi xf_lo "
                     "lgt_ps lgt lg_ps lg top topi oh mask newly taken takenb rank_ps rank fits placed0 "
                     "placed picked slotf slot_now slots dl dls tanhw wts1 wts "
                     "scattered_even scattered_odd").split()
            S = {n: sem(n) for n in names}
            NW = 15

            mv_mean = lambda t, j: t[:, 2 * j:2 * j + 1]
            var_of = lambda t: t[:, :].rearrange("p (j s) -> p j s", s=2)[:, :, 1]
            je = lambda t: t[:, :].rearrange("p (j e) -> p j e", e=E)

            block = c1.enter_context(nc.Block())

            @block.sync
            def _(sp):
                loads = [(wqkv[:, :], w_qkv_t), (wo[:, :], w_out_t), (g1[:, :], w_g1), (g2[:, :], w_g2_t),
                         (bqkv[:, :], b_qkv_t),
                         (bg1[:, :], b_g1.rearrange("(p o) -> p o", o=1)),
                         (bg2[:, :], b_g2.rearrange("(p o) -> p o", o=1)),
                         (lng[:, :], ln_g.rearrange("(p o) -> p o", o=1)),
                         (lnb[:, :], ln_b.rearrange("(p o) -> p o", o=1)),
                         (bv_row[:, :], b_qkv[2 * H:3 * H].rearrange("(o h) -> o h", o=1).broadcast_to([P, H])),
                         (bo_row[:, :], b_out.rearrange("(o h) -> o h", o=1)),
                         (wr[:, :], router_t)]

                def load_x(i, s):
                    sp.dma_start(res[:, ds(i * N, N)],
                                 x[ds(i, 1)].rearrange("b (p j) h -> p (b j h)", p=P)).then_inc(s, 16)

                load_x(0, S["x_even"])
                load_x(1, S["x_odd"])
                for dst, src in loads:
                    sp.dma_start(dst, src).then_inc(S["weights"], 16)
                sp.wait_ge(S["zeros_ready"], 1)
                for n in range(SLOTS * H // P // 1280):
                    sp.dma_start(slot_x.rearrange("(p r) h -> p (r h)", p=P)[:, n * 1280:(n + 1) * 1280],
                                 zeros[:, :]).then_inc(S["filled"], 16)
                sp.dma_start(slot_y[SLOTS:SLOTS + 1, :], zeros[0:1, 0:H]).then_inc(S["filled"], 16)
                with sp.Fori(1, B // 2) as h:
                    sp.wait_ge(S["mv1"], h * 2 - 1)
                    load_x(h * 2, S["x_even"])
                    sp.wait_ge(S["mv1"], h * 2)
                    load_x(h * 2 + 1, S["x_odd"])

            FILLS = SLOTS * H // P // 1280 + 1

            @block.gpsimd
            def _(g):
                g.memset(ident[:, :], 0.0).then_inc(S["consts"], 1)
                g.memset(identb[:, :], 0.0).then_inc(S["consts"], 1)
                g.memset(before[:, :], 1.0).then_inc(S["consts"], 1)
                g.memset(head_mask[:, :], 1.0).then_inc(S["consts"], 1)
                g.memset(mhalf[:, :], -0.5).then_inc(S["consts"], 1)
                g.wait_ge(S["consts"], 5)
                for t in (ident, identb):
                    g.affine_select(out=t[:, :], in_=t[:, :], compare_op=ALU.not_equal, fill=1.0, base=0,
                                    pattern=[[-1, P]], channel_multiplier=1).then_inc(S["ident"], 1)
                g.affine_select(out=before[:, :], in_=before[:, :], compare_op=ALU.is_ge, fill=0.0, base=-1,
                                pattern=[[1, P]], channel_multiplier=-1).then_inc(S["ident"], 1)
                hm = head_mask[:, :].rearrange("p (g r) -> p g r", r=HEAD_DIM)
                g.affine_select(out=hm, in_=hm, compare_op=ALU.is_ge, fill=0.0, base=0,
                                pattern=[[-HEAD_DIM, H // HEAD_DIM], [0, HEAD_DIM]],
                                channel_multiplier=1).then_inc(S["ident"], 1)
                g.wait_ge(S["ident"], 4)
                g.affine_select(out=hm, in_=hm, compare_op=ALU.is_ge, fill=0.0, base=HEAD_DIM - 1,
                                pattern=[[HEAD_DIM, H // HEAD_DIM], [0, HEAD_DIM]],
                                channel_multiplier=-1).then_inc(S["ident"], 1)
                g.iota(expert_id[:, :], pattern=[[0, J], [1, E]], base=0, channel_multiplier=0,
                       allow_small_or_imprecise_dtypes=True).then_inc(S["ident"], 1)
                g.iota(expert_base[:, :], pattern=[[0, J], [CAP, E]], base=-SLOTS, channel_multiplier=0,
                       allow_small_or_imprecise_dtypes=True).then_inc(S["ident"], 1)

                def rsqrt(mean_var, eps_out, r, have, eps_done, done, n):
                    g.wait_ge(have, n + 1)
                    alone(g)
                    g.tensor_scalar(eps_out[:, :], var_of(mean_var), LN_EPS, None, ALU.add).then_inc(eps_done, 1)
                    g.wait_ge(eps_done, n + 1)
                    g.tensor_tensor(r[:, :], eps_out[:, :], mhalf[:, 0:J], ALU.pow).then_inc(done, 1)

                def step(i, a, b):
                    if a:
                        rsqrt(mv, ve, rstd, S["mv1"], S["eps1"], S["rstd1"], i)
                    if b:
                        n = i - 1
                        rsqrt(mv2, ve2, rstd2, S["mv2"], S["eps2"], S["rstd2"], n)
                        rsqrt(mv2, ve2, rstd2, S["mv3"], S["eps3"], S["rstd3"], n)
                        rsqrt(mv2, ve2, rstd2, S["mv4"], S["eps4"], S["rstd4"], n)
                        g.wait_ge(S["rstd4"], n + 1)
                        g.tensor_tensor(ms[:, :], rstd2[:, :], rstd2[:, :], ALU.mult).then_inc(S["ms"], 1)
                        g.wait_ge(S["ms"], n * 3 + 1)
                        g.tensor_tensor(ve2[:, :], ms[:, :], var_of(mv2), ALU.mult).then_inc(S["ms"], 1)
                        g.wait_ge(S["ms"], n * 3 + 2)
                        alone(g)
                        g.tensor_scalar(ms[:, :], ve2[:, :], RMS_EPS, None, ALU.add).then_inc(S["ms"], 1)
                        g.wait_ge(S["ms"], n * 3 + 3)
                        g.tensor_tensor(rms[:, :], ms[:, :], mhalf[:, 0:J], ALU.pow).then_inc(S["rms"], 1)
                        g.wait_ge(S["slot_now"], n + 1)
                        g.wait_ge(S["xf"], n + 1)
                        alone(g)
                        for k in range(K):
                            for j in range(J):
                                c = k * J + j
                                g.indirect_dma_start(
                                    out=slot_x, out_offset=bass.IndirectOffsetOnAxis(ap=slot_now[:, c:c + 1], axis=0),
                                    in_=xf[:, j * H:(j + 1) * H], in_offset=None,
                                    bounds_check=SLOTS - 1, oob_is_err=False).then_inc(S["scattered_even"], 16)

                g.wait_ge(S["ident"], 7)
                step(0, True, False)
                g.wait_ge(S["filled"], 16 * FILLS)
                with g.Fori(1, B) as i:
                    step(i, True, True)
                step(B, False, True)
                g.wait_ge(S["scattered_even"], 16 * B * K * J)

            @block.scalar
            def _(act):
                act.wait_ge(S["weights"], 12 * 16)
                nc.scalar.activation(wr_hi[:, :], wr[:, :], ACT.Copy).then_inc(S["wg_ready"], 1)
                nc.scalar.mul(wo_half[:, :], wo[:, :], 0.5).then_inc(S["wg_ready"], 1)

                def a_step(i):
                    act.wait_ge(S["xnT_ps"], i + 1)
                    nc.scalar.activation(xn_t[:, :], bank[0][:, :], ACT.Copy).then_inc(S["xnT"], 1)

                def affine(n):
                    act.wait_ge(S["onT_ps"], n + 1)
                    nc.scalar.activation(oa[:, :], bank[4][:, :], ACT.Identity, bias=lnb[:, 0:1],
                                         scale=lng[:, 0:1]).then_inc(S["oa"], 1)

                def a_step2(i, warm):
                    act.wait_ge(S["kbias"], i + 1)
                    nc.scalar.activation(ek_t[:, :], bank[2][:, :], ACT.Exp, bias=kbias[:, 0:1], scale=1.0,
                                         accum_out=ksum[:, 0:1]).then_inc(S["exp"], 1)
                    act.wait_ge(S["q_ps"], i + 1)
                    nc.scalar.activation(q_t[:, :], bank[1][:, :], ACT.Silu, bias=bqkv[:, 0:1],
                                         scale=1.0).then_inc(S["silu"], 1)
                    act.wait_ge(S["g_ps"], i + 1)
                    if warm:
                        act.wait_ge(S["u"], i)
                    nc.scalar.activation(tg[:, :], bank[3][:, :], ACT.Tanh, bias=bg_half[:, 0:1],
                                         scale=0.5).then_inc(S["tanh"], 1)
                    act.wait_ge(S["ekT_ps"], i + 1)
                    nc.scalar.activation(ek[:, :], bank[4][:, :], ACT.Copy).then_inc(S["ek"], 1)

                def b_step(n):
                    act.wait_ge(S["xfT_ps"], n + 1)
                    nc.scalar.activation(xf_hi[:, ds(n * N, N)], bank[0][:, :], ACT.Copy).then_inc(S["xf_hi"], 1)
                    act.wait_ge(S["lgt_ps"], n + 1)
                    nc.scalar.activation(lgt[:, :], bank[1][0:E, :], ACT.Copy).then_inc(S["lgt"], 1)
                    act.wait_ge(S["dls"], n + 1)
                    nc.scalar.activation(tw[:, :], dls[:, :], ACT.Tanh, scale=0.5).then_inc(S["tanhw"], 1)

                act.wait_ge(S["bg_ready"], 1)
                a_step(0)
                a_step2(0, False)
                with act.Fori(1, B) as i:
                    a_step(i)
                    affine(i - 1)
                    a_step2(i, True)
                    b_step(i - 1)
                affine(B - 1)
                b_step(B - 1)

            @block.vector
            def _(v):
                v.memset(zeros[:, :], 0.0).then_inc(S["zeros_ready"], 1)
                v.memset(onesb[:, :], 1.0).then_inc(S["setup_dve"], 1)
                v.memset(ones_row[:, :], 1.0).then_inc(S["setup_dve"], 1)
                v.memset(taken[:, :], 0.0).then_inc(S["setup_dve"], 1)
                v.memset(takenb[:, :], 0.0).then_inc(S["setup_dve"], 1)
                v.wait_ge(S["wg_ready"], 1)
                v.tensor_tensor(wr_lo[:, :], wr[:, :], wr_hi[:, :].bitcast(F32), ALU.subtract).then_inc(S["setup_dve"], 1)
                v.wait_ge(S["wg_psum"], 1)
                v.tensor_copy(wg[:, :], bank[7][:, 0:H]).then_inc(S["wg_copied"], 1)
                v.tensor_scalar(bg_half[:, :], bank[7][:, H:H + 1], bg2[:, 0:1], 0.5, ALU.add,
                                ALU.mult).then_inc(S["bg_ready"], 1)

                def stats(src, t, m, st_done, mv_done, n):
                    alone(v)
                    for j in range(J):
                        o = v.bn_stats(t[:, 6 * j:6 * j + 6], src(j))
                    o.then_inc(st_done, 1)
                    v.wait_ge(st_done, n + 1)
                    alone(v)
                    for j in range(J):
                        o = v.bn_aggr(m[:, 2 * j:2 * j + 2], t[:, 6 * j:6 * j + 6])
                    o.then_inc(mv_done, 1)

                def normalise(dst, src, m, r, done):
                    for j in range(J):
                        o = v.tensor_scalar(dst[:, j * H:(j + 1) * H], src(j), mv_mean(m, j), r[:, j:j + 1],
                                            ALU.subtract, ALU.mult)
                    o.then_inc(done, 1)

                def a1(i, x_sem, count, warm):
                    v.wait_ge(x_sem, count)
                    src = lambda j: res[:, ds(i * N + j * H, H)]
                    stats(src, st, mv, S["stats1"], S["mv1"], i)

                def a2(i, warm):
                    src = lambda j: res[:, ds(i * N + j * H, H)]
                    v.wait_ge(S["rstd1"], i + 1)
                    if warm:
                        v.wait_ge(S["aT_ps"], i)
                    normalise(xn, src, mv, rstd, S["xn"])

                def a3(i):
                    v.wait_ge(S["k_ps"], i + 1)
                    v.tensor_reduce(kmax[:, :], bank[2][:, :], AX.X, ALU.max, negate=True).then_inc(S["kmax"], 1)
                    v.wait_ge(S["kmax"], i + 1)
                    v.tensor_scalar(kbias[:, :], kmax[:, :], bqkv[:, 1:2], bqkv[:, 1:2], ALU.subtract,
                                    ALU.add).then_inc(S["kbias"], 1)

                def a4(i):
                    v.wait_ge(S["aT_ps"], i + 1)
                    v.tensor_copy(a_t[:, :], bank[7][:, 0:H]).then_inc(S["aT"], 1)
                    v.wait_ge(S["exp"], i + 1)
                    v.reciprocal(rksum[:, :], ksum[:, :]).then_inc(S["rksum"], 1)

                def a5(i, warm):
                    v.wait_ge(S["kv_ps"], i + 1)
                    v.wait_ge(S["rksum"], i + 1)
                    v.scalar_tensor_tensor(out=kv[:, :], in0=bank[7][:, 0:H], scalar=rksum[:, 0:1],
                                           in1=bv_row[:, :], op0=ALU.mult, op1=ALU.add).then_inc(S["kvn"], 1)
                    v.wait_ge(S["kvn"], i + 1)
                    if warm:
                        v.wait_ge(S["out_ps"], i)
                    v.tensor_tensor(kvm[:, :], kv[:, :], head_mask[:, :], ALU.mult).then_inc(S["kvm"], 1)

                def b1(n):
                    v.wait_ge(S["out_ps"], n + 1)
                    stats(lambda j: bank[5][:, j * H:(j + 1) * H], st2, mv2, S["st2"], S["mv2"], n)

                def b2(n):
                    v.wait_ge(S["rstd2"], n + 1)
                    normalise(on, lambda j: bank[5][:, j * H:(j + 1) * H], mv2, rstd2, S["on"])

                def b3(n):
                    v.wait_ge(S["oa"], n + 1)
                    v.wait_ge(S["tanh"], n + 1)
                    v.scalar_tensor_tensor(out=u[:, :], in0=tg[:, :], scalar=1.0, in1=oa[:, :],
                                           op0=ALU.add, op1=ALU.mult).then_inc(S["u"], 1)

                def b4(n):
                    v.wait_ge(S["y_ps"], n + 1)
                    stats(lambda j: bank[6][:, j * H:(j + 1) * H], st2, mv2, S["st3"], S["mv3"], n)

                def b5(n):
                    v.wait_ge(S["rstd3"], n + 1)
                    normalise(yn, lambda j: bank[6][:, j * H:(j + 1) * H], mv2, rstd2, S["yn"])
                    v.wait_ge(S["yn"], n + 1)
                    v.tensor_tensor(res[:, ds(n * N, N)], res[:, ds(n * N, N)], yn[:, :], ALU.add).then_inc(S["res"], 1)
                    v.wait_ge(S["res"], n + 1)
                    stats(lambda j: res[:, ds(n * N + j * H, H)], st2, mv2, S["st4"], S["mv4"], n)

                def b6(n, warm):
                    v.wait_ge(S["rstd4"], n + 1)
                    if warm:
                        v.wait_ge(S["scattered_even"], n * 16 * K * J)
                    normalise(xf, lambda j: res[:, ds(n * N + j * H, H)], mv2, rstd2, S["xf"])

                def b7(n):
                    v.wait_ge(S["xf_hi"], n + 1)
                    v.tensor_tensor(xf_lo[:, ds(n * N, N)], bank[0][:, :], xf_hi[:, ds(n * N, N)].bitcast(F32),
                                    ALU.subtract).then_inc(S["xf_lo"], 1)

                def c1_(n, warm):
                    v.wait_ge(S["lg_ps"], n + 1)
                    v.tensor_copy(lg[:, :], bank[7][:, 0:J * E]).then_inc(S["lg"], 1)
                    v.wait_ge(S["lg"], n + 1)
                    alone(v)
                    for j in range(J):
                        o = v.max(top[:, 8 * j:8 * j + 8], lg[:, E * j:E * j + E])
                    o.then_inc(S["top"], 1)
                    v.wait_ge(S["top"], n + 1)
                    alone(v)
                    for j in range(J):
                        o = v.max_index(topi[:, 8 * j:8 * j + 8], top[:, 8 * j:8 * j + 8], lg[:, E * j:E * j + E])
                    o.then_inc(S["topi"], 1)
                    t3 = top[:, :].rearrange("p (j r) -> p j r", r=8)
                    v.tensor_tensor(dl[:, :], t3[:, :, 0], t3[:, :, 1], ALU.subtract).then_inc(S["dl"], 1)
                    v.wait_ge(S["topi"], n + 1)
                    i3 = topi[:, :].rearrange("p (j r) -> p j r", r=8)
                    for k in range(K):
                        o = v.tensor_tensor(je(oh[:, k * J * E:(k + 1) * J * E]), je(expert_id[:, :]),
                                            i3[:, :, k:k + 1].broadcast_to([P, J, E]), ALU.is_equal)
                    o.then_inc(S["oh"], 1)
                    v.wait_ge(S["dl"], n + 1)
                    v.wait_ge(S["rms"], n + 1)
                    v.tensor_tensor(dls[:, :], dl[:, :], rms[:, :], ALU.mult).then_inc(S["dls"], 1)
                    v.wait_ge(S["oh"], n + 1)
                    v.tensor_tensor(mask[:, :], oh[:, 0:J * E], oh[:, J * E:], ALU.add).then_inc(S["mask"], 1)

                def c2(n):
                    v.wait_ge(S["rank_ps"], n + 1)
                    v.wait_ge(S["mask"], n + 1)
                    v.tensor_reduce(newly[:, :], mask[:, :].rearrange("p (j e) -> p e j", e=E), AX.X,
                                    ALU.add).then_inc(S["newly"], 1)
                    v.tensor_copy(rank[:, :], bank[7][:, 0:J * E]).then_inc(S["rank"], 1)
                    v.wait_ge(S["newly"], n + 1)
                    v.tensor_tensor(taken[:, :], taken[:, :], newly[:, :], ALU.add).then_inc(S["taken"], 1)
                    v.wait_ge(S["rank"], n + 1)
                    v.tensor_scalar(fits[:, :], rank[:, :], float(CAP), None, ALU.is_lt).then_inc(S["fits"], 1)
                    v.tensor_tensor(place[:, :], rank[:, :], expert_base[:, :], ALU.add).then_inc(S["placed0"], 1)
                    v.wait_ge(S["taken"], n + 1)
                    v.tensor_copy(takenb[:, :], taken[:, :]).then_inc(S["takenb"], 1)
                    v.wait_ge(S["placed0"], n + 1)
                    v.tensor_tensor(placed[:, :], place[:, :], fits[:, :], ALU.mult).then_inc(S["placed"], 1)
                    v.wait_ge(S["placed"], n + 1)
                    v.tensor_tensor(picked[:, :].rearrange("p (k c) -> p k c", k=K),
                                    placed[:, :].rearrange("p (o c) -> p o c", o=1).broadcast_to([P, K, J * E]),
                                    oh[:, :].rearrange("p (k c) -> p k c", k=K), ALU.mult).then_inc(S["picked"], 1)
                    v.wait_ge(S["picked"], n + 1)
                    v.tensor_reduce(slotf[:, :], picked[:, :].rearrange("p (c e) -> p c e", e=E), AX.X,
                                    ALU.add).then_inc(S["slotf"], 1)
                    v.wait_ge(S["slotf"], n + 1)
                    v.tensor_scalar(slot_now[:, :], slotf[:, :], float(SLOTS), None, ALU.add).then_inc(S["slot_now"], 1)
                    v.tensor_scalar(slots[:, ds(n * K * J, K * J)], slotf[:, :], float(SLOTS), None,
                                    ALU.add).then_inc(S["slots"], 1)
                    v.wait_ge(S["tanhw"], n + 1)
                    v.tensor_scalar(wts[:, ds(n * K * J, J)], tw[:, :], 0.5, 0.5, ALU.mult, ALU.add).then_inc(S["wts1"], 1)
                    v.tensor_scalar(wts[:, ds(n * K * J + J, J)], tw[:, :], -0.5, 0.5, ALU.mult,
                                    ALU.add).then_inc(S["wts"], 1)

                def both(i, x_sem, count, warm):
                    a1(i, x_sem, count, True)
                    b1(i - 1)
                    a2(i, True)
                    b2(i - 1)
                    b3(i - 1)
                    a3(i)
                    b4(i - 1)
                    b5(i - 1)
                    a4(i)
                    b6(i - 1, warm)
                    a5(i, True)
                    b7(i - 1)
                    c1_(i - 1, warm)
                    c2(i - 1)

                a1(0, S["x_even"], 16, False)
                v.wait_ge(S["ident"], 7)
                a2(0, False)
                a3(0)
                a4(0)
                a5(0, False)
                both(1, S["x_odd"], 16, False)
                with v.Fori(1, B // 2) as h:
                    both(h * 2, S["x_even"], h * 16 + 16, True)
                    both(h * 2 + 1, S["x_odd"], h * 16 + 16, True)
                n = B - 1
                b1(n)
                b2(n)
                b3(n)
                b4(n)
                b5(n)
                b6(n, True)
                b7(n)
                c1_(n, True)
                c2(n)

            @block.tensor
            def _(pe):
                mm = nc.tensor.matmul

                def transposes(dst, src):
                    for j in range(J):
                        o = nc.tensor.transpose(dst[:, j * P:(j + 1) * P], src[:, j * P:(j + 1) * P], ident[:, :])
                    return o

                pe.wait_ge(S["weights"], 12 * 16)
                mm(bank[7][:, 0:H], g1[:, :], g2[:, :], start=True, stop=True)
                mm(bank[7][:, H:H + 1], g2[:, :], bg1[:, :], start=True, stop=True).then_inc(S["wg_psum"], 1)

                def e1(i, warm):
                    pe.wait_ge(S["xn"], i + 1)
                    if warm:
                        pe.wait_ge(S["xf_lo"], i - 1)
                    transposes(bank[0], xn).then_inc(S["xnT_ps"], 1)

                def e7(n):
                    pe.wait_ge(S["on"], n + 1)
                    pe.wait_ge(S["ek"], n + 1)
                    transposes(bank[4], on).then_inc(S["onT_ps"], 1)

                def e2(i, warm, warm2):
                    pe.wait_ge(S["xnT"], i + 1)
                    if warm:
                        pe.wait_ge(S["exp"], i)
                    mm(bank[2][:, :], wqkv[:, H:2 * H], xn_t[:, :], start=True, stop=True).then_inc(S["k_ps"], 1)
                    if warm:
                        pe.wait_ge(S["silu"], i)
                    if warm2:
                        pe.wait_ge(S["lgt"], i - 1)
                    mm(bank[1][:, :], wqkv[:, 0:H], xn_t[:, :], start=True, stop=True).then_inc(S["q_ps"], 1)
                    if warm:
                        pe.wait_ge(S["tanh"], i)
                    mm(bank[3][:, :], wg[:, :], xn_t[:, :], start=True, stop=True).then_inc(S["g_ps"], 1)

                def e8(n):
                    pe.wait_ge(S["u"], n + 1)
                    mm(bank[6][:, :], ones_row[:, :], bo_row[:, :].rearrange("p (o h) -> p o h", o=1)
                       .broadcast_to([1, J, H]), start=True, stop=False, skip_group_check=True)
                    for j in range(J):
                        o = mm(bank[6][:, j * H:(j + 1) * H], u[:, j * P:(j + 1) * P], wo_half[:, :],
                               start=False, stop=(j == J - 1), skip_group_check=True)
                    o.then_inc(S["y_ps"], 1)

                def e3(i, warm):
                    pe.wait_ge(S["exp"], i + 1)
                    if warm:
                        pe.wait_ge(S["oa"], i)
                    transposes(bank[4], ek_t).then_inc(S["ekT_ps"], 1)

                def e4(i, warm):
                    pe.wait_ge(S["ek"], i + 1)
                    if warm:
                        pe.wait_ge(S["rank"], i - 1)
                    for j in range(J):
                        o = mm(bank[7][:, 0:H], xn[:, j * H:(j + 1) * H], ek[:, j * H:(j + 1) * H],
                               start=(j == 0), stop=(j == J - 1))
                    o.then_inc(S["aT_ps"], 1)

                def e5(i):
                    pe.wait_ge(S["aT"], i + 1)
                    mm(bank[7][:, 0:H], a_t[:, :], wqkv[:, 2 * H:3 * H], start=True, stop=True).then_inc(S["kv_ps"], 1)

                def e6(i, warm):
                    pe.wait_ge(S["kvm"], i + 1)
                    pe.wait_ge(S["silu"], i + 1)
                    if warm:
                        pe.wait_ge(S["on"], i)
                    for j in range(J):
                        o = mm(bank[5][:, j * H:(j + 1) * H], q_t[:, j * P:(j + 1) * P], kvm[:, :],
                               start=True, stop=True)
                    o.then_inc(S["out_ps"], 1)

                def e9(n):
                    pe.wait_ge(S["xf"], n + 1)
                    transposes(bank[0], xf).then_inc(S["xfT_ps"], 1)

                def e10(n):
                    pe.wait_ge(S["xf_lo"], n + 1)
                    hi, lo = xf_hi[:, ds(n * N, N)], xf_lo[:, ds(n * N, N)]
                    mm(bank[1][0:E, :], wr_lo[:, :], hi, start=True, stop=False)
                    mm(bank[1][0:E, :], wr_hi[:, :], lo, start=False, stop=False)
                    mm(bank[1][0:E, :], wr_hi[:, :], hi, start=False, stop=True).then_inc(S["lgt_ps"], 1)
                    pe.wait_ge(S["lgt"], n + 1)
                    alone(pe)
                    for j in range(J):
                        o = nc.tensor.transpose(bank[7][:, j * E:(j + 1) * E], lgt[:, j * P:(j + 1) * P],
                                                ident[0:E, 0:E])
                    o.then_inc(S["lg_ps"], 1)

                def e12(n, warm):
                    pe.wait_ge(S["mask"], n + 1)
                    if warm:
                        pe.wait_ge(S["takenb"], n)
                    r = je(bank[7][:, 0:J * E])
                    m = je(mask[:, :])
                    mm(r, onesb[:, :], takenb[:, :].rearrange("p (o e) -> p o e", o=1).broadcast_to([P, J, E]),
                       start=True, stop=False, skip_group_check=True)
                    for j in range(J):
                        o = mm(r, before[:, :], m[:, j:j + 1, :].broadcast_to([P, J, E]), start=False,
                               stop=(j == J - 1), skip_group_check=True)
                        if j < J - 1:
                            mm(r[:, j + 1:J, :], identb[:, :], m[:, j:j + 1, :].broadcast_to([P, J - 1 - j, E]),
                               start=False, stop=False, skip_group_check=True)
                    o.then_inc(S["rank_ps"], 1)

                def both(i, warm):
                    e1(i, warm)
                    e7(i - 1)
                    e2(i, True, warm)
                    e8(i - 1)
                    e3(i, True)
                    e4(i, warm)
                    e9(i - 1)
                    e5(i)
                    e6(i, True)
                    e10(i - 1)
                    e12(i - 1, warm)

                pe.wait_ge(S["ident"], 7)
                pe.wait_ge(S["wg_copied"], 1)
                pe.wait_ge(S["setup_dve"], 5)
                pe.wait_ge(S["wg_ready"], 2)
                pe.wait_ge(S["bg_ready"], 1)
                e1(0, False)
                e2(0, False, False)
                e3(0, False)
                e4(0, False)
                e5(0)
                e6(0, False)
                both(1, False)
                with pe.Fori(2, B) as i:
                    both(i, True)
                n = B - 1
                e7(n)
                e8(n)
                e9(n)
                e10(n)
                e12(n, True)

        LAG = 2
        RING = 4
        with ExitStack() as c2:
            def sb2(name, shape, dt=F32):
                return c2.enter_context(nc.sbuf_tensor(name, shape, dt))

            UPB = CR
            UPE = NBLK * CR
            W = CR * P
            raw = [sb2(f"raw{q}", [P, 3 * W]) for q in range(2)]
            w_hi = [sb2(f"w_hi{q}", [P, 3 * W], F32R) for q in range(2)]
            w_lo = [sb2(f"w_lo{q}", [P, 3 * W], F32R) for q in range(2)]
            xg = [sb2(f"xg{q}", [P, N]) for q in range(2)]
            xt_hi = [sb2(f"xt_hi{q}", [P, N], F32R) for q in range(2)]
            xt_lo = [sb2(f"xt_lo{q}", [P, N], F32R) for q in range(2)]
            gated = [sb2(f"gated{q}", [P, N]) for q in range(2)]
            hid = [sb2(f"hid{q}", [P, N]) for q in range(2)]
            h_hi = [sb2(f"h_hi{q}", [P, N], F32R) for q in range(RING)]
            h_lo = [sb2(f"h_lo{q}", [P, N], F32R) for q in range(RING)]
            y_t = [sb2(f"y_t{q}", [P, N]) for q in range(2)]
            y_rows = [sb2(f"y_rows{q}", [P, N]) for q in range(2)]
            gate_ps, up_ps, y_ps, xt_ps, yr_ps = bank[0:2], bank[2:4], bank[4:6], bank[6], bank[7]

            names = ("r_whi r_wlo r_xt_ps r_xt_hi r_xt_lo r_gate r_up r_silu r_hid r_hhi r_hlo r_down "
                     "r_yt r_yr_ps r_yr").split()
            R = {n: sem(n) for n in names}
            w_in = [sem(f"r_w_in{q}") for q in range(2)]
            x_in = [sem(f"r_x_in{q}") for q in range(2)]
            y_out = [sem(f"r_y_out{q}") for q in range(2)]

            PAIR = 2 * NBLK
            assert PAIR % 2 == 0 and NBLK * CR % RING == 0

            def size(k):
                return BLOCKS[k % NBLK][1]

            block = c2.enter_context(nc.Block())

            @block.sync
            def _(sp):
                def load_w(e, q):
                    for c, src in enumerate((rg, ru)):
                        sp.dma_start(raw[q][:, c * W:(c + 1) * W],
                                     src[ds(e, 1)].rearrange("e p i -> p (e i)")).then_inc(w_in[q], 16)
                    sp.dma_start(raw[q][:, 2 * W:3 * W].rearrange("p (c h) -> p c h", h=H),
                                 rd[ds(e, 1)].rearrange("e (c p) h -> p (e c) h", p=P)).then_inc(w_in[q], 16)

                def slot_rows(t, e, k):
                    a, n = BLOCKS[k % NBLK]
                    return t[ds(e * CAP + a, n)].rearrange("(p j) h -> p (j h)", p=P)

                def load_x(e, k):
                    sp.dma_start(xg[k % 2][:, 0:size(k)], slot_rows(slot_x, e, k)).then_inc(x_in[k % 2], 16)

                def store_y(m, k, cold):
                    sp.wait_ge(R["r_yr"], m * PAIR + k + 1)
                    sp.dma_start(slot_rows(slot_y, m * 2 + k // NBLK, k), y_rows[k % 2][:, 0:size(k)])\
                      .then_inc(y_out[k % 2], 16)

                load_w(0, 0)
                load_x(0, 0)
                load_x(0, 1)
                load_w(1, 1)

                def pair(m, first, last):
                    for k in range(PAIR):
                        nxt = k + 2
                        if not (last and nxt >= PAIR):
                            sp.wait_ge(R["r_xt_ps"], m * PAIR + k + 1)
                            load_x(m * 2 + nxt // NBLK, nxt)
                        if not (first and k < 1):
                            if k >= 1:
                                store_y(m, k - 1, first)
                            else:
                                store_y(m - 1, PAIR - 1, first)
                        if not last and k % NBLK == 1:
                            q = k // NBLK
                            sp.wait_ge(R["r_wlo"], m * 2 + q + 1)
                            sp.wait_ge(R["r_whi"], m * 2 + q + 1)
                            load_w(m * 2 + 2 + q, q)

                M = E // 2
                pair(0, True, False)
                with sp.Fori(1, M - 1) as m:
                    pair(m, False, False)
                pair(M - 1, False, True)
                store_y(M - 1, PAIR - 1, False)
                for q in range(2):
                    sp.wait_ge(y_out[q], 16 * E * NBLK // 2)

            def unit(m, c):
                return m * (2 * UPE) + c

            @block.scalar
            def _(act):
                def split_w(m, q, warm):
                    act.wait_ge(w_in[q], (m + 1) * 48)
                    if warm:
                        act.wait_ge(R["r_down"], unit(m - 1, (q + 1) * UPE))
                    nc.scalar.activation(w_hi[q][:, :], raw[q][:, :], ACT.Copy).then_inc(R["r_whi"], 1)

                def split_x(m, k, warm):
                    b = m * PAIR + k
                    act.wait_ge(R["r_xt_ps"], b + 1)
                    if warm or k >= 2:
                        act.wait_ge(R["r_up"], unit(m, (k - 1) * CR))
                    nc.scalar.activation(xt_hi[k % 2][:, 0:size(k)], xt_ps[:, 0:size(k)],
                                         ACT.Copy).then_inc(R["r_xt_hi"], 1)

                def silu(m, c, warm):
                    act.wait_ge(R["r_gate"], unit(m, c) + 1)
                    if warm or c >= 2:
                        act.wait_ge(R["r_hid"], unit(m, c) - 1)
                    n = size(c // CR)
                    nc.scalar.activation(gated[c % 2][:, 0:n], gate_ps[c % 2][:, 0:n], ACT.Silu).then_inc(R["r_silu"], 1)

                def high(m, c, warm):
                    act.wait_ge(R["r_hid"], unit(m, c) + 1)
                    if warm or c >= RING:
                        act.wait_ge(R["r_down"], unit(m, c) - RING + 1)
                    n = size(c % (2 * UPE) // CR)
                    nc.scalar.activation(h_hi[c % RING][:, 0:n], hid[c % 2][:, 0:n], ACT.Copy).then_inc(R["r_hhi"], 1)

                def y_copy(m, k, warm):
                    b = m * PAIR + k
                    act.wait_ge(R["r_down"], b * CR + CR)
                    if warm:
                        act.wait_ge(R["r_yr_ps"], b - 1)
                    n = size(k)
                    nc.scalar.activation(y_t[k % 2][:, 0:n], y_ps[k % 2][:, 0:n], ACT.Copy).then_inc(R["r_yt"], 1)

                def pair(m, first, last):
                    for c in range(2 * UPE):
                        k = c // CR
                        silu(m, c, not first)
                        if not (first and c < 1):
                            if c >= 1:
                                high(m, c - 1, not first)
                            else:
                                high(m - 1, 2 * UPE - 1, True)
                        if c % CR == 1 and not (last and k == PAIR - 1):
                            if k + 1 < PAIR:
                                split_x(m, k + 1, not first)
                            else:
                                split_x(m + 1, 0, True)
                        if c % CR == 3 and not (first and k == 0):
                            if k >= 1:
                                y_copy(m, k - 1, not first or k >= 3)
                            else:
                                y_copy(m - 1, PAIR - 1, True)
                        if c % UPE == UPE // 2:
                            q = c // UPE
                            if q == 0:
                                split_w(m, 1, not first)
                            elif not last:
                                split_w(m + 1, 0, True)

                M = E // 2
                split_w(0, 0, False)
                split_x(0, 0, False)
                pair(0, True, False)
                with act.Fori(1, M - 1) as m:
                    pair(m, False, False)
                pair(M - 1, False, True)
                high(M - 1, 2 * UPE - 1, True)
                y_copy(M - 1, PAIR - 1, True)

            @block.gpsimd
            def _(g):
                def low(m, c, warm):
                    g.wait_ge(R["r_hhi"], unit(m, c) + 1)
                    if warm or c >= RING:
                        g.wait_ge(R["r_down"], unit(m, c) - RING + 1)
                    n = size(c // CR)
                    g.tensor_tensor(h_lo[c % RING][:, 0:n], hid[c % 2][:, 0:n],
                                    h_hi[c % RING][:, 0:n].bitcast(F32), ALU.subtract).then_inc(R["r_hlo"], 1)

                for c in range(2 * UPE):
                    low(0, c, False)
                with g.Fori(1, E // 2) as m:
                    for c in range(2 * UPE):
                        low(m, c, True)

            @block.vector
            def _(v):
                def split_w(m, q, warm):
                    v.wait_ge(R["r_whi"], m * 2 + q + 1)
                    v.tensor_tensor(w_lo[q][:, :], raw[q][:, :], w_hi[q][:, :].bitcast(F32),
                                    ALU.subtract).then_inc(R["r_wlo"], 1)

                def split_x(m, k):
                    b = m * PAIR + k
                    v.wait_ge(R["r_xt_hi"], b + 1)
                    v.tensor_tensor(xt_lo[k % 2][:, 0:size(k)], xt_ps[:, 0:size(k)],
                                    xt_hi[k % 2][:, 0:size(k)].bitcast(F32), ALU.subtract).then_inc(R["r_xt_lo"], 1)

                def hidden(m, c, warm):
                    v.wait_ge(R["r_silu"], unit(m, c) + 1)
                    v.wait_ge(R["r_up"], unit(m, c) + 1)
                    if warm or c >= 2:
                        v.wait_ge(R["r_hlo"], unit(m, c) - 1)
                    n = size(c // CR)
                    v.tensor_tensor(hid[c % 2][:, 0:n], gated[c % 2][:, 0:n], up_ps[c % 2][:, 0:n],
                                    ALU.mult).then_inc(R["r_hid"], 1)

                def y_copy(m, k, warm):
                    b = m * PAIR + k
                    v.wait_ge(R["r_yr_ps"], b + 1)
                    if warm or k >= 2:
                        v.wait_ge(y_out[k % 2], (m * (PAIR // 2) + k // 2) * 16)
                    n = size(k)
                    v.tensor_copy(y_rows[k % 2][:, 0:n], yr_ps[:, 0:n]).then_inc(R["r_yr"], 1)

                def pair(m, first, last):
                    for c in range(2 * UPE):
                        k = c // CR
                        hidden(m, c, not first)
                        if c % CR == 1 and not (last and k == PAIR - 1):
                            if k + 1 < PAIR:
                                split_x(m, k + 1)
                            else:
                                split_x(m + 1, 0)
                        if c % CR == 0 and not (first and k < 2):
                            if k >= 2:
                                y_copy(m, k - 2, not first)
                            else:
                                y_copy(m - 1, PAIR - 2 + k, True)
                        if c % UPE == UPE // 2:
                            q = c // UPE
                            if q == 0:
                                split_w(m, 1, True)
                            elif not last:
                                split_w(m + 1, 0, True)

                M = E // 2
                split_w(0, 0, False)
                split_x(0, 0)
                pair(0, True, False)
                with v.Fori(1, M - 1) as m:
                    pair(m, False, False)
                pair(M - 1, False, True)
                y_copy(M - 1, PAIR - 2, True)
                y_copy(M - 1, PAIR - 1, True)

            @block.tensor
            def _(pe):
                mm = nc.tensor.matmul

                def x_in_t(m, k, warm):
                    n = size(k)
                    half = m * (PAIR // 2) + k // 2
                    pe.wait_ge(x_in[k % 2], half * 16 + 16)
                    if warm or k >= 1:
                        pe.wait_ge(R["r_xt_lo"], m * PAIR + k)
                    for j in range(n // P):
                        o = nc.tensor.transpose(xt_ps[:, j * P:(j + 1) * P], xg[k % 2][:, j * P:(j + 1) * P],
                                                ident[:, :])
                    o.then_inc(R["r_xt_ps"], 1)

                def product(dst, q, wa, a_hi, a_lo, start, stop):
                    mm(dst, w_lo[q][:, wa:wa + P], a_hi, start=start, stop=False)
                    mm(dst, w_hi[q][:, wa:wa + P], a_lo, start=False, stop=False)
                    return mm(dst, w_hi[q][:, wa:wa + P], a_hi, start=False, stop=stop)

                def gate_up(m, c, warm):
                    k, q = c // CR, c // UPE
                    n = size(k)
                    if c % CR == 0:
                        pe.wait_ge(R["r_xt_lo"], m * PAIR + k + 1)
                    if c % UPE == 0:
                        pe.wait_ge(R["r_wlo"], m * 2 + q + 1)
                    if warm or c >= 2:
                        pe.wait_ge(R["r_silu"], unit(m, c) - 1)
                    a = (xt_hi[k % 2][:, 0:n], xt_lo[k % 2][:, 0:n])
                    wa = (c % CR) * P
                    product(gate_ps[c % 2][:, 0:n], q, wa, *a, True, True).then_inc(R["r_gate"], 1)
                    if warm or c >= 2:
                        pe.wait_ge(R["r_hid"], unit(m, c) - 1)
                    product(up_ps[c % 2][:, 0:n], q, W + wa, *a, True, True).then_inc(R["r_up"], 1)

                def down(m, c, warm):
                    k, q = c // CR, c // UPE
                    n = size(k)
                    pe.wait_ge(R["r_hlo"], unit(m, c) + 1)
                    if c % CR == 0 and (warm or k >= 2):
                        pe.wait_ge(R["r_yt"], m * PAIR + k - 1)
                    product(y_ps[k % 2][:, 0:n], q, 2 * W + (c % CR) * P, h_hi[c % RING][:, 0:n],
                            h_lo[c % RING][:, 0:n], c % CR == 0, c % CR == CR - 1).then_inc(R["r_down"], 1)

                def y_in_rows(m, k, warm):
                    b = m * PAIR + k
                    pe.wait_ge(R["r_yt"], b + 1)
                    if warm or k >= 1:
                        pe.wait_ge(R["r_yr"], b)
                    for j in range(size(k) // P):
                        o = nc.tensor.transpose(yr_ps[:, j * P:(j + 1) * P], y_t[k % 2][:, j * P:(j + 1) * P],
                                                ident[:, :])
                    o.then_inc(R["r_yr_ps"], 1)

                def pair(m, first, last):
                    U = 2 * UPE
                    for c in range(U):
                        k = c // CR
                        gate_up(m, c, not first)
                        if c % CR == 0 and not (last and k == PAIR - 1):
                            if k + 1 < PAIR:
                                x_in_t(m, k + 1, True)
                            else:
                                x_in_t(m + 1, 0, True)
                        if c >= LAG:
                            down(m, c - LAG, not first)
                        elif not first:
                            down(m - 1, U + c - LAG, True)
                        if c % CR == CR - 1 and not (first and k == 0):
                            if k >= 1:
                                y_in_rows(m, k - 1, True)
                            else:
                                y_in_rows(m - 1, PAIR - 1, True)

                M = E // 2
                x_in_t(0, 0, False)
                pair(0, True, False)
                with pe.Fori(1, M - 1) as m:
                    pair(m, False, False)
                pair(M - 1, False, True)
                for c in range(2 * UPE - LAG, 2 * UPE):
                    down(M - 1, c, True)
                y_in_rows(M - 1, PAIR - 1, True)

        with ExitStack() as c3:
            def sb3(name, shape, dt=F32):
                return c3.enter_context(nc.sbuf_tensor(name, shape, dt))

            W = IS
            s_raw = sb3("s_raw", [P, 3 * W])
            s_hi = sb3("s_hi", [P, 3 * W], F32R)
            s_lo = sb3("s_lo", [P, 3 * W], F32R)
            gated = [sb3(f"s_gated{q}", [P, N]) for q in range(2)]
            hid = [sb3(f"s_hid{q}", [P, N]) for q in range(2)]
            h_hi = [sb3(f"s_h_hi{q}", [P, N], F32R) for q in range(RING)]
            h_lo = [sb3(f"s_h_lo{q}", [P, N], F32R) for q in range(RING)]
            y_t = sb3("s_y_t", [P, N])
            routed = [sb3(f"routed{k}", [P, N]) for k in range(K)]
            idx = sb3("idx", [P, K * J], U32)
            z1 = sb3("z1", [P, N])
            z2 = sb3("z2", [P, N])
            zn = sb3("zn", [P, N])
            st = sb3("s_st", [P, J * 6])
            mv = sb3("s_mv", [P, J * 2])
            ve = sb3("s_ve", [P, J])
            rstd = sb3("s_rstd", [P, J])
            fin = [sb3(f"fin{q}", [P, N]) for q in range(2)]
            gate_ps, up_ps, y_ps, yr_ps = bank[0:2], bank[2:4], bank[4], bank[6]

            names = ("s_w_in s_whi s_wlo s_gate s_up s_silu s_hid s_hhi s_hlo s_down s_yt s_yr_ps s_idx s_gathered "
                     "s_z1 s_z2 s_st s_mv s_eps s_rstd s_zn s_fin").split()
            Q = {n: sem(n) for n in names}
            stored = [sem(f"s_stored{q}") for q in range(2)]
            block = c3.enter_context(nc.Block())

            @block.sync
            def _(sp):
                sp.dma_start(s_raw[:, 0:W], sg).then_inc(Q["s_w_in"], 16)
                sp.dma_start(s_raw[:, W:2 * W], su).then_inc(Q["s_w_in"], 16)
                sp.dma_start(s_raw[:, 2 * W:].rearrange("p (c h) -> p c h", h=H),
                             sd.rearrange("(c p) h -> p c h", p=P)).then_inc(Q["s_w_in"], 16)

                def store(b, q, count):
                    sp.wait_ge(Q["s_fin"], count)
                    sp.dma_start(out[ds(b, 1)].rearrange("b (p j) h -> p (b j h)", p=P), fin[q][:, :])\
                      .then_inc(stored[q], 16)

                with sp.Fori(0, B // 2) as h:
                    for q in range(2):
                        store(h * 2 + q, q, h * 2 + q + 1)
                for q in range(2):
                    sp.wait_ge(stored[q], 16 * B // 2)

            @block.scalar
            def _(act):
                act.wait_ge(Q["s_w_in"], 48)
                nc.scalar.activation(s_hi[:, :], s_raw[:, :], ACT.Copy).then_inc(Q["s_whi"], 1)

                def silu(b, c, warm):
                    act.wait_ge(Q["s_gate"], b * CS + c + 1)
                    if warm or c >= 2:
                        act.wait_ge(Q["s_hid"], b * CS + c - 1)
                    nc.scalar.activation(gated[c % 2][:, :], gate_ps[c % 2][:, :], ACT.Silu).then_inc(Q["s_silu"], 1)

                def high(b, c, warm):
                    act.wait_ge(Q["s_hid"], b * CS + c + 1)
                    if warm or c >= RING:
                        act.wait_ge(Q["s_down"], b * CS + c - RING + 1)
                    nc.scalar.activation(h_hi[c % RING][:, :], hid[c % 2][:, :], ACT.Copy).then_inc(Q["s_hhi"], 1)

                def y_copy(b, warm):
                    act.wait_ge(Q["s_down"], b * CS + CS)
                    if warm:
                        act.wait_ge(Q["s_yr_ps"], b)
                    nc.scalar.activation(y_t[:, :], y_ps[:, :], ACT.Copy).then_inc(Q["s_yt"], 1)

                def step(b, first):
                    for c in range(CS):
                        silu(b, c, not first)
                        if c >= 1:
                            high(b, c - 1, not first)
                        elif not first:
                            high(b - 1, CS - 1, True)
                        if c == LAG and not first:
                            y_copy(b - 1, True)

                step(0, True)
                with act.Fori(1, B) as b:
                    step(b, False)
                high(B - 1, CS - 1, True)
                y_copy(B - 1, True)

            @block.gpsimd
            def _(g):
                def low(b, c, warm):
                    g.wait_ge(Q["s_hhi"], b * CS + c + 1)
                    if warm or c >= RING:
                        g.wait_ge(Q["s_down"], b * CS + c - RING + 1)
                    g.tensor_tensor(h_lo[c % RING][:, :], hid[c % 2][:, :], h_hi[c % RING][:, :].bitcast(F32),
                                    ALU.subtract).then_inc(Q["s_hlo"], 1)

                def gather(b, k, j):
                    c = k * J + j
                    g.indirect_dma_start(out=routed[k][:, j * H:(j + 1) * H], out_offset=None, in_=slot_y,
                                         in_offset=bass.IndirectOffsetOnAxis(ap=idx[:, c:c + 1], axis=0),
                                         bounds_check=SLOTS, oob_is_err=False).then_inc(Q["s_gathered"], 16)

                def rsqrt(b):
                    g.wait_ge(Q["s_mv"], b + 1)
                    alone(g)
                    g.tensor_scalar(ve[:, :], mv[:, :].rearrange("p (j s) -> p j s", s=2)[:, :, 1], LN_EPS, None,
                                    ALU.add).then_inc(Q["s_eps"], 1)
                    g.wait_ge(Q["s_eps"], b + 1)
                    g.tensor_tensor(rstd[:, :], ve[:, :], mhalf[:, 0:J], ALU.pow).then_inc(Q["s_rstd"], 1)

                def step(b, first):
                    for c in range(CS):
                        low(b, c, not first)
                        if c == 5 and not first:
                            rsqrt(b - 1)
                        if c == 6:
                            g.wait_ge(Q["s_idx"], b + 1)
                            if not first:
                                g.wait_ge(Q["s_z2"], b)
                            alone(g)
                        if c >= 6:
                            for j in range(J):
                                gather(b, c - 6, j)

                step(0, True)
                with g.Fori(1, B) as b:
                    step(b, False)
                rsqrt(B - 1)

            @block.vector
            def _(v):
                def hidden(b, c, warm):
                    v.wait_ge(Q["s_silu"], b * CS + c + 1)
                    v.wait_ge(Q["s_up"], b * CS + c + 1)
                    if warm or c >= 2:
                        v.wait_ge(Q["s_hlo"], b * CS + c - 1)
                    v.tensor_tensor(hid[c % 2][:, :], gated[c % 2][:, :], up_ps[c % 2][:, :],
                                    ALU.mult).then_inc(Q["s_hid"], 1)

                def index(b, warm):
                    if warm:
                        v.wait_ge(Q["s_gathered"], b * 16 * K * J)
                    v.tensor_copy(idx[:, :], slots[:, ds(b * K * J, K * J)]).then_inc(Q["s_idx"], 1)

                def mix(b):
                    v.wait_ge(Q["s_yr_ps"], b + 1)
                    v.wait_ge(Q["s_gathered"], b * 16 * K * J + 16 * K * J)
                    for j in range(J):
                        r = slice(j * H, (j + 1) * H)
                        o = v.scalar_tensor_tensor(out=z1[:, r], in0=routed[0][:, r],
                                                   scalar=wts[:, ds(b * K * J + j, 1)], in1=yr_ps[:, r],
                                                   op0=ALU.mult, op1=ALU.add)
                    o.then_inc(Q["s_z1"], 1)
                    v.wait_ge(Q["s_z1"], b + 1)
                    for j in range(J):
                        r = slice(j * H, (j + 1) * H)
                        o = v.scalar_tensor_tensor(out=z2[:, r], in0=routed[1][:, r],
                                                   scalar=wts[:, ds(b * K * J + J + j, 1)], in1=z1[:, r],
                                                   op0=ALU.mult, op1=ALU.add)
                    o.then_inc(Q["s_z2"], 1)

                def mix_stats(b):
                    v.wait_ge(Q["s_z2"], b + 1)
                    alone(v)
                    for j in range(J):
                        o = v.bn_stats(st[:, 6 * j:6 * j + 6], z2[:, j * H:(j + 1) * H])
                    o.then_inc(Q["s_st"], 1)
                    v.wait_ge(Q["s_st"], b + 1)
                    alone(v)
                    for j in range(J):
                        o = v.bn_aggr(mv[:, 2 * j:2 * j + 2], st[:, 6 * j:6 * j + 6])
                    o.then_inc(Q["s_mv"], 1)

                def final(b, q, stored_before):
                    v.wait_ge(Q["s_rstd"], b + 1)
                    for j in range(J):
                        r = slice(j * H, (j + 1) * H)
                        o = v.tensor_scalar(zn[:, r], z2[:, r], mv[:, 2 * j:2 * j + 1], rstd[:, j:j + 1],
                                            ALU.subtract, ALU.mult)
                    o.then_inc(Q["s_zn"], 1)
                    v.wait_ge(Q["s_zn"], b + 1)
                    if stored_before is not None:
                        v.wait_ge(stored[q], stored_before)
                    v.tensor_tensor(fin[q][:, :], zn[:, :], res[:, ds(b * N, N)], ALU.add).then_inc(Q["s_fin"], 1)

                def step(b, q, first, stored_before):
                    for c in range(CS):
                        hidden(b, c, not first)
                        if not first:
                            if c == 4:
                                mix(b - 1)
                            if c == 5:
                                mix_stats(b - 1)
                            if c == 7:
                                final(b - 1, q, stored_before)
                        if c == 4:
                            index(b, not first)

                v.wait_ge(Q["s_whi"], 1)
                v.tensor_tensor(s_lo[:, :], s_raw[:, :], s_hi[:, :].bitcast(F32), ALU.subtract).then_inc(Q["s_wlo"], 1)
                step(0, 1, True, None)
                step(1, 0, False, None)
                step(2, 1, False, None)
                step(3, 0, False, 16)
                with v.Fori(2, B // 2) as h:
                    step(h * 2, 1, False, h * 16 - 16)
                    step(h * 2 + 1, 0, False, h * 16)
                mix(B - 1)
                mix_stats(B - 1)
                final(B - 1, 1, (B // 2 - 1) * 16)

            @block.tensor
            def _(pe):
                mm = nc.tensor.matmul

                def product(dst, wa, a_hi, a_lo, start, stop):
                    mm(dst, s_lo[:, wa:wa + P], a_hi, start=start, stop=False)
                    mm(dst, s_hi[:, wa:wa + P], a_lo, start=False, stop=False)
                    return mm(dst, s_hi[:, wa:wa + P], a_hi, start=False, stop=stop)

                def gate_up(b, c, warm):
                    if warm or c >= 2:
                        pe.wait_ge(Q["s_silu"], b * CS + c - 1)
                    a = (xf_hi[:, ds(b * N, N)], xf_lo[:, ds(b * N, N)])
                    product(gate_ps[c % 2][:, :], c * P, *a, True, True).then_inc(Q["s_gate"], 1)
                    if warm or c >= 2:
                        pe.wait_ge(Q["s_hid"], b * CS + c - 1)
                    product(up_ps[c % 2][:, :], W + c * P, *a, True, True).then_inc(Q["s_up"], 1)

                def down(b, c, warm):
                    pe.wait_ge(Q["s_hlo"], b * CS + c + 1)
                    if c == 0 and warm:
                        pe.wait_ge(Q["s_yt"], b)
                    product(y_ps[:, :], 2 * W + c * P, h_hi[c % RING][:, :], h_lo[c % RING][:, :],
                            c == 0, c == CS - 1).then_inc(Q["s_down"], 1)

                def y_in_rows(b, warm):
                    pe.wait_ge(Q["s_yt"], b + 1)
                    if warm:
                        pe.wait_ge(Q["s_z1"], b)
                    for j in range(J):
                        o = nc.tensor.transpose(yr_ps[:, j * P:(j + 1) * P], y_t[:, j * P:(j + 1) * P], ident[:, :])
                    o.then_inc(Q["s_yr_ps"], 1)

                def step(b, first, second):
                    for c in range(CS):
                        gate_up(b, c, not first)
                        if c >= LAG:
                            down(b, c - LAG, not first)
                        elif not first:
                            down(b - 1, CS + c - LAG, not second)
                        if c == LAG + 1 and not first:
                            y_in_rows(b - 1, not second)

                pe.wait_ge(Q["s_wlo"], 1)
                step(0, True, False)
                step(1, False, True)
                with pe.Fori(2, B) as b:
                    step(b, False, False)
                for c in range(CS - LAG, CS):
                    down(B - 1, c, True)
                y_in_rows(B - 1, True)


def kernel(**inputs):
    import numpy as np
    import concourse.bacc as bacc
    from concourse.bass_utils import run_bass_kernel_spmd

    a = {n: np.ascontiguousarray(v) for n, v in inputs.items()}
    arrays = {
        "x": a["L0_attn_x"],
        "w_qkv_t": np.ascontiguousarray(a["L0_attn_w_qkv"].T),
        "b_qkv": a["L0_attn_b_qkv"],
        "b_qkv_t": np.ascontiguousarray(a["L0_attn_b_qkv"].reshape(3, H).T),
        "w_g1": a["L0_attn_w_g1"],
        "b_g1": a["L0_attn_b_g1"],
        "w_g2_t": np.ascontiguousarray(a["L0_attn_w_g2"].T),
        "b_g2": a["L0_attn_b_g2"],
        "w_out_t": np.ascontiguousarray(a["L0_attn_w_out"].T),
        "b_out": a["L0_attn_b_out"],
        "ln_g": a["L0_attn_ln_g"],
        "ln_b": a["L0_attn_ln_b"],
        "router_t": np.ascontiguousarray(a["L0_ffn_router_w"].T),
        "rg": a["L0_ffn_rg"],
        "ru": a["L0_ffn_ru"],
        "rd": a["L0_ffn_rd"],
        "sg": a["L0_ffn_sg"],
        "su": a["L0_ffn_su"],
        "sd": a["L0_ffn_sd"],
    }
    nc = bacc.Bacc("TRN2", target_bir_lowering=False, num_devices=1)
    args = [nc.dram_tensor(n, v.shape, F32, kind="ExternalInput").ap() for n, v in arrays.items()]
    out = nc.dram_tensor("out", arrays["x"].shape, F32, kind="ExternalOutput").ap()
    build(nc, *args, out)
    r = run_bass_kernel_spmd(nc, [arrays], core_ids=[0])
    return r.results[0]["out"]
```

```python
from contextlib import ExitStack

import concourse.bass as bass
from concourse import mybir

ALU = mybir.AluOpType
ACT = mybir.ActivationFunctionType
AX = mybir.AxisListType
F32 = mybir.dt.float32
F32R = mybir.dt.float32r
BF16 = mybir.dt.bfloat16
U32 = mybir.dt.uint32
ts = bass.ts
ds = bass.ds

P = 128
H = 128
LN_EPS = 1e-5
RMS_EPS = 1.1920929e-07
HEAD_DIM = 8


def build(nc, x, w_qkv_t, b_qkv, b_qkv_t, w_g1, b_g1, w_g2_t, b_g2, w_out_t, b_out, ln_g, ln_b,
          router_t, rg, ru, rd, sg, su, sd, out):
    B, N, _ = x.shape
    J = N // P
    E = rg.shape[0]
    IR = rg.shape[2]
    IS = sg.shape[1]
    CR = IR // P
    CS = IS // P
    CAP = max(int(1.25 * B * N / E), 1)
    SLOTS = E * CAP
    BLOCKS = [(a, min(N, CAP - a)) for a in range(0, CAP, N)]
    NBLK = len(BLOCKS)
    K = 2
    LAG = 3
    RING = 4

    slot_x = nc.dram_tensor("slot_x", [SLOTS, H], F32, kind="Internal").ap()
    slot_y = nc.dram_tensor("slot_y", [SLOTS + 1, H], F32, kind="Internal").ap()

    with ExitStack() as ctx:
        def sb(name, shape, dt=F32):
            return ctx.enter_context(nc.sbuf_tensor(name, shape, dt))

        def sem(name):
            return ctx.enter_context(nc.semaphore(name))

        bank = [ctx.enter_context(nc.psum_tensor(f"bank{i}", [P, 512], F32)) for i in range(8)]

        passed = sem("passed")

        def alone(eng):
            eng.sem_inc(passed, 1)

        def need(eng, s, count):
            if not isinstance(count, int) or count > 0:
                eng.wait_ge(s, count)

        res = sb("res", [P, B * N])
        xf_hi = sb("xf_hi", [P, B * N], F32R)
        xf_lo = sb("xf_lo", [P, B * N], F32R)
        slots = sb("slots", [P, B * K * J], U32)
        wts = sb("wts", [P, B * K * J])
        ident = sb("ident", [P, P])
        mhalf = sb("mhalf", [P, 3 * J])
        shared = sb("shared", [P, B // 2 * N])
        s_hi = sb("s_hi", [P, 3 * IS], F32R)
        s_lo = sb("s_lo", [P, 3 * IS], F32R)
        raw = sb("raw", [P, 3 * IR])

        w_in = sem("w_in")

        def expert_loads(e):
            return [(raw[:, 0:IR], rg[ds(e, 1)].rearrange("e p i -> p (e i)")),
                    (raw[:, IR:2 * IR], ru[ds(e, 1)].rearrange("e p i -> p (e i)")),
                    (raw[:, 2 * IR:3 * IR].rearrange("p (c h) -> p c h", h=H),
                     rd[ds(e, 1)].rearrange("e (c p) h -> p (e c) h", p=P))]

        with ExitStack() as c1:
            def sb1(name, shape, dt=F32):
                return c1.enter_context(nc.sbuf_tensor("a_" + name, shape, dt))

            wqkv = sb1("wqkv", [P, 3 * H])
            wo = sb1("wo", [P, H])
            wo_half = sb1("wo_half", [P, H])
            wo_sum = sb1("wo_sum", [P, 1])
            wo_c = sb1("wo_c", [P, H])
            g1 = sb1("g1", [8, H])
            g2 = sb1("g2", [8, H])
            wg = sb1("wg", [P, H])
            bqkv = sb1("bqkv", [P, 3])
            bg1 = sb1("bg1", [8, 1])
            bg2 = sb1("bg2", [P, 1])
            bg_half = sb1("bg_half", [P, 1])
            lng = sb1("lng", [P, 1])
            lnb = sb1("lnb", [P, 1])
            bv_row = sb1("bv_row", [P, H])
            bo_row = sb1("bo_row", [1, H])
            bo_sum = sb1("bo_sum", [1, 1])
            bo_c = sb1("bo_c", [1, H])
            ones_row = sb1("ones_row", [1, P])
            wr = sb1("wr", [P, E])
            wr_hi = sb1("wr_hi", [P, E], F32R)
            wr_lo = sb1("wr_lo", [P, E], F32R)
            head_mask = sb1("head_mask", [P, H])
            identb = sb1("identb", [P, P], BF16)
            before = sb1("before", [P, P], BF16)
            onesb = sb1("onesb", [P, P], BF16)
            expert_id = sb1("expert_id", [P, J * E])
            expert_base = sb1("expert_base", [P, J * E])
            st = sb1("st", [P, J * 6])
            mv = sb1("mv", [P, J * 2])
            ve = sb1("ve", [P, 2 * J])
            rs = sb1("rs", [P, 2 * J])
            ve_o = sb1("ve_o", [P, J])
            rs_o = sb1("rs_o", [P, J])
            xn = sb1("xn", [P, N])
            xn_t = sb1("xn_t", [P, N])
            q_t = sb1("q_t", [P, N])
            ek_t = sb1("ek_t", [P, N])
            ek = sb1("ek", [P, N])
            tg = [sb1(f"tg{q}", [P, N]) for q in range(2)]
            kmax = sb1("kmax", [P, 1])
            kbias = sb1("kbias", [P, 1])
            ksum = sb1("ksum", [P, 1])
            rksum = sb1("rksum", [P, 1])
            a_t = sb1("a_t", [P, H])
            kv = sb1("kv", [P, H])
            kvh = sb1("kvh", [P, H])
            kv_sum = sb1("kv_sum", [P, 1])
            kvm = sb1("kvm", [P, H])
            squares = ek
            ssq_o = sb1("ssq_o", [P, J])
            ssq_y = sb1("ssq_y", [P, J])
            wide = sb1("wide", [P, 8 * N])
            s_raw = wide[:, 0:3 * IS]
            on, oa, u = (wide[:, k * N:(k + 1) * N] for k in range(3))
            xf = [wide[:, k * N:(k + 1) * N] for k in (3, 4)]
            gated = wide[:, 5 * N:6 * N]
            hid = [wide[:, k * N:(k + 1) * N] for k in (6, 7)]
            assert 3 * IS <= 6 * N
            zeros = wide[:, 6 * N:8 * N]
            sd_sum = sb1("sd_sum", [P, CS])
            ve3 = sb1("ve3", [P, J])
            rs3 = sb1("rs3", [P, J])
            st4 = sb1("st4", [P, J * 6])
            mv4 = sb1("mv4", [P, J * 2])
            ve4 = sb1("ve4", [P, J])
            rs4 = sb1("rs4", [P, J])
            ms1 = sb1("ms1", [P, J])
            ms2 = sb1("ms2", [P, J])
            lgt = sb1("lgt", [E, N])
            lg = sb1("lg", [P, J * E])
            top = sb1("top", [P, J * 8])
            topi = sb1("topi", [P, J * 8], U32)
            oh = sb1("oh", [P, K * J * E], BF16)
            mask = sb1("mask", [P, J * E], BF16)
            taken = sb1("taken", [P, E], F32)
            takenb = sb1("takenb", [P, E], BF16)
            newly = sb1("newly", [P, E], F32)
            fits = sb1("fits", [P, J * E])
            place = sb1("place", [P, J * E])
            placed = sb1("placed", [P, J * E])
            picked = sb1("picked", [P, K * J * E])
            slotf = sb1("slotf", [P, K * J])
            slot_now = [sb1(f"slot_now{q}", [P, K * J], U32) for q in range(2)]
            dl = sb1("dl", [P, J])
            dls = sb1("dls", [P, J])
            tw = sb1("tw", [P, J])
            h_hi = [sb1(f"h_hi{q}", [P, N], F32R) for q in range(RING)]
            h_lo = [sb1(f"h_lo{q}", [P, N], F32R) for q in range(RING)]
            y_t = sb1("y_t", [P, N])

            turn_ps, kg_ps, q_ps, oy_ps, small_ps, gate_ps, up_ps, sy_ps = bank

            names = ("consts ident weights zeros_ready filled setup_dve setup_act wg_psum wg_copied bg_ready wo_sums "
                     "s_in sd_sums sd_centred s_hi_done s_lo_done "
                     "stats1 mv1 ve12 rs12 ve_o rs_o xn xnT_ps xnT q_in k_in g_in kmax kbias exp silu_q tanh_g "
                     "ekT_ps ek aT_ps aT kv_ps kvn kvh rksum kvm out_ps ssq_o on onT_ps oa u y_ps ssq_y "
                     "ve3 rs3 res st4 mv4 ve4 rs4 ms1 ms2 xf xfT_ps xf_hi xf_lo "
                     "lgt_ps lgt lg_ps lg top topi dl oh mask newly taken takenb rank_ps place "
                     "placed picked slotf slot_now slots dls tanh_w wts "
                     "gate up silu hid hhi hlo_even hlo_odd down yt yr_ps yr").split()
            S = {n: sem(n) for n in names}
            x_in = [sem("x_in_even"), sem("x_in_odd")]
            scattered = [sem("scattered_even"), sem("scattered_odd")]
            SCATTERS = 16 * K * J
            SHARED_1 = B // 2
            FILLS = SLOTS * H // P // 1024 + 1

            mean_of = lambda t, j: t[:, 2 * j:2 * j + 1]
            var_of = lambda t: t[:, :].rearrange("p (j s) -> p j s", s=2)[:, :, 1]
            je = lambda t: t.rearrange("p (j e) -> p j e", e=E)
            jh = lambda t: t.rearrange("p (j h) -> p j h", h=H)
            tile_of = lambda t, j: t[:, j * H:(j + 1) * H]

            def over_features(t):
                return t.rearrange("p (j o) -> p j o", o=1).broadcast_to([P, J, H])

            def steps(fori, step):
                for i in range(4):
                    step(i // 2, i, i % 2)
                with fori(2, B // 2 - 1) as h:
                    step(h, h * 2, 0)
                    step(h, h * 2 + 1, 1)
                for i in range(B - 2, B + 2):
                    step(i // 2, i, i % 2)

            def stages(i):
                if not isinstance(i, int):
                    return (True,) * 6
                return i < B, 1 <= i <= B, i >= 2, i >= 2, i + 1 < B, i >= 3

            block = c1.enter_context(nc.Block())

            @block.sync
            def _(sp):
                loads = [(wqkv[:, :], w_qkv_t), (wo[:, :], w_out_t), (g1[:, :], w_g1), (g2[:, :], w_g2_t),
                         (bqkv[:, :], b_qkv_t),
                         (bg1[:, :], b_g1.rearrange("(p o) -> p o", o=1)),
                         (bg2[:, :], b_g2.rearrange("(p o) -> p o", o=1)),
                         (lng[:, :], ln_g.rearrange("(p o) -> p o", o=1)),
                         (lnb[:, :], ln_b.rearrange("(p o) -> p o", o=1)),
                         (bv_row[:, :], b_qkv[2 * H:3 * H].rearrange("(o h) -> o h", o=1).broadcast_to([P, H])),
                         (bo_row[:, :], b_out.rearrange("(o h) -> o h", o=1)),
                         (wr[:, :], router_t)]

                def load_x(i, q):
                    sp.dma_start(res[:, ds(i * N, N)],
                                 x[ds(i, 1)].rearrange("b (p j) h -> p (b j h)", p=P)).then_inc(x_in[q], 16)

                load_x(0, 0)
                for dst, src in loads:
                    sp.dma_start(dst, src).then_inc(S["weights"], 16)
                load_x(1, 1)
                sp.dma_start(s_raw[:, 0:IS], sg).then_inc(S["s_in"], 16)
                sp.dma_start(s_raw[:, IS:2 * IS], su).then_inc(S["s_in"], 16)
                sp.dma_start(s_raw[:, 2 * IS:3 * IS].rearrange("p (c h) -> p c h", h=H),
                             sd.rearrange("(c p) h -> p c h", p=P)).then_inc(S["s_in"], 16)
                sp.wait_ge(S["zeros_ready"], 1)
                for n in range(FILLS - 1):
                    sp.dma_start(slot_x.rearrange("(p r) h -> p (r h)", p=P)[:, n * 1024:(n + 1) * 1024],
                                 zeros).then_inc(S["filled"], 16)
                sp.dma_start(slot_y[SLOTS:SLOTS + 1, :], zeros[0:1, 0:H]).then_inc(S["filled"], 16)
                with sp.Fori(1, B // 2) as h:
                    for q in range(2):
                        sp.wait_ge(S["mv1"], h * 2 - 1 + q)
                        load_x(h * 2 + q, q)
                for dst, src in expert_loads(0):
                    sp.dma_start(dst, src).then_inc(w_in, 16)

            @block.gpsimd
            def _(g):
                g.memset(ident[:, :], 0.0).then_inc(S["consts"], 1)
                g.memset(identb[:, :], 0.0).then_inc(S["consts"], 1)
                g.memset(before[:, :], 1.0).then_inc(S["consts"], 1)
                g.memset(head_mask[:, :], 1.0).then_inc(S["consts"], 1)
                g.memset(mhalf[:, :], -0.5).then_inc(S["consts"], 1)
                g.wait_ge(S["consts"], 5)
                for t in (ident, identb):
                    g.affine_select(out=t[:, :], in_=t[:, :], compare_op=ALU.not_equal, fill=1.0, base=0,
                                    pattern=[[-1, P]], channel_multiplier=1).then_inc(S["ident"], 1)
                g.affine_select(out=before[:, :], in_=before[:, :], compare_op=ALU.is_ge, fill=0.0, base=-1,
                                pattern=[[1, P]], channel_multiplier=-1).then_inc(S["ident"], 1)
                hm = head_mask[:, :].rearrange("p (g r) -> p g r", r=HEAD_DIM)
                g.affine_select(out=hm, in_=hm, compare_op=ALU.is_ge, fill=0.0, base=0,
                                pattern=[[-HEAD_DIM, H // HEAD_DIM], [0, HEAD_DIM]],
                                channel_multiplier=1).then_inc(S["ident"], 1)
                g.wait_ge(S["ident"], 4)
                g.affine_select(out=hm, in_=hm, compare_op=ALU.is_ge, fill=0.0, base=HEAD_DIM - 1,
                                pattern=[[HEAD_DIM, H // HEAD_DIM], [0, HEAD_DIM]],
                                channel_multiplier=-1).then_inc(S["ident"], 1)
                g.iota(expert_id[:, :], pattern=[[0, J], [1, E]], base=0, channel_multiplier=0,
                       allow_small_or_imprecise_dtypes=True).then_inc(S["ident"], 1)
                g.iota(expert_base[:, :], pattern=[[0, J], [CAP, E]], base=-SLOTS, channel_multiplier=0,
                       allow_small_or_imprecise_dtypes=True).then_inc(S["ident"], 1)

                def power(dst, src, ready, done, n, width):
                    g.wait_ge(S[ready], n + 1)
                    g.tensor_tensor(dst[:, 0:width], src[:, 0:width], mhalf[:, 0:width], ALU.pow).then_inc(S[done], 1)

                def low(m, c):
                    g.wait_ge(S["hhi"], m * CS + c + 1)
                    need(g, S["down"], m * CS + c - RING + 1)
                    g.tensor_tensor(h_lo[c % RING][:, :], hid[c % 2], h_hi[c % RING][:, :].bitcast(F32),
                                    ALU.subtract).then_inc(S["hlo_odd"], 1)

                def scatter(q, cs):
                    for c in cs:
                        g.indirect_dma_start(
                            out=slot_x, out_offset=bass.IndirectOffsetOnAxis(ap=slot_now[q][:, c:c + 1], axis=0),
                            in_=tile_of(xf[q], c % J), in_offset=None,
                            bounds_check=SLOTS - 1, oob_is_err=False).then_inc(scattered[q], 16)

                def step(h, i, q):
                    attend, project, route, share, ahead, routed = stages(i)
                    if routed:
                        scatter(1 - q, range(5, 8))
                    power(rs, ve, "ve12", "rs12", i + 1, 2 * J)
                    if share:
                        low(h - 1, 4 * q + 1)
                    if project:
                        power(rs3, ve3, "ve3", "rs3", i - 1, J)
                    if isinstance(i, int) and i == 2:
                        g.wait_ge(S["filled"], 16 * FILLS)
                    if route:
                        g.wait_ge(S["slot_now"], i - 1)
                        alone(g)
                        scatter(q, range(0, 2))
                    if project:
                        power(rs4, ve4, "ve4", "rs4", i - 1, J)
                    if attend:
                        power(rs_o, ve_o, "ve_o", "rs_o", i, J)
                    if route:
                        scatter(q, range(2, 5))
                    if share:
                        low(h - 1, 4 * q + 3)

                g.wait_ge(S["ident"], 7)
                power(rs, ve, "ve12", "rs12", 0, 2 * J)
                steps(g.Fori, step)
                scatter((B - 1) % 2, range(5, 8))
                for q in range(2):
                    g.wait_ge(scattered[q], SCATTERS * B // 2)

            @block.scalar
            def _(act):
                act.wait_ge(S["weights"], 12 * 16)
                nc.scalar.activation(wr_hi[:, :], wr[:, :], ACT.Copy).then_inc(S["setup_act"], 1)
                nc.scalar.mul(wo_half[:, :], wo[:, :], 0.5).then_inc(S["setup_act"], 1)

                def copy(dst, src):
                    return nc.scalar.activation(dst, src, ACT.Copy)

                def squares_of(ready, n, ssq, done):
                    act.wait_ge(S[ready], n + 1)
                    for j in range(J):
                        o = nc.scalar.activation(tile_of(squares, j), tile_of(oy_ps, j), ACT.Square,
                                                 accum_out=ssq[:, j:j + 1])
                    o.then_inc(S[done], 1)

                def silu(m, c):
                    act.wait_ge(S["gate"], m * CS + c + 1)
                    need(act, S["hid"], m * CS + c)
                    nc.scalar.activation(gated, gate_ps[:, :], ACT.Silu).then_inc(S["silu"], 1)

                def high(m, c):
                    act.wait_ge(S["hid"], m * CS + c + 1)
                    need(act, S["down"], m * CS + c - RING + 1)
                    copy(h_hi[c % RING][:, :], hid[c % 2]).then_inc(S["hhi"], 1)

                def shared_out(m):
                    act.wait_ge(S["down"], m * CS + CS)
                    need(act, S["yr_ps"], m)
                    copy(y_t[:, :], sy_ps[:, :]).then_inc(S["yt"], 1)

                def shared_rows(m):
                    act.wait_ge(S["yr_ps"], m + 1)
                    copy(shared[:, ds(m * N, N)], turn_ps[:, :]).then_inc(S["yr"], 1)

                def weight_tanh(r):
                    act.wait_ge(S["dls"], r + 1)
                    nc.scalar.activation(tw[:, :], dls[:, :], ACT.Tanh, scale=0.5).then_inc(S["tanh_w"], 1)

                def turn_xn(b):
                    act.wait_ge(S["xnT_ps"], b + 1)
                    need(act, S["g_in"], b)
                    copy(xn_t[:, :], turn_ps[:, :]).then_inc(S["xnT"], 1)

                def step(h, i, q):
                    attend, project, route, share, ahead, routed = stages(i)
                    n, r, m, c = i - 1, i - 2, h - 1, 4 * q
                    later = not (isinstance(m, int) and m == 0)
                    if attend:
                        act.wait_ge(S["kbias"], i + 1)
                        nc.scalar.activation(ek_t[:, :], kg_ps[:, :], ACT.Exp, bias=kbias[:, 0:1], scale=1.0,
                                             accum_out=ksum[:, 0:1]).then_inc(S["exp"], 1)
                    if project:
                        act.wait_ge(S["onT_ps"], n + 1)
                        nc.scalar.activation(oa, turn_ps[:, :], ACT.Identity, bias=lnb[:, 0:1],
                                             scale=lng[:, 0:1]).then_inc(S["oa"], 1)
                    if attend:
                        act.wait_ge(S["ekT_ps"], i + 1)
                        copy(ek[:, :], turn_ps[:, :]).then_inc(S["ek"], 1)
                    if routed:
                        weight_tanh(r - 1)
                    if attend:
                        act.wait_ge(S["g_in"], i + 1)
                        nc.scalar.activation(tg[q][:, :], kg_ps[:, :], ACT.Tanh, bias=bg_half[:, 0:1],
                                             scale=0.5).then_inc(S["tanh_g"], 1)
                    if share:
                        silu(m, c)
                    if route:
                        act.wait_ge(S["lgt_ps"], r + 1)
                        copy(lgt[:, :], kg_ps[0:E, :]).then_inc(S["lgt"], 1)
                    if attend:
                        act.wait_ge(S["q_in"], i + 1)
                        nc.scalar.activation(q_t[:, :], q_ps[:, :], ACT.Silu, bias=bqkv[:, 0:1],
                                             scale=1.0).then_inc(S["silu_q"], 1)
                    if share:
                        high(m, c)
                    if project:
                        squares_of("y_ps", n, ssq_y, "ssq_y")
                    if share:
                        silu(m, c + 1)
                        high(m, c + 1)
                        silu(m, c + 2)
                    if ahead:
                        turn_xn(i + 1)
                    if isinstance(i, int) and i == 0:
                        act.wait_ge(S["sd_centred"], 1)
                        copy(s_hi[:, :], s_raw).then_inc(S["s_hi_done"], 1)
                    if share:
                        high(m, c + 2)
                        if q == 0 and later:
                            shared_out(m - 1)
                    if attend:
                        squares_of("out_ps", i, ssq_o, "ssq_o")
                    if share:
                        if q == 0 and later:
                            shared_rows(m - 1)
                        silu(m, c + 3)
                    if project:
                        act.wait_ge(S["xfT_ps"], n + 1)
                        copy(xf_hi[:, ds(n * N, N)], turn_ps[:, :]).then_inc(S["xf_hi"], 1)
                    if share:
                        high(m, c + 3)

                act.wait_ge(S["bg_ready"], 1)
                turn_xn(0)
                steps(act.Fori, step)
                weight_tanh(B - 1)
                shared_out(SHARED_1 - 1)
                shared_rows(SHARED_1 - 1)

            @block.vector
            def _(v):
                v.memset(zeros, 0.0).then_inc(S["zeros_ready"], 1)
                v.memset(onesb[:, :], 1.0).then_inc(S["setup_dve"], 1)
                v.memset(ones_row[:, :], 1.0).then_inc(S["setup_dve"], 1)
                v.memset(taken[:, :], 0.0).then_inc(S["setup_dve"], 1)
                v.memset(takenb[:, :], 0.0).then_inc(S["setup_dve"], 1)
                v.memset(ve[:, :], 1.0).then_inc(S["setup_dve"], 1)
                v.wait_ge(S["setup_act"], 2)
                v.tensor_tensor(wr_lo[:, :], wr[:, :], wr_hi[:, :].bitcast(F32), ALU.subtract).then_inc(S["setup_dve"], 1)
                v.reduce_sum(wo_sum[:, :], wo_half[:, :], AX.X).then_inc(S["wo_sums"], 1)
                v.reduce_sum(bo_sum[:, :], bo_row[:, :], AX.X).then_inc(S["wo_sums"], 1)
                v.wait_ge(S["wo_sums"], 2)
                v.scalar_tensor_tensor(out=wo_c[:, :], in0=wo_sum[:, 0:1].broadcast_to([P, H]), scalar=-1.0 / H,
                                       in1=wo_half[:, :], op0=ALU.mult, op1=ALU.add).then_inc(S["setup_dve"], 1)
                v.scalar_tensor_tensor(out=bo_c[:, :], in0=bo_sum[:, 0:1].broadcast_to([1, H]), scalar=-1.0 / H,
                                       in1=bo_row[:, :], op0=ALU.mult, op1=ALU.add).then_inc(S["setup_dve"], 1)
                v.wait_ge(S["wg_psum"], 1)
                v.tensor_copy(wg[:, :], small_ps[:, 0:H]).then_inc(S["wg_copied"], 1)
                v.tensor_scalar(bg_half[:, :], small_ps[:, H:H + 1], bg2[:, 0:1], 0.5, ALU.add,
                                ALU.mult).then_inc(S["bg_ready"], 1)

                def res_tile(b, j):
                    return res[:, ds(b * N + j * H, H)]

                def split_shared():
                    w = s_raw[:, 2 * IS:3 * IS].rearrange("p (c h) -> p c h", h=H)
                    v.wait_ge(S["s_in"], 48)
                    v.reduce_sum(sd_sum[:, :], w, AX.X).then_inc(S["sd_sums"], 1)
                    v.wait_ge(S["sd_sums"], 1)
                    v.scalar_tensor_tensor(out=w, in0=sd_sum[:, :].rearrange("p (c o) -> p c o", o=1)
                                           .broadcast_to([P, CS, H]), scalar=-1.0 / H, in1=w,
                                           op0=ALU.mult, op1=ALU.add).then_inc(S["sd_centred"], 1)
                    v.wait_ge(S["s_hi_done"], 1)
                    v.tensor_tensor(s_lo[:, :], s_raw, s_hi[:, :].bitcast(F32),
                                    ALU.subtract).then_inc(S["s_lo_done"], 1)
                    v.wait_ge(S["s_lo_done"], 1)

                def hidden(m, c):
                    v.wait_ge(S["silu"], m * CS + c + 1)
                    v.wait_ge(S["up"], m * CS + c + 1)
                    need(v, S["hlo_odd" if c % 2 else "hlo_even"], m * (CS // 2) + c // 2)
                    v.tensor_tensor(hid[c % 2], gated, up_ps[:, :], ALU.mult).then_inc(S["hid"], 1)

                def low(m, c):
                    v.wait_ge(S["hhi"], m * CS + c + 1)
                    need(v, S["down"], m * CS + c - RING + 1)
                    v.tensor_tensor(h_lo[c % RING][:, :], hid[c % 2], h_hi[c % RING][:, :].bitcast(F32),
                                    ALU.subtract).then_inc(S["hlo_even"], 1)

                def stats_of_x(b, q, loads):
                    v.wait_ge(x_in[q], loads * 16)
                    alone(v)
                    for j in range(J):
                        o = v.bn_stats(st[:, 6 * j:6 * j + 6], res_tile(b, j))
                    o.then_inc(S["stats1"], 1)

                def moments_of_x(b):
                    v.wait_ge(S["stats1"], b + 1)
                    alone(v)
                    for j in range(J):
                        o = v.bn_aggr(mv[:, 2 * j:2 * j + 2], st[:, 6 * j:6 * j + 6])
                    o.then_inc(S["mv1"], 1)
                    v.wait_ge(S["mv1"], b + 1)
                    return v.tensor_scalar(ve[:, 0:J], var_of(mv), LN_EPS, None, ALU.add)

                def normalise_x(b):
                    v.wait_ge(S["rs12"], b + 1)
                    need(v, S["aT_ps"], b)
                    for j in range(J):
                        o = v.tensor_scalar(tile_of(xn, j), res_tile(b, j), mean_of(mv, j), rs[:, j:j + 1],
                                            ALU.subtract, ALU.mult)
                    o.then_inc(S["xn"], 1)

                def weights_of(r):
                    v.wait_ge(S["tanh_w"], r + 1)
                    v.tensor_scalar(wts[:, ds(r * K * J, J)], tw[:, :], 0.5, 0.5, ALU.mult, ALU.add)
                    v.tensor_scalar(wts[:, ds(r * K * J + J, J)], tw[:, :], -0.5, 0.5, ALU.mult,
                                    ALU.add).then_inc(S["wts"], 1)

                def step(h, i, q):
                    attend, project, route, share, ahead, routed = stages(i)
                    n, r, m, c = i - 1, i - 2, h - 1, 4 * q
                    if attend:
                        v.wait_ge(S["k_in"], i + 1)
                        v.tensor_reduce(kmax[:, :], kg_ps[:, :], AX.X, ALU.max, negate=True).then_inc(S["kmax"], 1)
                        v.wait_ge(S["kmax"], i + 1)
                        v.tensor_scalar(kbias[:, :], kmax[:, :], bqkv[:, 1:2], bqkv[:, 1:2], ALU.subtract,
                                        ALU.add).then_inc(S["kbias"], 1)
                    if ahead:
                        stats_of_x(i + 1, 1 - q, h + q + 1)
                    if route:
                        v.tensor_tensor(ms1[:, :], rs4[:, :], rs4[:, :], ALU.mult).then_inc(S["ms1"], 1)
                        v.wait_ge(S["ms1"], r + 1)
                        v.tensor_tensor(ms2[:, :], ms1[:, :], var_of(mv4), ALU.mult).then_inc(S["ms2"], 1)
                    if ahead:
                        o = moments_of_x(i + 1)
                    if route:
                        v.wait_ge(S["ms2"], r + 1)
                        o = v.tensor_scalar(ve[:, J:2 * J], ms2[:, :], RMS_EPS, None, ALU.add)
                    o.then_inc(S["ve12"], 1)
                    if attend:
                        v.wait_ge(S["exp"], i + 1)
                        v.reciprocal(rksum[:, :], ksum[:, :]).then_inc(S["rksum"], 1)
                    if project:
                        v.wait_ge(S["oa"], n + 1)
                        v.wait_ge(S["tanh_g"], n + 1)
                        v.scalar_tensor_tensor(out=u, in0=tg[1 - q][:, :], scalar=1.0, in1=oa,
                                               op0=ALU.add, op1=ALU.mult).then_inc(S["u"], 1)
                    if routed:
                        weights_of(r - 1)
                    if attend:
                        v.wait_ge(S["aT_ps"], i + 1)
                        v.tensor_copy(a_t[:, :], small_ps[:, 0:H]).then_inc(S["aT"], 1)
                    if isinstance(i, int) and i == 2:
                        v.wait_ge(S["filled"], 16 * FILLS)
                    if share:
                        hidden(m, c)
                    if attend:
                        v.wait_ge(S["kv_ps"], i + 1)
                        v.scalar_tensor_tensor(out=kv[:, :], in0=small_ps[:, 0:H], scalar=rksum[:, 0:1],
                                               in1=bv_row[:, :], op0=ALU.mult, op1=ALU.add).then_inc(S["kvn"], 1)
                    if route:
                        v.wait_ge(S["lg_ps"], r + 1)
                        v.tensor_copy(lg[:, :], kg_ps[:, 0:J * E]).then_inc(S["lg"], 1)
                    if attend:
                        v.wait_ge(S["kvn"], i + 1)
                        v.tensor_tensor_reduce(out=kvh[:, :], in0=kv[:, :], in1=head_mask[:, :], scale=1.0,
                                               scalar=0.0, op0=ALU.mult, op1=ALU.add,
                                               accum_out=kv_sum[:, 0:1]).then_inc(S["kvh"], 1)
                    if route:
                        v.wait_ge(S["lg"], r + 1)
                        alone(v)
                        for j in range(J):
                            o = v.max(top[:, 8 * j:8 * j + 8], lg[:, E * j:E * j + E])
                        o.then_inc(S["top"], 1)
                    if attend:
                        v.wait_ge(S["kvh"], i + 1)
                        need(v, S["out_ps"], i)
                        v.scalar_tensor_tensor(out=kvm[:, :], in0=kv_sum[:, 0:1].broadcast_to([P, H]),
                                               scalar=-1.0 / H, in1=kvh[:, :], op0=ALU.mult,
                                               op1=ALU.add).then_inc(S["kvm"], 1)
                    if route:
                        v.wait_ge(S["top"], r + 1)
                        alone(v)
                        for j in range(J):
                            o = v.max_index(topi[:, 8 * j:8 * j + 8], top[:, 8 * j:8 * j + 8], lg[:, E * j:E * j + E])
                        o.then_inc(S["topi"], 1)
                        t3 = top[:, :].rearrange("p (j r) -> p j r", r=8)
                        v.tensor_tensor(dl[:, :], t3[:, :, 0], t3[:, :, 1], ALU.subtract).then_inc(S["dl"], 1)
                        v.wait_ge(S["topi"], r + 1)
                        i3 = topi[:, :].rearrange("p (j r) -> p j r", r=8)
                        for k in range(K):
                            o = v.tensor_tensor(je(oh[:, k * J * E:(k + 1) * J * E]), je(expert_id[:, :]),
                                                i3[:, :, k:k + 1].broadcast_to([P, J, E]), ALU.is_equal)
                        o.then_inc(S["oh"], 1)
                        v.wait_ge(S["dl"], r + 1)
                        v.wait_ge(S["rs12"], i + 2)
                        v.tensor_tensor(dls[:, :], dl[:, :], rs[:, J:2 * J], ALU.mult).then_inc(S["dls"], 1)
                        v.wait_ge(S["oh"], r + 1)
                        v.tensor_tensor(mask[:, :], oh[:, 0:J * E], oh[:, J * E:], ALU.add).then_inc(S["mask"], 1)
                    if share:
                        low(m, c)
                    if route:
                        v.wait_ge(S["mask"], r + 1)
                        v.tensor_reduce(newly[:, :], mask[:, :].rearrange("p (j e) -> p e j", e=E), AX.X,
                                        ALU.add).then_inc(S["newly"], 1)
                    if share:
                        hidden(m, c + 1)
                    if project:
                        v.wait_ge(S["ssq_y"], n + 1)
                        v.tensor_scalar(ve3[:, :], ssq_y[:, :], 1.0 / H, LN_EPS, ALU.mult,
                                        ALU.add).then_inc(S["ve3"], 1)
                    if route:
                        v.wait_ge(S["rank_ps"], r + 1)
                        v.tensor_scalar(fits[:, :], kg_ps[:, 0:J * E], float(CAP), None, ALU.is_lt)
                        v.tensor_tensor(place[:, :], kg_ps[:, 0:J * E], expert_base[:, :],
                                        ALU.add).then_inc(S["place"], 1)
                        v.wait_ge(S["newly"], r + 1)
                        v.tensor_tensor(taken[:, :], taken[:, :], newly[:, :], ALU.add).then_inc(S["taken"], 1)
                        v.wait_ge(S["place"], r + 1)
                        v.tensor_tensor(placed[:, :], place[:, :], fits[:, :], ALU.mult).then_inc(S["placed"], 1)
                        v.wait_ge(S["taken"], r + 1)
                        v.tensor_copy(takenb[:, :], taken[:, :]).then_inc(S["takenb"], 1)
                        v.wait_ge(S["placed"], r + 1)
                        v.tensor_tensor(picked[:, :].rearrange("p (k c) -> p k c", k=K),
                                        placed[:, :].rearrange("p (o c) -> p o c", o=1).broadcast_to([P, K, J * E]),
                                        oh[:, :].rearrange("p (k c) -> p k c", k=K), ALU.mult).then_inc(S["picked"], 1)
                        v.wait_ge(S["picked"], r + 1)
                        v.tensor_reduce(slotf[:, :], picked[:, :].rearrange("p (c e) -> p c e", e=E), AX.X,
                                        ALU.add).then_inc(S["slotf"], 1)
                        v.wait_ge(S["slotf"], r + 1)
                        v.tensor_scalar(slot_now[q][:, :], slotf[:, :], float(SLOTS), None,
                                        ALU.add).then_inc(S["slot_now"], 1)
                        v.tensor_scalar(slots[:, ds(r * K * J, K * J)], slotf[:, :], float(SLOTS), None,
                                        ALU.add).then_inc(S["slots"], 1)
                    if ahead:
                        normalise_x(i + 1)
                    if share:
                        hidden(m, c + 2)
                    if project:
                        v.wait_ge(S["rs3"], n + 1)
                        for j in range(J):
                            o = v.scalar_tensor_tensor(out=res_tile(n, j), in0=tile_of(oy_ps, j), scalar=rs3[:, j:j + 1],
                                                       in1=res_tile(n, j), op0=ALU.mult, op1=ALU.add)
                        o.then_inc(S["res"], 1)
                        v.wait_ge(S["res"], n + 1)
                        alone(v)
                        for j in range(J):
                            o = v.bn_stats(st4[:, 6 * j:6 * j + 6], res_tile(n, j))
                        o.then_inc(S["st4"], 1)
                        v.wait_ge(S["st4"], n + 1)
                        alone(v)
                        for j in range(J):
                            o = v.bn_aggr(mv4[:, 2 * j:2 * j + 2], st4[:, 6 * j:6 * j + 6])
                        o.then_inc(S["mv4"], 1)
                        v.wait_ge(S["mv4"], n + 1)
                        v.tensor_scalar(ve4[:, :], var_of(mv4), LN_EPS, None, ALU.add).then_inc(S["ve4"], 1)
                    if share:
                        low(m, c + 2)
                    if isinstance(i, int) and i == 0:
                        split_shared()
                    if attend:
                        v.wait_ge(S["ssq_o"], i + 1)
                        v.tensor_scalar(ve_o[:, :], ssq_o[:, :], 1.0 / H, LN_EPS, ALU.mult,
                                        ALU.add).then_inc(S["ve_o"], 1)
                    if project:
                        v.wait_ge(S["rs4"], n + 1)
                        need(v, scattered[1 - q], SCATTERS * (h - 1 + q))
                        need(v, S["xfT_ps"], n - 1)
                        for j in range(J):
                            o = v.tensor_scalar(tile_of(xf[1 - q], j), res_tile(n, j), mean_of(mv4, j),
                                                rs4[:, j:j + 1], ALU.subtract, ALU.mult)
                        o.then_inc(S["xf"], 1)
                    if share:
                        hidden(m, c + 3)
                    if attend:
                        v.wait_ge(S["rs_o"], i + 1)
                        need(v, S["onT_ps"], i)
                        v.tensor_tensor(jh(on), jh(oy_ps[:, :]), over_features(rs_o[:, :]),
                                        ALU.mult).then_inc(S["on"], 1)
                    if project:
                        v.wait_ge(S["xf_hi"], n + 1)
                        v.tensor_tensor(xf_lo[:, ds(n * N, N)], turn_ps[:, :], xf_hi[:, ds(n * N, N)].bitcast(F32),
                                        ALU.subtract).then_inc(S["xf_lo"], 1)

                v.wait_ge(S["ident"], 7)
                stats_of_x(0, 0, 1)
                moments_of_x(0).then_inc(S["ve12"], 1)
                normalise_x(0)
                steps(v.Fori, step)
                weights_of(B - 1)

            @block.tensor
            def _(pe):
                mm = nc.tensor.matmul

                def transposes(dst, src):
                    for j in range(J):
                        o = nc.tensor.transpose(dst[:, j * P:(j + 1) * P], src[:, j * P:(j + 1) * P], ident[:, :])
                    return o

                def product(dst, wa, a_hi, a_lo, start, stop):
                    mm(dst, s_lo[:, wa:wa + P], a_hi, start=start, stop=False)
                    mm(dst, s_hi[:, wa:wa + P], a_lo, start=False, stop=False)
                    return mm(dst, s_hi[:, wa:wa + P], a_hi, start=False, stop=stop)

                def gate(m, c):
                    need(pe, S["silu"], m * CS + c)
                    product(gate_ps[:, :], c * P, xf_hi[:, ds(m * N, N)], xf_lo[:, ds(m * N, N)], True,
                            True).then_inc(S["gate"], 1)

                def up(m, c):
                    need(pe, S["hid"], m * CS + c)
                    product(up_ps[:, :], IS + c * P, xf_hi[:, ds(m * N, N)], xf_lo[:, ds(m * N, N)], True,
                            True).then_inc(S["up"], 1)

                def down(m, c):
                    pe.wait_ge(S["hlo_odd" if c % 2 else "hlo_even"], m * (CS // 2) + c // 2 + 1)
                    if c == 0:
                        need(pe, S["yt"], m)
                    product(sy_ps[:, :], 2 * IS + c * P, h_hi[c % RING][:, :], h_lo[c % RING][:, :],
                            c == 0, c == CS - 1).then_inc(S["down"], 1)

                def down_behind(m, c):
                    if c >= LAG:
                        down(m, c - LAG)
                    elif not (isinstance(m, int) and m == 0):
                        down(m - 1, CS + c - LAG)

                def shared_rows(m):
                    pe.wait_ge(S["yt"], m + 1)
                    transposes(turn_ps, y_t).then_inc(S["yr_ps"], 1)

                def turn_xn(b):
                    pe.wait_ge(S["xn"], b + 1)
                    need(pe, S["ek"], b)
                    transposes(turn_ps, xn).then_inc(S["xnT_ps"], 1)

                def step(h, i, q):
                    attend, project, route, share, ahead, routed = stages(i)
                    n, r, m, c = i - 1, i - 2, h - 1, 4 * q
                    later = not (isinstance(m, int) and m == 0)
                    if attend:
                        pe.wait_ge(S["xnT"], i + 1)
                        need(pe, S["tanh_g"], i)
                        need(pe, S["place"], r)
                        mm(kg_ps[:, :], wqkv[:, H:2 * H], xn_t[:, :], start=True, stop=True).then_inc(S["k_in"], 1)
                        need(pe, S["silu_q"], i)
                        mm(q_ps[:, :], wqkv[:, 0:H], xn_t[:, :], start=True, stop=True).then_inc(S["q_in"], 1)
                    if isinstance(i, int) and i == 2:
                        pe.wait_ge(S["s_lo_done"], 1)
                        pe.wait_ge(S["xf_lo"], 1)
                    if share:
                        gate(m, c)
                        up(m, c)
                    if project:
                        pe.wait_ge(S["on"], n + 1)
                        need(pe, S["xf_lo"], n)
                        transposes(turn_ps, on).then_inc(S["onT_ps"], 1)
                    if attend:
                        pe.wait_ge(S["exp"], i + 1)
                        if project:
                            pe.wait_ge(S["oa"], n + 1)
                        transposes(turn_ps, ek_t).then_inc(S["ekT_ps"], 1)
                        mm(kg_ps[:, :], wg[:, :], xn_t[:, :], start=True, stop=True).then_inc(S["g_in"], 1)
                    if share:
                        down_behind(m, c)
                    if attend:
                        pe.wait_ge(S["ek"], i + 1)
                        need(pe, S["kvn"], i)
                        for j in range(J):
                            o = mm(small_ps[:, 0:H], tile_of(xn, j), tile_of(ek, j), start=(j == 0),
                                   stop=(j == J - 1))
                        o.then_inc(S["aT_ps"], 1)
                    if route:
                        pe.wait_ge(S["xf_lo"], r + 1)
                        need(pe, S["tanh_g"], i + 1 if attend else B)
                        need(pe, S["place"], r)
                        hi, lo = xf_hi[:, ds(r * N, N)], xf_lo[:, ds(r * N, N)]
                        mm(kg_ps[0:E, :], wr_lo[:, :], hi, start=True, stop=False)
                        mm(kg_ps[0:E, :], wr_hi[:, :], lo, start=False, stop=False)
                        mm(kg_ps[0:E, :], wr_hi[:, :], hi, start=False, stop=True).then_inc(S["lgt_ps"], 1)
                    if project:
                        pe.wait_ge(S["u"], n + 1)
                        mm(oy_ps[:, :], ones_row[:, :], bo_c[:, :].rearrange("p (o h) -> p o h", o=1)
                           .broadcast_to([1, J, H]), start=True, stop=False, skip_group_check=True)
                        for j in range(J):
                            o = mm(tile_of(oy_ps, j), u[:, j * P:(j + 1) * P], wo_c[:, :],
                                   start=False, stop=(j == J - 1), skip_group_check=True)
                        o.then_inc(S["y_ps"], 1)
                    if attend:
                        pe.wait_ge(S["aT"], i + 1)
                        mm(small_ps[:, 0:H], a_t[:, :], wqkv[:, 2 * H:3 * H], start=True, stop=True)\
                            .then_inc(S["kv_ps"], 1)
                    if route:
                        pe.wait_ge(S["lgt"], r + 1)
                        alone(pe)
                        for j in range(J):
                            o = nc.tensor.transpose(kg_ps[:, j * E:(j + 1) * E], lgt[:, j * P:(j + 1) * P],
                                                    ident[0:E, 0:E])
                        o.then_inc(S["lg_ps"], 1)
                    if share:
                        gate(m, c + 1)
                        up(m, c + 1)
                        down_behind(m, c + 1)
                    if route:
                        pe.wait_ge(S["mask"], r + 1)
                        need(pe, S["takenb"], r)
                        rank, chosen = je(kg_ps[:, 0:J * E]), je(mask[:, :])
                        mm(rank, onesb[:, :], takenb[:, :].rearrange("p (o e) -> p o e", o=1).broadcast_to([P, J, E]),
                           start=True, stop=False, skip_group_check=True)
                        for j in range(J):
                            o = mm(rank, before[:, :], chosen[:, j:j + 1, :].broadcast_to([P, J, E]), start=False,
                                   stop=(j == J - 1), skip_group_check=True)
                            if j < J - 1:
                                mm(rank[:, j + 1:J, :], identb[:, :],
                                   chosen[:, j:j + 1, :].broadcast_to([P, J - 1 - j, E]),
                                   start=False, stop=False, skip_group_check=True)
                        o.then_inc(S["rank_ps"], 1)
                    if share:
                        gate(m, c + 2)
                        up(m, c + 2)
                        down_behind(m, c + 2)
                    if ahead:
                        turn_xn(i + 1)
                    if share and q == 0 and later:
                        if ahead:
                            pe.wait_ge(S["xnT"], i + 2)
                        elif project:
                            pe.wait_ge(S["oa"], n + 1)
                        shared_rows(m - 1)
                    if attend:
                        pe.wait_ge(S["kvm"], i + 1)
                        pe.wait_ge(S["silu_q"], i + 1)
                        if project:
                            pe.wait_ge(S["res"], n + 1)
                        for j in range(J):
                            o = mm(tile_of(oy_ps, j), q_t[:, j * P:(j + 1) * P], kvm[:, :], start=True, stop=True)
                        o.then_inc(S["out_ps"], 1)
                    if share:
                        gate(m, c + 3)
                        up(m, c + 3)
                    if project:
                        pe.wait_ge(S["xf"], n + 1)
                        if ahead:
                            pe.wait_ge(S["xnT"], i + 2)
                        elif attend:
                            pe.wait_ge(S["ek"], i + 1)
                        if share and q == 0 and later:
                            pe.wait_ge(S["yr"], m)
                        transposes(turn_ps, xf[1 - q]).then_inc(S["xfT_ps"], 1)
                    if share:
                        down_behind(m, c + 3)

                pe.wait_ge(S["weights"], 12 * 16)
                mm(small_ps[:, 0:H], g1[:, :], g2[:, :], start=True, stop=True)
                mm(small_ps[:, H:H + 1], g2[:, :], bg1[:, :], start=True, stop=True).then_inc(S["wg_psum"], 1)
                pe.wait_ge(S["ident"], 7)
                pe.wait_ge(S["wg_copied"], 1)
                pe.wait_ge(S["bg_ready"], 1)
                pe.wait_ge(S["setup_dve"], 8)
                turn_xn(0)
                steps(pe.Fori, step)
                pe.wait_ge(S["xf_lo"], B)
                for c in range(CS - LAG, CS):
                    down(SHARED_1 - 1, c)
                shared_rows(SHARED_1 - 1)

        with ExitStack() as c2:
            def sb2(name, shape, dt=F32):
                return c2.enter_context(nc.sbuf_tensor(name, shape, dt))

            UPB = CR
            UPE = NBLK * CR
            W = CR * P
            w_hi = [sb2(f"w_hi{q}", [P, 3 * W], F32R) for q in range(2)]
            w_lo = [sb2(f"w_lo{q}", [P, 3 * W], F32R) for q in range(2)]
            xg = [sb2(f"xg{q}", [P, N]) for q in range(2)]
            xt_hi = [sb2(f"xt_hi{q}", [P, N], F32R) for q in range(2)]
            xt_lo = [sb2(f"xt_lo{q}", [P, N], F32R) for q in range(2)]
            gated = sb2("gated", [P, N])
            hid = [sb2(f"hid{q}", [P, N]) for q in range(2)]
            h_hi = [sb2(f"h_hi{q}", [P, N], F32R) for q in range(RING)]
            h_lo = [sb2(f"h_lo{q}", [P, N], F32R) for q in range(RING)]
            y_t = sb2("y_t", [P, N])
            y_rows = [sb2(f"y_rows{q}", [P, N]) for q in range(2)]
            gate_ps, up_ps, y_ps, xt_ps, yr_ps = bank[0:2], bank[2:4], bank[4:6], bank[6], bank[7]

            rd_sum = sb2("rd_sum", [P, CR])
            names = ("r_wsum r_wcentred r_whi r_wlo r_xt_ps r_xt_hi r_xt_lo r_gate r_up r_silu r_hid r_hhi r_hlo r_down "
                     "r_yt r_yr_ps r_yr").split()
            R = {n: sem(n) for n in names}
            x_in = [sem(f"r_x_in{q}") for q in range(2)]
            y_out = [sem(f"r_y_out{q}") for q in range(2)]

            PAIR = 2 * NBLK
            assert PAIR % 2 == 0 and NBLK * CR % RING == 0

            def size(k):
                return BLOCKS[k % NBLK][1]

            block = c2.enter_context(nc.Block())

            @block.sync
            def _(sp):
                def load_w(e):
                    for dst, src in expert_loads(e):
                        sp.dma_start(dst, src).then_inc(w_in, 16)

                def slot_rows(t, e, k):
                    a, n = BLOCKS[k % NBLK]
                    return t[ds(e * CAP + a, n)].rearrange("(p j) h -> p (j h)", p=P)

                def load_x(e, k):
                    sp.dma_start(xg[k % 2][:, 0:size(k)], slot_rows(slot_x, e, k)).then_inc(x_in[k % 2], 16)

                def store_y(m, k, cold):
                    sp.wait_ge(R["r_yr"], m * PAIR + k + 1)
                    sp.dma_start(slot_rows(slot_y, m * 2 + k // NBLK, k), y_rows[k % 2][:, 0:size(k)])\
                      .then_inc(y_out[k % 2], 16)

                def pair(m, first, last):
                    for k in range(PAIR):
                        nxt = k + 2
                        if not (last and nxt >= PAIR):
                            sp.wait_ge(R["r_xt_ps"], m * PAIR + k + 1)
                            load_x(m * 2 + nxt // NBLK, nxt)
                        if k >= 3:
                            store_y(m, k - 3, first)
                        elif not first:
                            store_y(m - 1, PAIR + k - 3, first)
                        if k % NBLK == 0 and not (last and k >= NBLK):
                            sp.wait_ge(R["r_wlo"], m * 2 + k // NBLK + 1)
                            load_w(m * 2 + k // NBLK + 1)

                M = E // 2
                load_x(0, 0)
                load_x(0, 1)
                pair(0, True, False)
                with sp.Fori(1, M - 1) as m:
                    pair(m, False, False)
                pair(M - 1, False, True)
                for k in range(PAIR - 3, PAIR):
                    store_y(M - 1, k, False)
                for q in range(2):
                    sp.wait_ge(y_out[q], 16 * E * NBLK // 2)

            def unit(m, c):
                return m * (2 * UPE) + c

            @block.scalar
            def _(act):
                def split_w(m, q, warm):
                    act.wait_ge(R["r_wcentred"], m * 2 + q + 1)
                    if warm:
                        act.wait_ge(R["r_down"], unit(m - 1, (q + 1) * UPE))
                    nc.scalar.activation(w_hi[q][:, :], raw[:, :], ACT.Copy).then_inc(R["r_whi"], 1)

                def split_x(m, k, warm):
                    b = m * PAIR + k
                    act.wait_ge(R["r_xt_ps"], b + 1)
                    if warm or k >= 2:
                        act.wait_ge(R["r_up"], unit(m, (k - 1) * CR))
                    nc.scalar.activation(xt_hi[k % 2][:, 0:size(k)], xt_ps[:, 0:size(k)],
                                         ACT.Copy).then_inc(R["r_xt_hi"], 1)

                def silu(m, c, warm):
                    act.wait_ge(R["r_gate"], unit(m, c) + 1)
                    if warm or c >= 1:
                        act.wait_ge(R["r_hid"], unit(m, c))
                    n = size(c // CR)
                    nc.scalar.activation(gated[:, 0:n], gate_ps[c % 2][:, 0:n], ACT.Silu).then_inc(R["r_silu"], 1)

                def high(m, c, warm):
                    act.wait_ge(R["r_hid"], unit(m, c) + 1)
                    if warm or c >= RING:
                        act.wait_ge(R["r_down"], unit(m, c) - RING + 1)
                    n = size(c % (2 * UPE) // CR)
                    nc.scalar.activation(h_hi[c % RING][:, 0:n], hid[c % 2][:, 0:n], ACT.Copy).then_inc(R["r_hhi"], 1)

                def y_copy(m, k, warm):
                    b = m * PAIR + k
                    act.wait_ge(R["r_down"], b * CR + CR)
                    if warm or k >= 1:
                        act.wait_ge(R["r_yr_ps"], b)
                    n = size(k)
                    nc.scalar.activation(y_t[:, 0:n], y_ps[k % 2][:, 0:n], ACT.Copy).then_inc(R["r_yt"], 1)

                def pair(m, first, last):
                    for c in range(2 * UPE):
                        k = c // CR
                        silu(m, c, not first)
                        if not (first and c < 1):
                            if c >= 1:
                                high(m, c - 1, not first)
                            else:
                                high(m - 1, 2 * UPE - 1, True)
                        if c % CR == 1 and not (last and k == PAIR - 1):
                            if k + 1 < PAIR:
                                split_x(m, k + 1, not first)
                            else:
                                split_x(m + 1, 0, True)
                        if c % CR == 3 and not (first and k == 0):
                            if k >= 1:
                                y_copy(m, k - 1, not first or k >= 3)
                            else:
                                y_copy(m - 1, PAIR - 1, True)
                        if c % UPE == UPE // 2:
                            q = c // UPE
                            if q == 0:
                                split_w(m, 1, not first)
                            elif not last:
                                split_w(m + 1, 0, True)

                M = E // 2
                split_w(0, 0, False)
                split_x(0, 0, False)
                pair(0, True, False)
                with act.Fori(1, M - 1) as m:
                    pair(m, False, False)
                pair(M - 1, False, True)
                high(M - 1, 2 * UPE - 1, True)
                y_copy(M - 1, PAIR - 1, True)

            @block.gpsimd
            def _(g):
                def low(m, c, warm):
                    g.wait_ge(R["r_hhi"], unit(m, c) + 1)
                    if warm or c >= RING:
                        g.wait_ge(R["r_down"], unit(m, c) - RING + 1)
                    n = size(c // CR)
                    g.tensor_tensor(h_lo[c % RING][:, 0:n], hid[c % 2][:, 0:n],
                                    h_hi[c % RING][:, 0:n].bitcast(F32), ALU.subtract).then_inc(R["r_hlo"], 1)

                for c in range(2 * UPE):
                    low(0, c, False)
                with g.Fori(1, E // 2) as m:
                    for c in range(2 * UPE):
                        low(m, c, True)

            @block.vector
            def _(v):
                def centre_w(m, q):
                    w = raw[:, 2 * W:3 * W].rearrange("p (c h) -> p c h", h=H)
                    v.wait_ge(w_in, (m * 2 + q + 1) * 48)
                    v.reduce_sum(rd_sum[:, :], w, AX.X).then_inc(R["r_wsum"], 1)
                    v.wait_ge(R["r_wsum"], m * 2 + q + 1)
                    v.scalar_tensor_tensor(out=w, in0=rd_sum[:, :].rearrange("p (c o) -> p c o", o=1)
                                           .broadcast_to([P, CR, H]), scalar=-1.0 / H, in1=w,
                                           op0=ALU.mult, op1=ALU.add).then_inc(R["r_wcentred"], 1)

                def split_w(m, q, warm):
                    v.wait_ge(R["r_whi"], m * 2 + q + 1)
                    v.tensor_tensor(w_lo[q][:, :], raw[:, :], w_hi[q][:, :].bitcast(F32),
                                    ALU.subtract).then_inc(R["r_wlo"], 1)

                def split_x(m, k):
                    b = m * PAIR + k
                    v.wait_ge(R["r_xt_hi"], b + 1)
                    v.tensor_tensor(xt_lo[k % 2][:, 0:size(k)], xt_ps[:, 0:size(k)],
                                    xt_hi[k % 2][:, 0:size(k)].bitcast(F32), ALU.subtract).then_inc(R["r_xt_lo"], 1)

                def hidden(m, c, warm):
                    v.wait_ge(R["r_silu"], unit(m, c) + 1)
                    v.wait_ge(R["r_up"], unit(m, c) + 1)
                    if warm or c >= 2:
                        v.wait_ge(R["r_hlo"], unit(m, c) - 1)
                    n = size(c // CR)
                    v.tensor_tensor(hid[c % 2][:, 0:n], gated[:, 0:n], up_ps[c % 2][:, 0:n],
                                    ALU.mult).then_inc(R["r_hid"], 1)

                def y_copy(m, k, warm):
                    b = m * PAIR + k
                    v.wait_ge(R["r_yr_ps"], b + 1)
                    if warm or k >= 2:
                        v.wait_ge(y_out[k % 2], (m * (PAIR // 2) + k // 2) * 16)
                    n = size(k)
                    v.tensor_copy(y_rows[k % 2][:, 0:n], yr_ps[:, 0:n]).then_inc(R["r_yr"], 1)

                def pair(m, first, last):
                    for c in range(2 * UPE):
                        k = c // CR
                        hidden(m, c, not first)
                        if c % CR == 1 and not (last and k == PAIR - 1):
                            if k + 1 < PAIR:
                                split_x(m, k + 1)
                            else:
                                split_x(m + 1, 0)
                        if c % CR == 2 and not (first and k < 2):
                            if k >= 2:
                                y_copy(m, k - 2, not first)
                            else:
                                y_copy(m - 1, PAIR - 2 + k, True)
                        if c % UPE in (CR - 1, UPE // 2):
                            work = centre_w if c % UPE == CR - 1 else lambda m, q: split_w(m, q, True)
                            if c < UPE:
                                work(m, 1)
                            elif not last:
                                work(m + 1, 0)

                M = E // 2
                centre_w(0, 0)
                split_w(0, 0, False)
                split_x(0, 0)
                pair(0, True, False)
                with v.Fori(1, M - 1) as m:
                    pair(m, False, False)
                pair(M - 1, False, True)
                y_copy(M - 1, PAIR - 2, True)
                y_copy(M - 1, PAIR - 1, True)

            @block.tensor
            def _(pe):
                mm = nc.tensor.matmul

                def x_in_t(m, k, warm):
                    n = size(k)
                    half = m * (PAIR // 2) + k // 2
                    pe.wait_ge(x_in[k % 2], half * 16 + 16)
                    if warm or k >= 1:
                        pe.wait_ge(R["r_xt_lo"], m * PAIR + k)
                    for j in range(n // P):
                        o = nc.tensor.transpose(xt_ps[:, j * P:(j + 1) * P], xg[k % 2][:, j * P:(j + 1) * P],
                                                ident[:, :])
                    o.then_inc(R["r_xt_ps"], 1)

                def product(dst, q, wa, a_hi, a_lo, start, stop):
                    mm(dst, w_lo[q][:, wa:wa + P], a_hi, start=start, stop=False)
                    mm(dst, w_hi[q][:, wa:wa + P], a_lo, start=False, stop=False)
                    return mm(dst, w_hi[q][:, wa:wa + P], a_hi, start=False, stop=stop)

                def gate_up(m, c, warm):
                    k, q = c // CR, c // UPE
                    n = size(k)
                    if c % CR == 0:
                        pe.wait_ge(R["r_xt_lo"], m * PAIR + k + 1)
                    if c % UPE == 0:
                        pe.wait_ge(R["r_wlo"], m * 2 + q + 1)
                    if warm or c >= 2:
                        pe.wait_ge(R["r_silu"], unit(m, c) - 1)
                    a = (xt_hi[k % 2][:, 0:n], xt_lo[k % 2][:, 0:n])
                    wa = (c % CR) * P
                    product(gate_ps[c % 2][:, 0:n], q, wa, *a, True, True).then_inc(R["r_gate"], 1)
                    if warm or c >= 2:
                        pe.wait_ge(R["r_hid"], unit(m, c) - 1)
                    product(up_ps[c % 2][:, 0:n], q, W + wa, *a, True, True).then_inc(R["r_up"], 1)

                def down(m, c, warm):
                    k, q = c // CR, c // UPE
                    n = size(k)
                    pe.wait_ge(R["r_hlo"], unit(m, c) + 1)
                    if c % CR == 0 and (warm or k >= 2):
                        pe.wait_ge(R["r_yt"], m * PAIR + k - 1)
                    product(y_ps[k % 2][:, 0:n], q, 2 * W + (c % CR) * P, h_hi[c % RING][:, 0:n],
                            h_lo[c % RING][:, 0:n], c % CR == 0, c % CR == CR - 1).then_inc(R["r_down"], 1)

                def y_in_rows(m, k, warm):
                    b = m * PAIR + k
                    pe.wait_ge(R["r_yt"], b + 1)
                    if warm or k >= 1:
                        pe.wait_ge(R["r_yr"], b)
                    for j in range(size(k) // P):
                        o = nc.tensor.transpose(yr_ps[:, j * P:(j + 1) * P], y_t[:, j * P:(j + 1) * P],
                                                ident[:, :])
                    o.then_inc(R["r_yr_ps"], 1)

                def pair(m, first, last):
                    U = 2 * UPE
                    for c in range(U):
                        k = c // CR
                        gate_up(m, c, not first)
                        if c % CR == 0 and not (last and k == PAIR - 1):
                            if k + 1 < PAIR:
                                x_in_t(m, k + 1, True)
                            else:
                                x_in_t(m + 1, 0, True)
                        if c >= LAG:
                            down(m, c - LAG, not first)
                        elif not first:
                            down(m - 1, U + c - LAG, True)
                        if c % CR == 1 and not (first and k < 2):
                            if k >= 2:
                                y_in_rows(m, k - 2, True)
                            else:
                                y_in_rows(m - 1, PAIR - 2 + k, True)

                M = E // 2
                x_in_t(0, 0, False)
                pair(0, True, False)
                with pe.Fori(1, M - 1) as m:
                    pair(m, False, False)
                pair(M - 1, False, True)
                for c in range(2 * UPE - LAG, 2 * UPE):
                    down(M - 1, c, True)
                y_in_rows(M - 1, PAIR - 2, True)
                y_in_rows(M - 1, PAIR - 1, True)

        with ExitStack() as c3:
            def sb3(name, shape, dt=F32):
                return c3.enter_context(nc.sbuf_tensor(name, shape, dt))

            HB = B // 2
            gated = [sb3(f"t_gated{q}", [P, N]) for q in range(2)]
            hid = [sb3(f"t_hid{q}", [P, N]) for q in range(2)]
            h_hi = [sb3(f"t_h_hi{q}", [P, N], F32R) for q in range(RING)]
            h_lo = [sb3(f"t_h_lo{q}", [P, N], F32R) for q in range(RING)]
            y_t = sb3("t_y_t", [P, N])
            KEPT, FRESH = 0, 1
            routed = [[sb3(f"routed{w}{k}", [P, N]) for k in range(K)] for w in range(2)]
            idx = [sb3(f"idx{w}", [P, K * J], U32) for w in range(2)]
            z = [sb3(f"z{w}", [P, N]) for w in range(2)]
            squares = sb3("t_squares", [P, N])
            ssq = [sb3(f"ssq{w}", [P, J]) for w in range(2)]
            ve = sb3("t_ve", [P, 2 * J])
            rs = sb3("t_rs", [P, 2 * J])
            fin = [sb3(f"fin{w}", [P, N]) for w in range(2)]
            gate_ps, up_ps, y_ps, yr_ps = bank[0:2], bank[2:4], bank[4], bank[6]

            names = ("t_ones t_gate t_up t_silu t_hid t_hhi t_hlo t_down "
                     "t_yt t_yr_ps t_ve t_rs").split()
            Q = {n: sem(n) for n in names}
            idx_set, gathered, z_first, z_done, ssq_done, fin_done, stored = (
                [sem(f"t_{n}{w}") for w in range(2)]
                for n in "idx gathered z_first z_done ssq fin stored".split())
            GATHERS = 16 * K * J
            tile_of = lambda t, j: t[:, j * H:(j + 1) * H]
            batch = (lambda g: g, lambda g: g + HB)

            block = c3.enter_context(nc.Block())

            @block.sync
            def _(sp):
                with sp.Fori(0, HB) as g:
                    for w in range(2):
                        sp.wait_ge(fin_done[w], g + 1)
                        sp.dma_start(out[ds(batch[w](g), 1)].rearrange("b (p j) h -> p (b j h)", p=P), fin[w][:, :])\
                          .then_inc(stored[w], 16)
                for w in range(2):
                    sp.wait_ge(stored[w], 16 * HB)

            @block.scalar
            def _(act):
                def copy(dst, src):
                    return nc.scalar.activation(dst, src, ACT.Copy)

                def silu(g, c):
                    act.wait_ge(Q["t_gate"], g * CS + c + 1)
                    need(act, Q["t_hid"], g * CS + c - 1)
                    nc.scalar.activation(gated[c % 2][:, :], gate_ps[c % 2][:, :], ACT.Silu).then_inc(Q["t_silu"], 1)

                def high(g, c):
                    act.wait_ge(Q["t_hid"], g * CS + c + 1)
                    need(act, Q["t_down"], g * CS + c - RING + 1)
                    copy(h_hi[c % RING][:, :], hid[c % 2][:, :]).then_inc(Q["t_hhi"], 1)

                def y_copy(g):
                    act.wait_ge(Q["t_down"], g * CS + CS)
                    need(act, Q["t_yr_ps"], g)
                    copy(y_t[:, :], y_ps[:, :]).then_inc(Q["t_yt"], 1)

                def squares_of(w, g):
                    act.wait_ge(z_done[w], g + 1)
                    for j in range(J):
                        o = nc.scalar.activation(tile_of(squares, j), tile_of(z[w], j), ACT.Square,
                                                 accum_out=ssq[w][:, j:j + 1])
                    o.then_inc(ssq_done[w], 1)

                def step(g, first):
                    for c in range(CS):
                        silu(g, c)
                        if c >= 1:
                            high(g, c - 1)
                        elif not first:
                            high(g - 1, CS - 1)
                        if c == LAG and not first:
                            y_copy(g - 1)
                        if c == LAG:
                            squares_of(KEPT, g)
                        if c == CS - 2 and not first:
                            squares_of(FRESH, g - 1)

                step(0, True)
                step(1, False)
                with act.Fori(2, HB) as g:
                    step(g, False)
                high(HB - 1, CS - 1)
                y_copy(HB - 1)
                squares_of(FRESH, HB - 1)

            @block.gpsimd
            def _(gp):
                def gather(w, g, cs):
                    for c in cs:
                        gp.indirect_dma_start(out=tile_of(routed[w][c // J], c % J), out_offset=None, in_=slot_y,
                                              in_offset=bass.IndirectOffsetOnAxis(ap=idx[w][:, c:c + 1], axis=0),
                                              bounds_check=SLOTS, oob_is_err=False).then_inc(gathered[w], 16)

                def step(g, first, last):
                    if not last:
                        gp.wait_ge(idx_set[KEPT], g + 2)
                        gp.wait_ge(z_done[KEPT], g + 1)
                        alone(gp)
                        gather(KEPT, g + 1, range(K * J))
                    gp.wait_ge(idx_set[FRESH], g + 1)
                    if not first:
                        gp.wait_ge(z_done[FRESH], g)
                    alone(gp)
                    gather(FRESH, g, range(0, J))
                    gp.wait_ge(Q["t_ve"], g + 1)
                    gp.tensor_tensor(rs[:, :], ve[:, :], mhalf[:, 0:2 * J], ALU.pow).then_inc(Q["t_rs"], 1)
                    gather(FRESH, g, range(J, 2 * J))

                gp.wait_ge(idx_set[KEPT], 1)
                gather(KEPT, 0, range(K * J))
                step(0, True, False)
                with gp.Fori(1, HB - 1) as g:
                    step(g, False, False)
                step(HB - 1, False, True)
                gp.wait_ge(Q["t_ve"], HB + 1)
                gp.tensor_tensor(rs[:, :], ve[:, :], mhalf[:, 0:2 * J], ALU.pow).then_inc(Q["t_rs"], 1)

            @block.vector
            def _(v):
                def index(w, g):
                    need(v, gathered[w], g * GATHERS)
                    v.tensor_copy(idx[w][:, :], slots[:, ds(batch[w](g) * K * J, K * J)]).then_inc(idx_set[w], 1)

                def hidden(g, c):
                    v.wait_ge(Q["t_silu"], g * CS + c + 1)
                    v.wait_ge(Q["t_up"], g * CS + c + 1)
                    need(v, Q["t_hlo"], g * CS + c - 1)
                    v.tensor_tensor(hid[c % 2][:, :], gated[c % 2][:, :], up_ps[c % 2][:, :],
                                    ALU.mult).then_inc(Q["t_hid"], 1)

                def low(g, c):
                    v.wait_ge(Q["t_hhi"], g * CS + c + 1)
                    need(v, Q["t_down"], g * CS + c - RING + 1)
                    v.tensor_tensor(h_lo[c % RING][:, :], hid[c % 2][:, :], h_hi[c % RING][:, :].bitcast(F32),
                                    ALU.subtract).then_inc(Q["t_hlo"], 1)

                def mix_first(w, g):
                    v.wait_ge(gathered[w], g * GATHERS + GATHERS)
                    if w == FRESH:
                        v.wait_ge(Q["t_yr_ps"], g + 1)
                    need(v, fin_done[w], g)
                    for j in range(J):
                        part = tile_of(yr_ps, j) if w == FRESH else shared[:, ds(g * N + j * H, H)]
                        o = v.scalar_tensor_tensor(out=tile_of(z[w], j), in0=tile_of(routed[w][0], j),
                                                   scalar=wts[:, ds(batch[w](g) * K * J + j, 1)], in1=part,
                                                   op0=ALU.mult, op1=ALU.add)
                    o.then_inc(z_first[w], 1)

                def mix_second(w, g):
                    v.wait_ge(z_first[w], g + 1)
                    alone(v)
                    for j in range(J):
                        o = v.scalar_tensor_tensor(out=tile_of(z[w], j), in0=tile_of(routed[w][1], j),
                                                   scalar=wts[:, ds(batch[w](g) * K * J + J + j, 1)],
                                                   in1=tile_of(z[w], j), op0=ALU.mult, op1=ALU.add)
                    o.then_inc(z_done[w], 1)

                def variance(w, g):
                    v.wait_ge(ssq_done[w], g + 1)
                    return v.tensor_scalar(ve[:, w * J:(w + 1) * J], ssq[w][:, :], 1.0 / H, LN_EPS, ALU.mult, ALU.add)

                def final(w, g, powers):
                    v.wait_ge(Q["t_rs"], powers)
                    need(v, stored[w], g * 16)
                    alone(v)
                    for j in range(J):
                        o = v.scalar_tensor_tensor(out=tile_of(fin[w], j), in0=tile_of(z[w], j),
                                                   scalar=rs[:, w * J + j:w * J + j + 1],
                                                   in1=res[:, ds(batch[w](g) * N + j * H, H)],
                                                   op0=ALU.mult, op1=ALU.add)
                    o.then_inc(fin_done[w], 1)

                def step(g, first, second, last):
                    for c in range(CS):
                        hidden(g, c)
                        if c >= 1:
                            low(g, c - 1)
                        elif not first:
                            low(g - 1, CS - 1)
                        if c == 0:
                            if not first:
                                final(KEPT, g - 1, g)
                            if not first and not second:
                                final(FRESH, g - 2, g)
                            if first:
                                index(FRESH, g)
                        if c == 1:
                            mix_first(KEPT, g)
                            if not last:
                                index(KEPT, g + 1)
                        if c == 2:
                            mix_second(KEPT, g)
                        if c == 4 and not first:
                            index(FRESH, g)
                            mix_first(FRESH, g - 1)
                        if c == 5 and not first:
                            mix_second(FRESH, g - 1)
                        if c == CS - 1:
                            o = variance(KEPT, g)
                            if not first:
                                o = variance(FRESH, g - 1)
                            o.then_inc(Q["t_ve"], 1)

                index(KEPT, 0)
                v.memset(ve[:, :], 1.0).then_inc(Q["t_ones"], 1)
                step(0, True, False, False)
                step(1, False, True, False)
                with v.Fori(2, HB - 1) as g:
                    step(g, False, False, False)
                step(HB - 1, False, False, True)
                low(HB - 1, CS - 1)
                final(KEPT, HB - 1, HB)
                final(FRESH, HB - 2, HB)
                mix_first(FRESH, HB - 1)
                mix_second(FRESH, HB - 1)
                variance(FRESH, HB - 1).then_inc(Q["t_ve"], 1)
                final(FRESH, HB - 1, HB + 1)

            @block.tensor
            def _(pe):
                mm = nc.tensor.matmul

                def product(dst, wa, a_hi, a_lo, start, stop):
                    mm(dst, s_lo[:, wa:wa + P], a_hi, start=start, stop=False)
                    mm(dst, s_hi[:, wa:wa + P], a_lo, start=False, stop=False)
                    return mm(dst, s_hi[:, wa:wa + P], a_hi, start=False, stop=stop)

                def gate_up(g, c):
                    b = batch[FRESH](g)
                    need(pe, Q["t_silu"], g * CS + c - 1)
                    a = (xf_hi[:, ds(b * N, N)], xf_lo[:, ds(b * N, N)])
                    product(gate_ps[c % 2][:, :], c * P, *a, True, True).then_inc(Q["t_gate"], 1)
                    need(pe, Q["t_hid"], g * CS + c - 1)
                    product(up_ps[c % 2][:, :], IS + c * P, *a, True, True).then_inc(Q["t_up"], 1)

                def down(g, c):
                    pe.wait_ge(Q["t_hlo"], g * CS + c + 1)
                    if c == 0:
                        need(pe, Q["t_yt"], g)
                    product(y_ps[:, :], 2 * IS + c * P, h_hi[c % RING][:, :], h_lo[c % RING][:, :],
                            c == 0, c == CS - 1).then_inc(Q["t_down"], 1)

                def y_in_rows(g):
                    pe.wait_ge(Q["t_yt"], g + 1)
                    need(pe, z_first[FRESH], g)
                    for j in range(J):
                        o = nc.tensor.transpose(yr_ps[:, j * P:(j + 1) * P], y_t[:, j * P:(j + 1) * P], ident[:, :])
                    o.then_inc(Q["t_yr_ps"], 1)

                def step(g, first):
                    for c in range(CS):
                        gate_up(g, c)
                        if c >= LAG:
                            down(g, c - LAG)
                        elif not first:
                            down(g - 1, CS + c - LAG)
                        if c == LAG + 1 and not first:
                            y_in_rows(g - 1)

                step(0, True)
                step(1, False)
                with pe.Fori(2, HB) as g:
                    step(g, False)
                for c in range(CS - LAG, CS):
                    down(HB - 1, c)
                y_in_rows(HB - 1)


def kernel(**inputs):
    import numpy as np
    import concourse.bacc as bacc
    from concourse.bass_utils import run_bass_kernel_spmd

    a = {n: np.ascontiguousarray(v) for n, v in inputs.items()}
    arrays = {
        "x": a["L0_attn_x"],
        "w_qkv_t": np.ascontiguousarray(a["L0_attn_w_qkv"].T),
        "b_qkv": a["L0_attn_b_qkv"],
        "b_qkv_t": np.ascontiguousarray(a["L0_attn_b_qkv"].reshape(3, H).T),
        "w_g1": a["L0_attn_w_g1"],
        "b_g1": a["L0_attn_b_g1"],
        "w_g2_t": np.ascontiguousarray(a["L0_attn_w_g2"].T),
        "b_g2": a["L0_attn_b_g2"],
        "w_out_t": np.ascontiguousarray(a["L0_attn_w_out"].T),
        "b_out": a["L0_attn_b_out"],
        "ln_g": a["L0_attn_ln_g"],
        "ln_b": a["L0_attn_ln_b"],
        "router_t": np.ascontiguousarray(a["L0_ffn_router_w"].T),
        "rg": a["L0_ffn_rg"],
        "ru": a["L0_ffn_ru"],
        "rd": a["L0_ffn_rd"],
        "sg": a["L0_ffn_sg"],
        "su": a["L0_ffn_su"],
        "sd": a["L0_ffn_sd"],
    }
    nc = bacc.Bacc("TRN2", target_bir_lowering=False, num_devices=1)
    args = [nc.dram_tensor(n, v.shape, F32, kind="ExternalInput").ap() for n, v in arrays.items()]
    out = nc.dram_tensor("out", arrays["x"].shape, F32, kind="ExternalOutput").ap()
    build(nc, *args, out)
    r = run_bass_kernel_spmd(nc, [arrays], core_ids=[0])
    return r.results[0]["out"]
```

```python
from contextlib import ExitStack

import concourse.bass as bass
from concourse import mybir

ALU = mybir.AluOpType
ACT = mybir.ActivationFunctionType
AX = mybir.AxisListType
F32 = mybir.dt.float32
F32R = mybir.dt.float32r
BF16 = mybir.dt.bfloat16
U32 = mybir.dt.uint32
ts = bass.ts
ds = bass.ds

P = 128
H = 128
LN_EPS = 1e-5
RMS_EPS = 1.1920929e-07
HEAD_DIM = 8


def build(nc, x, w_qkv_t, b_qkv, b_qkv_t, w_g1, b_g1, w_g2_t, b_g2, w_out_t, b_out, ln_g, ln_b,
          router_t, rg, ru, rd, sg, su, sd, out):
    B, N, _ = x.shape
    J = N // P
    E = rg.shape[0]
    IR = rg.shape[2]
    IS = sg.shape[1]
    CR = IR // P
    CS = IS // P
    CAP = max(int(1.25 * B * N / E), 1)
    SLOTS = E * CAP
    BLOCKS = [(a, min(N, CAP - a)) for a in range(0, CAP, N)]
    NBLK = len(BLOCKS)
    K = 2
    LAG = 3
    RING = 4

    slot_x = nc.dram_tensor("slot_x", [SLOTS, H], F32, kind="Internal").ap()
    slot_y = nc.dram_tensor("slot_y", [SLOTS + 1, H], F32, kind="Internal").ap()

    with ExitStack() as ctx:
        def sb(name, shape, dt=F32):
            return ctx.enter_context(nc.sbuf_tensor(name, shape, dt))

        def sem(name):
            return ctx.enter_context(nc.semaphore(name))

        bank = [ctx.enter_context(nc.psum_tensor(f"bank{i}", [P, 512], F32)) for i in range(8)]

        passed = sem("passed")

        def alone(eng):
            eng.sem_inc(passed, 1)

        def need(eng, s, count):
            if not isinstance(count, int) or count > 0:
                eng.wait_ge(s, count)

        res = sb("res", [P, B * N])
        xf_hi = sb("xf_hi", [P, B * N], F32R)
        xf_lo = sb("xf_lo", [P, B * N], F32R)
        slots = sb("slots", [P, B * K * J], U32)
        wts = sb("wts", [P, B * K * J])
        ident = sb("ident", [P, P])
        mhalf = sb("mhalf", [P, 3 * J])
        shared = sb("shared", [P, B // 2 * N])
        s_hi = sb("s_hi", [P, 3 * IS], F32R)
        s_lo = sb("s_lo", [P, 3 * IS], F32R)
        raw = sb("raw", [P, 3 * IR])

        w_in = sem("w_in")

        def expert_loads(e):
            return [(raw[:, 0:IR], rg[ds(e, 1)].rearrange("e p i -> p (e i)")),
                    (raw[:, IR:2 * IR], ru[ds(e, 1)].rearrange("e p i -> p (e i)")),
                    (raw[:, 2 * IR:3 * IR].rearrange("p (c h) -> p c h", h=H),
                     rd[ds(e, 1)].rearrange("e (c p) h -> p (e c) h", p=P))]

        rd_sum = sb("rd_sum", [P, IR // P])
        w_summed, w_centred = sem("w_summed"), sem("w_centred")

        def centre_rd(v, e):
            w = raw[:, 2 * IR:3 * IR].rearrange("p (c h) -> p c h", h=H)
            v.wait_ge(w_in, e * 48 + 48)
            v.reduce_sum(rd_sum[:, :], w, AX.X).then_inc(w_summed, 1)
            v.wait_ge(w_summed, e + 1)
            v.scalar_tensor_tensor(out=w, in0=rd_sum[:, :].rearrange("p (c o) -> p c o", o=1)
                                   .broadcast_to([P, CR, H]), scalar=-1.0 / H, in1=w,
                                   op0=ALU.mult, op1=ALU.add).then_inc(w_centred, 1)

        with ExitStack() as c1:
            def sb1(name, shape, dt=F32):
                return c1.enter_context(nc.sbuf_tensor("a_" + name, shape, dt))

            wqkv = sb1("wqkv", [P, 3 * H])
            wo = sb1("wo", [P, H])
            wo_half = sb1("wo_half", [P, H])
            wo_sum = sb1("wo_sum", [P, 1])
            wo_c = sb1("wo_c", [P, H])
            g1 = sb1("g1", [8, H])
            g2 = sb1("g2", [8, H])
            wg = sb1("wg", [P, H])
            bqkv = sb1("bqkv", [P, 3])
            bg1 = sb1("bg1", [8, 1])
            bg2 = sb1("bg2", [P, 1])
            bg_half = sb1("bg_half", [P, 1])
            lng = sb1("lng", [P, 1])
            lnb = sb1("lnb", [P, 1])
            bv_row = sb1("bv_row", [P, H])
            bo_row = sb1("bo_row", [1, H])
            bo_sum = sb1("bo_sum", [1, 1])
            bo_c = sb1("bo_c", [1, H])
            bo_hi = sb1("bo_hi", [1, H], F32R)
            bo_lo = sb1("bo_lo", [1, H], F32R)
            ones_row = sb1("ones_row", [1, P])
            ones_r = sb1("ones_r", [1, P], F32R)
            wr = sb1("wr", [P, E])
            wr_hi = sb1("wr_hi", [P, E], F32R)
            wr_lo = sb1("wr_lo", [P, E], F32R)
            head_mask = sb1("head_mask", [P, H])
            identb = sb1("identb", [P, P], BF16)
            before = sb1("before", [P, P], BF16)
            onesb = sb1("onesb", [P, P], BF16)
            expert_id = sb1("expert_id", [P, J * E])
            expert_base = sb1("expert_base", [P, J * E])
            st = sb1("st", [P, J * 6])
            mv = [sb1(f"mv{q}", [P, J * 2]) for q in range(2)]
            ve = sb1("ve", [P, 2 * J])
            rs = sb1("rs", [P, 2 * J])
            ve_o = sb1("ve_o", [P, J])
            rs_o = sb1("rs_o", [P, J])
            xn = sb1("xn", [P, N])
            xn_t = sb1("xn_t", [P, N])
            q_t = sb1("q_t", [P, N])
            ek_t = sb1("ek_t", [P, N])
            ek = sb1("ek", [P, N])
            tg = [sb1(f"tg{q}", [P, N]) for q in range(2)]
            kmax = sb1("kmax", [P, 1])
            kbias = sb1("kbias", [P, 1])
            ksum = sb1("ksum", [P, 1])
            rksum = sb1("rksum", [P, 1])
            a_t = sb1("a_t", [P, H])
            kv = sb1("kv", [P, H])
            kvh = sb1("kvh", [P, H])
            kv_sum = sb1("kv_sum", [P, 1])
            kvm = sb1("kvm", [P, H])
            ssq_o = sb1("ssq_o", [P, J])
            ssq_y = sb1("ssq_y", [P, J])
            wide = sb1("wide", [P, 8 * N])
            s_raw = wide[:, 0:3 * IS]
            on, oa, u = (wide[:, k * N:(k + 1) * N] for k in range(3))
            xf = [wide[:, k * N:(k + 1) * N] for k in (3, 4)]
            gated = wide[:, 5 * N:6 * N]
            hid = [wide[:, k * N:(k + 1) * N] for k in (6, 7)]
            assert 3 * IS <= 6 * N
            zeros = wide[:, 6 * N:8 * N]
            sd_sum = sb1("sd_sum", [P, CS])
            ve3 = sb1("ve3", [P, J])
            rs3 = sb1("rs3", [P, J])
            st4 = sb1("st4", [P, J * 6])
            mv4 = sb1("mv4", [P, J * 2])
            ve4 = sb1("ve4", [P, J])
            rs4 = sb1("rs4", [P, J])
            ms1 = sb1("ms1", [P, J])
            ms2 = sb1("ms2", [P, J])
            lgt = sb1("lgt", [E, N])
            lg = sb1("lg", [P, J * E])
            top = sb1("top", [P, J * 8])
            topi = sb1("topi", [P, J * 8], U32)
            oh = sb1("oh", [P, K * J * E], BF16)
            mask = sb1("mask", [P, J * E], BF16)
            taken = sb1("taken", [P, E], F32)
            takenb = sb1("takenb", [P, E], BF16)
            newly = sb1("newly", [P, E], F32)
            fits = sb1("fits", [P, J * E])
            place = sb1("place", [P, J * E])
            placed = sb1("placed", [P, J * E])
            picked = sb1("picked", [P, K * J * E])
            slotf = sb1("slotf", [P, K * J])
            slot_now = [sb1(f"slot_now{q}", [P, K * J], U32) for q in range(2)]
            dl = sb1("dl", [P, J])
            dls = sb1("dls", [P, J])
            tw = sb1("tw", [P, J])
            h_hi = [sb1(f"h_hi{q}", [P, N], F32R) for q in range(RING)]
            h_lo = [sb1(f"h_lo{q}", [P, N], F32R) for q in range(RING)]
            y_t = sb1("y_t", [P, N])

            turn_ps, kg_ps, q_ps, oy_ps, small_ps, gate_ps, up_ps, sy_ps = bank

            names = ("consts ident weights zeros_ready filled setup_dve setup_act wg_psum wg_copied bg_ready wo_sums bo_centred bo_hi "
                     "sd_sums sd_centred s_hi_done s_lo_done "
                     "stats1 mv1 ve12 rs12 ve_o rs_o xn xnT_ps xnT q_in k_in g_in kmax kbias exp silu_q tanh_g "
                     "ekT_ps ek aT_ps aT kv_ps kvn kvh rksum kvm out_ps ssq_o on onT_ps oa u y_ps ssq_y "
                     "ve3 rs3 res st4 mv4 ve4 rs4 ms1 ms2 xf xfT_ps xf_hi xf_lo "
                     "lgt_ps lgt lg_ps lg top topi dl oh mask newly taken takenb rank_ps place "
                     "placed picked slotf slot_now slots dls tanh_w wts "
                     "gate up silu hid hhi hlo_even hlo_odd down yt yr_ps yr").split()
            S = {n: sem(n) for n in names}
            x_in = [sem("x_in_even"), sem("x_in_odd")]
            s_in = [sem(f"s_in{k}") for k in range(3)]
            scattered = [sem("scattered_even"), sem("scattered_odd")]
            SCATTERS = 16 * K * J
            SHARED_1 = B // 2
            FILLS = SLOTS * H // P // 1024 + 1

            mean_of = lambda t, j: t[:, 2 * j:2 * j + 1]
            var_of = lambda t: t[:, :].rearrange("p (j s) -> p j s", s=2)[:, :, 1]
            je = lambda t: t.rearrange("p (j e) -> p j e", e=E)
            jh = lambda t: t.rearrange("p (j h) -> p j h", h=H)
            tile_of = lambda t, j: t[:, j * H:(j + 1) * H]

            def over_features(t):
                return t.rearrange("p (j o) -> p j o", o=1).broadcast_to([P, J, H])

            def steps(fori, step):
                for i in range(4):
                    step(i // 2, i, i % 2)
                with fori(2, B // 2 - 1) as h:
                    step(h, h * 2, 0)
                    step(h, h * 2 + 1, 1)
                for i in range(B - 2, B + 2):
                    step(i // 2, i, i % 2)

            def stages(i):
                if not isinstance(i, int):
                    return (True,) * 7
                return i < B, 1 <= i <= B, i >= 2, i >= 2, i + 1 < B, i + 2 < B, i >= 3

            block = c1.enter_context(nc.Block())

            @block.sync
            def _(sp):
                loads = [(wqkv[:, :], w_qkv_t), (wo[:, :], w_out_t), (g1[:, :], w_g1), (g2[:, :], w_g2_t),
                         (bqkv[:, :], b_qkv_t),
                         (bg1[:, :], b_g1.rearrange("(p o) -> p o", o=1)),
                         (bg2[:, :], b_g2.rearrange("(p o) -> p o", o=1)),
                         (lng[:, :], ln_g.rearrange("(p o) -> p o", o=1)),
                         (lnb[:, :], ln_b.rearrange("(p o) -> p o", o=1)),
                         (bv_row[:, :], b_qkv[2 * H:3 * H].rearrange("(o h) -> o h", o=1).broadcast_to([P, H])),
                         (bo_row[:, :], b_out.rearrange("(o h) -> o h", o=1)),
                         (wr[:, :], router_t)]

                def load_x(i, q):
                    sp.dma_start(res[:, ds(i * N, N)],
                                 x[ds(i, 1)].rearrange("b (p j) h -> p (b j h)", p=P)).then_inc(x_in[q], 16)

                load_x(0, 0)
                for dst, src in loads:
                    sp.dma_start(dst, src).then_inc(S["weights"], 16)
                load_x(1, 1)

                def next_x(i, q):
                    sp.wait_ge(S["mv1"], i - 1)
                    load_x(i, q)

                next_x(2, 0)
                sp.dma_start(s_raw[:, 0:IS], sg).then_inc(s_in[0], 16)
                sp.dma_start(s_raw[:, IS:2 * IS], su).then_inc(s_in[1], 16)
                sp.dma_start(s_raw[:, 2 * IS:3 * IS].rearrange("p (c h) -> p c h", h=H),
                             sd.rearrange("(c p) h -> p c h", p=P)).then_inc(s_in[2], 16)
                next_x(3, 1)
                sp.wait_ge(S["zeros_ready"], 1)
                for n in range(FILLS - 1):
                    sp.dma_start(slot_x.rearrange("(p r) h -> p (r h)", p=P)[:, n * 1024:(n + 1) * 1024],
                                 zeros).then_inc(S["filled"], 16)
                sp.dma_start(slot_y[SLOTS:SLOTS + 1, :], zeros[0:1, 0:H]).then_inc(S["filled"], 16)
                with sp.Fori(2, B // 2) as h:
                    for q in range(2):
                        next_x(h * 2 + q, q)
                for dst, src in expert_loads(0):
                    sp.dma_start(dst, src).then_inc(w_in, 16)

            @block.gpsimd
            def _(g):
                g.memset(ident[:, :], 0.0).then_inc(S["consts"], 1)
                g.memset(identb[:, :], 0.0).then_inc(S["consts"], 1)
                g.memset(before[:, :], 1.0).then_inc(S["consts"], 1)
                g.memset(head_mask[:, :], 1.0).then_inc(S["consts"], 1)
                g.memset(mhalf[:, :], -0.5).then_inc(S["consts"], 1)
                g.wait_ge(S["consts"], 5)
                for t in (ident, identb):
                    g.affine_select(out=t[:, :], in_=t[:, :], compare_op=ALU.not_equal, fill=1.0, base=0,
                                    pattern=[[-1, P]], channel_multiplier=1).then_inc(S["ident"], 1)
                g.affine_select(out=before[:, :], in_=before[:, :], compare_op=ALU.is_ge, fill=0.0, base=-1,
                                pattern=[[1, P]], channel_multiplier=-1).then_inc(S["ident"], 1)
                hm = head_mask[:, :].rearrange("p (g r) -> p g r", r=HEAD_DIM)
                g.affine_select(out=hm, in_=hm, compare_op=ALU.is_ge, fill=0.0, base=0,
                                pattern=[[-HEAD_DIM, H // HEAD_DIM], [0, HEAD_DIM]],
                                channel_multiplier=1).then_inc(S["ident"], 1)
                g.wait_ge(S["ident"], 4)
                g.affine_select(out=hm, in_=hm, compare_op=ALU.is_ge, fill=0.0, base=HEAD_DIM - 1,
                                pattern=[[HEAD_DIM, H // HEAD_DIM], [0, HEAD_DIM]],
                                channel_multiplier=-1).then_inc(S["ident"], 1)
                g.iota(expert_id[:, :], pattern=[[0, J], [1, E]], base=0, channel_multiplier=0,
                       allow_small_or_imprecise_dtypes=True).then_inc(S["ident"], 1)
                g.iota(expert_base[:, :], pattern=[[0, J], [CAP, E]], base=-SLOTS, channel_multiplier=0,
                       allow_small_or_imprecise_dtypes=True).then_inc(S["ident"], 1)

                def power(dst, src, ready, done, n, width):
                    g.wait_ge(S[ready], n + 1)
                    g.tensor_tensor(dst[:, 0:width], src[:, 0:width], mhalf[:, 0:width], ALU.pow).then_inc(S[done], 1)

                def low(m, c):
                    g.wait_ge(S["hhi"], m * CS + c + 1)
                    need(g, S["down"], m * CS + c - RING + 1)
                    g.tensor_tensor(h_lo[c % RING][:, :], hid[c % 2], h_hi[c % RING][:, :].bitcast(F32),
                                    ALU.subtract).then_inc(S["hlo_odd"], 1)

                def scatter(q, cs):
                    for c in cs:
                        g.indirect_dma_start(
                            out=slot_x, out_offset=bass.IndirectOffsetOnAxis(ap=slot_now[q][:, c:c + 1], axis=0),
                            in_=tile_of(xf[q], c % J), in_offset=None,
                            bounds_check=SLOTS - 1, oob_is_err=False).then_inc(scattered[q], 16)

                def low_shared(k):
                    g.wait_ge(S["s_hi_done"], k + 1)
                    g.tensor_tensor(s_lo[:, k * IS:(k + 1) * IS], s_raw[:, k * IS:(k + 1) * IS],
                                    s_hi[:, k * IS:(k + 1) * IS].bitcast(F32), ALU.subtract).then_inc(S["s_lo_done"], 1)

                def step(h, i, q):
                    attend, project, route, share, ahead, moments, routed = stages(i)
                    if isinstance(i, int) and i == 0:
                        low_shared(0)
                    if isinstance(i, int) and i == 3:
                        g.wait_ge(S["filled"], 16 * FILLS)
                    if routed:
                        g.wait_ge(S["slot_now"], i - 2)
                        alone(g)
                        scatter(1 - q, range(0, 5))
                    if routed and not (isinstance(i, int) and i >= B):
                        low(h - 1 - (1 - q), 4 * (1 - q) + 3)
                    if project:
                        power(rs3, ve3, "ve3", "rs3", i - 1, J)
                    if routed:
                        scatter(1 - q, range(5, 8))
                    if project:
                        power(rs4, ve4, "ve4", "rs4", i - 1, J)
                    if share and not (isinstance(i, int) and i >= B):
                        low(h - 1, 4 * q + 1)
                    if attend:
                        power(rs_o, ve_o, "ve_o", "rs_o", i, J)
                    if ahead:
                        g.wait_ge(S["xn"], i + 2)
                    if not (isinstance(i, int) and i > B):
                        power(rs, ve, "ve12", "rs12", i + 2, 2 * J)
                    if isinstance(i, int) and i == 0:
                        low_shared(1)
                        low_shared(2)

                g.wait_ge(S["ident"], 7)
                for b in range(2):
                    power(rs, ve, "ve12", "rs12", b, 2 * J)
                steps(g.Fori, step)
                g.wait_ge(S["slot_now"], B)
                scatter((B - 1) % 2, range(K * J))
                power(rs, ve, "ve12", "rs12", B + 3, 2 * J)
                for q in range(2):
                    g.wait_ge(scattered[q], SCATTERS * B // 2)

            @block.scalar
            def _(act):
                def copy(dst, src):
                    return nc.scalar.activation(dst, src, ACT.Copy)

                def squares_of(ready, n, ssq, done, scratch):
                    act.wait_ge(S[ready], n + 1)
                    for j in range(J):
                        o = nc.scalar.activation(tile_of(scratch, j), tile_of(oy_ps, j), ACT.Square,
                                                 accum_out=ssq[:, j:j + 1])
                    o.then_inc(S[done], 1)

                def silu(m, c):
                    act.wait_ge(S["gate"], m * CS + c + 1)
                    need(act, S["hid"], m * CS + c)
                    nc.scalar.activation(gated, gate_ps[:, :], ACT.Silu).then_inc(S["silu"], 1)

                def high(m, c):
                    act.wait_ge(S["hid"], m * CS + c + 1)
                    need(act, S["down"], m * CS + c - RING + 1)
                    copy(h_hi[c % RING][:, :], hid[c % 2]).then_inc(S["hhi"], 1)

                def shared_out(m):
                    act.wait_ge(S["down"], m * CS + CS)
                    need(act, S["yr_ps"], m)
                    copy(y_t[:, :], sy_ps[:, :]).then_inc(S["yt"], 1)

                def shared_rows(m):
                    act.wait_ge(S["yr_ps"], m + 1)
                    copy(shared[:, ds(m * N, N)], small_ps[:, :]).then_inc(S["yr"], 1)

                def weight_tanh(r):
                    act.wait_ge(S["dls"], r + 1)
                    nc.scalar.activation(tw[:, :], dls[:, :], ACT.Tanh, scale=0.5).then_inc(S["tanh_w"], 1)

                def high_shared(k):
                    copy(s_hi[:, k * IS:(k + 1) * IS], s_raw[:, k * IS:(k + 1) * IS]).then_inc(S["s_hi_done"], 1)

                def logits_in(r):
                    act.wait_ge(S["lgt_ps"], r + 1)
                    copy(lgt[:, :], kg_ps[0:E, :]).then_inc(S["lgt"], 1)

                def turn_xn(b):
                    act.wait_ge(S["xnT_ps"], b + 1)
                    need(act, S["g_in"], b)
                    copy(xn_t[:, :], turn_ps[:, :]).then_inc(S["xnT"], 1)

                def step(h, i, q):
                    attend, project, route, share, ahead, moments, routed = stages(i)
                    n, r, m, c = i - 1, i - 2, h - 1, 4 * q
                    later = not (isinstance(m, int) and m == 0)
                    late = isinstance(i, int) and i >= B
                    if attend:
                        act.wait_ge(S["kbias"], i + 1)
                        nc.scalar.activation(ek_t[:, :], kg_ps[:, :], ACT.Exp, bias=kbias[:, 0:1], scale=1.0,
                                             accum_out=ksum[:, 0:1]).then_inc(S["exp"], 1)
                    if project:
                        act.wait_ge(S["onT_ps"], n + 1)
                        nc.scalar.activation(oa, turn_ps[:, :], ACT.Identity, bias=lnb[:, 0:1],
                                             scale=lng[:, 0:1]).then_inc(S["oa"], 1)
                    if attend:
                        act.wait_ge(S["ekT_ps"], i + 1)
                        copy(ek[:, :], small_ps[:, :]).then_inc(S["ek"], 1)
                    if routed:
                        high(m if q == 1 else m - 1, 3 if q == 1 else CS - 1)
                        weight_tanh(r - 1)
                    if attend:
                        act.wait_ge(S["g_in"], i + 1)
                        nc.scalar.activation(tg[q][:, :], kg_ps[:, :], ACT.Tanh, bias=bg_half[:, 0:1],
                                             scale=0.5).then_inc(S["tanh_g"], 1)
                    if share:
                        silu(m, c)
                    if late:
                        logits_in(r)
                    if project:
                        squares_of("y_ps", n, ssq_y, "ssq_y", ek_t)
                    if route and not late:
                        logits_in(r)
                    if attend:
                        act.wait_ge(S["q_in"], i + 1)
                        nc.scalar.activation(q_t[:, :], q_ps[:, :], ACT.Silu, bias=bqkv[:, 0:1],
                                             scale=1.0).then_inc(S["silu_q"], 1)
                    if isinstance(i, int) and i == 0:
                        act.wait_ge(S["bo_centred"], 1)
                        nc.scalar.activation(bo_hi[:, :], bo_c[:, :], ACT.Copy).then_inc(S["bo_hi"], 1)
                        for k in range(2):
                            act.wait_ge(s_in[k], 16)
                            high_shared(k)
                    if share:
                        high(m, c)
                        silu(m, c + 1)
                    if ahead:
                        turn_xn(i + 1)
                    if share:
                        silu(m, c + 2)
                        high(m, c + 1)
                    if attend:
                        squares_of("out_ps", i, ssq_o, "ssq_o", ek)
                    if isinstance(i, int) and i == 0:
                        act.wait_ge(S["sd_centred"], 1)
                        high_shared(2)
                    if share:
                        high(m, c + 2)
                        if q == 0 and later:
                            shared_out(m - 1)
                        silu(m, c + 3)
                    if project:
                        act.wait_ge(S["xfT_ps"], n + 1)
                        copy(xf_hi[:, ds(n * N, N)], turn_ps[:, :]).then_inc(S["xf_hi"], 1)
                    if share and q == 0 and later:
                        shared_rows(m - 1)

                turn_xn(0)
                act.wait_ge(S["weights"], 12 * 16)
                nc.scalar.activation(wr_hi[:, :], wr[:, :], ACT.Copy).then_inc(S["setup_act"], 1)
                nc.scalar.mul(wo_half[:, :], wo[:, :], 0.5).then_inc(S["setup_act"], 1)

                act.wait_ge(S["setup_dve"], 2)
                nc.scalar.activation(ones_r[:, :], ones_row[:, :], ACT.Copy).then_inc(S["bo_hi"], 1)
                act.wait_ge(S["bg_ready"], 1)
                steps(act.Fori, step)
                high(SHARED_1 - 1, CS - 1)
                shared_out(SHARED_1 - 1)
                shared_rows(SHARED_1 - 1)
                weight_tanh(B - 1)

            @block.vector
            def _(v):
                v.memset(zeros, 0.0).then_inc(S["zeros_ready"], 1)
                v.memset(onesb[:, :], 1.0).then_inc(S["setup_dve"], 1)
                v.memset(ones_row[:, :], 1.0).then_inc(S["setup_dve"], 1)
                v.memset(taken[:, :], 0.0).then_inc(S["setup_dve"], 1)
                v.memset(takenb[:, :], 0.0).then_inc(S["setup_dve"], 1)
                v.memset(ve[:, :], 1.0).then_inc(S["setup_dve"], 1)

                def res_tile(b, j):
                    return res[:, ds(b * N + j * H, H)]

                def centre_sd():
                    w = s_raw[:, 2 * IS:3 * IS].rearrange("p (c h) -> p c h", h=H)
                    v.wait_ge(s_in[2], 16)
                    v.reduce_sum(sd_sum[:, :], w, AX.X).then_inc(S["sd_sums"], 1)
                    v.wait_ge(S["sd_sums"], 1)
                    v.scalar_tensor_tensor(out=w, in0=sd_sum[:, :].rearrange("p (c o) -> p c o", o=1)
                                           .broadcast_to([P, CS, H]), scalar=-1.0 / H, in1=w,
                                           op0=ALU.mult, op1=ALU.add).then_inc(S["sd_centred"], 1)

                def hidden(m, c):
                    v.wait_ge(S["silu"], m * CS + c + 1)
                    v.wait_ge(S["up"], m * CS + c + 1)
                    need(v, S["hlo_odd" if c % 2 else "hlo_even"], m * (CS // 2) + c // 2)
                    v.tensor_tensor(hid[c % 2], gated, up_ps[:, :], ALU.mult).then_inc(S["hid"], 1)

                def low(m, c):
                    v.wait_ge(S["hhi"], m * CS + c + 1)
                    need(v, S["down"], m * CS + c - RING + 1)
                    v.tensor_tensor(h_lo[c % RING][:, :], hid[c % 2], h_hi[c % RING][:, :].bitcast(F32),
                                    ALU.subtract).then_inc(S["hlo_odd" if c % 2 else "hlo_even"], 1)

                def stats_of_x(b, q, loads):
                    v.wait_ge(x_in[q], loads * 16)
                    alone(v)
                    for j in range(J):
                        o = v.bn_stats(st[:, 6 * j:6 * j + 6], res_tile(b, j))
                    o.then_inc(S["stats1"], 1)

                def moments_of_x(b, q):
                    v.wait_ge(S["stats1"], b + 1)
                    alone(v)
                    for j in range(J):
                        o = v.bn_aggr(mv[q][:, 2 * j:2 * j + 2], st[:, 6 * j:6 * j + 6])
                    o.then_inc(S["mv1"], 1)
                    v.wait_ge(S["mv1"], b + 1)
                    need(v, S["rs12"], b)
                    return v.tensor_scalar(ve[:, 0:J], var_of(mv[q]), LN_EPS, None, ALU.add)

                def normalise_x(b, q):
                    v.wait_ge(S["rs12"], b + 1)
                    need(v, S["aT_ps"], b)
                    for j in range(J):
                        o = v.tensor_scalar(tile_of(xn, j), res_tile(b, j), mean_of(mv[q], j), rs[:, j:j + 1],
                                            ALU.subtract, ALU.mult)
                    o.then_inc(S["xn"], 1)

                def weights_of(r):
                    v.wait_ge(S["tanh_w"], r + 1)
                    v.tensor_scalar(wts[:, ds(r * K * J, J)], tw[:, :], 0.5, 0.5, ALU.mult, ALU.add)
                    v.tensor_scalar(wts[:, ds(r * K * J + J, J)], tw[:, :], -0.5, 0.5, ALU.mult,
                                    ALU.add).then_inc(S["wts"], 1)

                def logit_distance(r):
                    v.wait_ge(S["dl"], r + 1)
                    v.wait_ge(S["rs12"], r + 5)
                    v.tensor_tensor(dls[:, :], dl[:, :], rs[:, J:2 * J], ALU.mult).then_inc(S["dls"], 1)

                def sum_slots(r):
                    v.wait_ge(S["picked"], r + 1)
                    v.tensor_reduce(slotf[:, :], picked[:, :].rearrange("p (c e) -> p c e", e=E), AX.X,
                                    ALU.add).then_inc(S["slotf"], 1)

                def write_slots(r, q):
                    v.wait_ge(S["slotf"], r + 1)
                    v.tensor_scalar(slot_now[q][:, :], slotf[:, :], float(SLOTS), None,
                                    ALU.add).then_inc(S["slot_now"], 1)
                    v.tensor_scalar(slots[:, ds(r * K * J, K * J)], slotf[:, :], float(SLOTS), None,
                                    ALU.add).then_inc(S["slots"], 1)

                def logits_in(r):
                    v.wait_ge(S["lg_ps"], r + 1)
                    v.tensor_copy(lg[:, :], kg_ps[:, 0:J * E]).then_inc(S["lg"], 1)

                def top_of(r):
                    v.wait_ge(S["lg"], r + 1)
                    alone(v)
                    for j in range(J):
                        o = v.max(top[:, 8 * j:8 * j + 8], lg[:, E * j:E * j + E])
                    o.then_inc(S["top"], 1)

                def top_experts(r):
                    v.wait_ge(S["top"], r + 1)
                    alone(v)
                    for j in range(J):
                        o = v.max_index(topi[:, 8 * j:8 * j + 8], top[:, 8 * j:8 * j + 8], lg[:, E * j:E * j + E])
                    o.then_inc(S["topi"], 1)
                    t3 = top[:, :].rearrange("p (j r) -> p j r", r=8)
                    v.tensor_tensor(dl[:, :], t3[:, :, 0], t3[:, :, 1], ALU.subtract).then_inc(S["dl"], 1)

                def one_hot(r):
                    v.wait_ge(S["topi"], r + 1)
                    i3 = topi[:, :].rearrange("p (j r) -> p j r", r=8)
                    for k in range(K):
                        o = v.tensor_tensor(je(oh[:, k * J * E:(k + 1) * J * E]), je(expert_id[:, :]),
                                            i3[:, :, k:k + 1].broadcast_to([P, J, E]), ALU.is_equal)
                    o.then_inc(S["oh"], 1)

                def chosen_experts(r):
                    v.wait_ge(S["oh"], r + 1)
                    v.tensor_tensor(mask[:, :], oh[:, 0:J * E], oh[:, J * E:], ALU.add).then_inc(S["mask"], 1)

                def slots_of(r):
                    v.wait_ge(S["mask"], r + 1)
                    v.tensor_reduce(newly[:, :], mask[:, :].rearrange("p (j e) -> p e j", e=E), AX.X,
                                    ALU.add).then_inc(S["newly"], 1)
                    v.wait_ge(S["rank_ps"], r + 1)
                    v.tensor_scalar(fits[:, :], kg_ps[:, 0:J * E], float(CAP), None, ALU.is_lt)
                    v.tensor_tensor(place[:, :], kg_ps[:, 0:J * E], expert_base[:, :],
                                    ALU.add).then_inc(S["place"], 1)
                    v.wait_ge(S["newly"], r + 1)
                    v.tensor_tensor(taken[:, :], taken[:, :], newly[:, :], ALU.add).then_inc(S["taken"], 1)
                    v.wait_ge(S["place"], r + 1)
                    v.tensor_tensor(placed[:, :], place[:, :], fits[:, :], ALU.mult).then_inc(S["placed"], 1)
                    v.wait_ge(S["taken"], r + 1)
                    v.tensor_copy(takenb[:, :], taken[:, :]).then_inc(S["takenb"], 1)
                    v.wait_ge(S["placed"], r + 1)
                    v.tensor_tensor(picked[:, :].rearrange("p (k c) -> p k c", k=K),
                                    placed[:, :].rearrange("p (o c) -> p o c", o=1).broadcast_to([P, K, J * E]),
                                    oh[:, :].rearrange("p (k c) -> p k c", k=K), ALU.mult).then_inc(S["picked"], 1)

                def output_weights():
                    v.wait_ge(S["setup_act"], 2)
                    v.tensor_tensor(wr_lo[:, :], wr[:, :], wr_hi[:, :].bitcast(F32), ALU.subtract).then_inc(S["setup_dve"], 1)
                    v.reduce_sum(wo_sum[:, :], wo_half[:, :], AX.X).then_inc(S["wo_sums"], 1)
                    v.reduce_sum(bo_sum[:, :], bo_row[:, :], AX.X).then_inc(S["wo_sums"], 1)
                    v.wait_ge(S["wo_sums"], 2)
                    v.scalar_tensor_tensor(out=wo_c[:, :], in0=wo_sum[:, 0:1].broadcast_to([P, H]), scalar=-1.0 / H,
                                           in1=wo_half[:, :], op0=ALU.mult, op1=ALU.add).then_inc(S["setup_dve"], 1)
                    v.scalar_tensor_tensor(out=bo_c[:, :], in0=bo_sum[:, 0:1].broadcast_to([1, H]), scalar=-1.0 / H,
                                           in1=bo_row[:, :], op0=ALU.mult, op1=ALU.add).then_inc(S["bo_centred"], 1)

                def step(h, i, q):
                    attend, project, route, share, ahead, moments, routed = stages(i)
                    n, r, m, c = i - 1, i - 2, h - 1, 4 * q
                    late = isinstance(i, int) and i >= B
                    opening = isinstance(i, int) and i < 2
                    if attend:
                        v.wait_ge(S["k_in"], i + 1)
                        v.tensor_reduce(kmax[:, :], kg_ps[:, :], AX.X, ALU.max, negate=True).then_inc(S["kmax"], 1)
                        v.wait_ge(S["kmax"], i + 1)
                        v.tensor_scalar(kbias[:, :], kmax[:, :], bqkv[:, 1:2], bqkv[:, 1:2], ALU.subtract,
                                        ALU.add).then_inc(S["kbias"], 1)
                    if routed:
                        logit_distance(r - 1)
                        low(m if q == 1 else m - 1, 2 if q == 1 else CS // 2 + 2)
                    if isinstance(i, int) and i > B:
                        low(m, 3)
                    if project:
                        v.wait_ge(S["oa"], n + 1)
                        v.wait_ge(S["tanh_g"], n + 1)
                        if isinstance(i, int) and i == 1:
                            v.wait_ge(S["s_lo_done"], 2)
                        v.scalar_tensor_tensor(out=u, in0=tg[1 - q][:, :], scalar=1.0, in1=oa,
                                               op0=ALU.add, op1=ALU.mult).then_inc(S["u"], 1)
                    if moments:
                        stats_of_x(i + 2, q, h + 2)
                    if route:
                        v.tensor_tensor(ms1[:, :], rs4[:, :], rs4[:, :], ALU.mult).then_inc(S["ms1"], 1)
                        v.wait_ge(S["ms1"], r + 1)
                        v.tensor_tensor(ms2[:, :], ms1[:, :], var_of(mv4), ALU.mult).then_inc(S["ms2"], 1)
                    if moments:
                        o = moments_of_x(i + 2, q)
                    if route:
                        v.wait_ge(S["ms2"], r + 1)
                        v.wait_ge(S["rs12"], i + 2)
                        o = v.tensor_scalar(ve[:, J:2 * J], ms2[:, :], RMS_EPS, None, ALU.add)
                    o.then_inc(S["ve12"], 1)
                    if isinstance(i, int) and i == 0:
                        output_weights()
                    if attend:
                        v.wait_ge(S["exp"], i + 1)
                        v.reciprocal(rksum[:, :], ksum[:, :]).then_inc(S["rksum"], 1)
                    if routed:
                        weights_of(r - 1)
                    if attend:
                        v.wait_ge(S["aT_ps"], i + 1)
                        v.tensor_copy(a_t[:, :], small_ps[:, 0:H]).then_inc(S["aT"], 1)
                    if opening:
                        normalise_x(i + 1, 1 - q)
                    if isinstance(i, int) and i == 2:
                        v.wait_ge(S["filled"], 16 * FILLS)
                    if share:
                        hidden(m, c)
                    if late and project:
                        low(m - 1, CS - 1)
                    if attend:
                        v.wait_ge(S["kv_ps"], i + 1)
                        v.scalar_tensor_tensor(out=kv[:, :], in0=small_ps[:, 0:H], scalar=rksum[:, 0:1],
                                               in1=bv_row[:, :], op0=ALU.mult, op1=ALU.add).then_inc(S["kvn"], 1)
                        v.wait_ge(S["kvn"], i + 1)
                        v.tensor_tensor_reduce(out=kvh[:, :], in0=kv[:, :], in1=head_mask[:, :], scale=1.0,
                                               scalar=0.0, op0=ALU.mult, op1=ALU.add,
                                               accum_out=kv_sum[:, 0:1]).then_inc(S["kvh"], 1)
                    if project:
                        v.wait_ge(S["ssq_y"], n + 1)
                        v.tensor_scalar(ve3[:, :], ssq_y[:, :], 1.0 / H, LN_EPS, ALU.mult,
                                        ALU.add).then_inc(S["ve3"], 1)
                    if attend:
                        v.wait_ge(S["kvh"], i + 1)
                        need(v, S["out_ps"], i)
                        v.scalar_tensor_tensor(out=kvm[:, :], in0=kv_sum[:, 0:1].broadcast_to([P, H]),
                                               scalar=-1.0 / H, in1=kvh[:, :], op0=ALU.mult,
                                               op1=ALU.add).then_inc(S["kvm"], 1)
                    if ahead and not opening:
                        normalise_x(i + 1, 1 - q)
                    if isinstance(i, int) and i == 0:
                        v.wait_ge(S["bo_hi"], 2)
                        v.tensor_tensor(bo_lo[:, :], bo_c[:, :], bo_hi[:, :].bitcast(F32),
                                        ALU.subtract).then_inc(S["setup_dve"], 1)
                        centre_sd()
                    if late and project:
                        logits_in(r)
                        top_of(r)
                    if project:
                        v.wait_ge(S["rs3"], n + 1)
                        for j in range(J):
                            o = v.scalar_tensor_tensor(out=res_tile(n, j), in0=tile_of(oy_ps, j), scalar=rs3[:, j:j + 1],
                                                       in1=res_tile(n, j), op0=ALU.mult, op1=ALU.add)
                        o.then_inc(S["res"], 1)
                    if route and not late:
                        logits_in(r)
                    if late and not project:
                        logits_in(r)
                        top_of(r)
                        top_experts(r)
                        one_hot(r)
                        chosen_experts(r)
                        slots_of(r)
                        sum_slots(r)
                        write_slots(r, q)
                    if share:
                        hidden(m, c + 1)
                    if project:
                        v.wait_ge(S["res"], n + 1)
                        alone(v)
                        for j in range(J):
                            o = v.bn_stats(st4[:, 6 * j:6 * j + 6], res_tile(n, j))
                        o.then_inc(S["st4"], 1)
                    if late and project:
                        top_experts(r)
                    if share:
                        low(m, c)
                    if project:
                        v.wait_ge(S["st4"], n + 1)
                        alone(v)
                        for j in range(J):
                            o = v.bn_aggr(mv4[:, 2 * j:2 * j + 2], st4[:, 6 * j:6 * j + 6])
                        o.then_inc(S["mv4"], 1)
                    if route and not late:
                        top_of(r)
                    if project:
                        v.wait_ge(S["mv4"], n + 1)
                        v.tensor_scalar(ve4[:, :], var_of(mv4), LN_EPS, None, ALU.add).then_inc(S["ve4"], 1)
                    if late and project:
                        one_hot(r)
                        chosen_experts(r)
                    if share:
                        hidden(m, c + 2)
                    if late and project:
                        slots_of(r)
                        sum_slots(r)
                        write_slots(r, q)
                    if route and not late:
                        top_experts(r)
                    if route and not late:
                        one_hot(r)
                    if attend:
                        v.wait_ge(S["ssq_o"], i + 1)
                        v.tensor_scalar(ve_o[:, :], ssq_o[:, :], 1.0 / H, LN_EPS, ALU.mult,
                                        ALU.add).then_inc(S["ve_o"], 1)
                    if route and not late:
                        chosen_experts(r)
                    if project:
                        v.wait_ge(S["rs4"], n + 1)
                        need(v, scattered[1 - q], SCATTERS * (h - 1 + q))
                        need(v, S["xfT_ps"], n - 1)
                        for j in range(J):
                            o = v.tensor_scalar(tile_of(xf[1 - q], j), res_tile(n, j), mean_of(mv4, j),
                                                rs4[:, j:j + 1], ALU.subtract, ALU.mult)
                        o.then_inc(S["xf"], 1)
                    if late:
                        low(m, c + 1)
                    if route and not late:
                        slots_of(r)
                    if share:
                        hidden(m, c + 3)
                    if route and not late:
                        sum_slots(r)
                    if attend:
                        v.wait_ge(S["rs_o"], i + 1)
                        need(v, S["onT_ps"], i)
                        if isinstance(i, int) and i == 0:
                            v.wait_ge(S["s_lo_done"], 1)
                        v.tensor_tensor(jh(on), jh(oy_ps[:, :]), over_features(rs_o[:, :]),
                                        ALU.mult).then_inc(S["on"], 1)
                    if route and not late:
                        write_slots(r, q)
                    if project:
                        v.wait_ge(S["xf_hi"], n + 1)
                        v.tensor_tensor(xf_lo[:, ds(n * N, N)], turn_ps[:, :], xf_hi[:, ds(n * N, N)].bitcast(F32),
                                        ALU.subtract).then_inc(S["xf_lo"], 1)

                v.wait_ge(S["ident"], 7)
                stats_of_x(0, 0, 1)
                moments_of_x(0, 0).then_inc(S["ve12"], 1)
                normalise_x(0, 0)
                v.wait_ge(S["wg_psum"], 1)
                v.tensor_copy(wg[:, :], small_ps[:, 0:H]).then_inc(S["wg_copied"], 1)
                v.tensor_scalar(bg_half[:, :], small_ps[:, H:H + 1], bg2[:, 0:1], 0.5, ALU.add,
                                ALU.mult).then_inc(S["bg_ready"], 1)
                stats_of_x(1, 1, 1)
                moments_of_x(1, 1).then_inc(S["ve12"], 1)
                steps(v.Fori, step)
                low(SHARED_1 - 1, CS - 2)
                low(SHARED_1 - 1, CS - 1)
                centre_rd(v, 0)
                logit_distance(B - 1)
                weights_of(B - 1)

            @block.tensor
            def _(pe):
                mm = nc.tensor.matmul

                def transposes(dst, src):
                    for j in range(J):
                        o = nc.tensor.transpose(dst[:, j * P:(j + 1) * P], src[:, j * P:(j + 1) * P], ident[:, :])
                    return o

                def product(dst, wa, a_hi, a_lo, start, stop):
                    mm(dst, s_lo[:, wa:wa + P], a_hi, start=start, stop=False)
                    mm(dst, s_hi[:, wa:wa + P], a_lo, start=False, stop=False)
                    return mm(dst, s_hi[:, wa:wa + P], a_hi, start=False, stop=stop)

                def gate(m, c):
                    need(pe, S["silu"], m * CS + c)
                    product(gate_ps[:, :], c * P, xf_hi[:, ds(m * N, N)], xf_lo[:, ds(m * N, N)], True,
                            True).then_inc(S["gate"], 1)

                def up(m, c):
                    need(pe, S["hid"], m * CS + c)
                    product(up_ps[:, :], IS + c * P, xf_hi[:, ds(m * N, N)], xf_lo[:, ds(m * N, N)], True,
                            True).then_inc(S["up"], 1)

                def down(m, c):
                    pe.wait_ge(S["hlo_odd" if c % 2 else "hlo_even"], m * (CS // 2) + c // 2 + 1)
                    if c == 0:
                        need(pe, S["yt"], m)
                    product(sy_ps[:, :], 2 * IS + c * P, h_hi[c % RING][:, :], h_lo[c % RING][:, :],
                            c == 0, c == CS - 1).then_inc(S["down"], 1)

                def down_behind(m, c):
                    if c >= LAG:
                        down(m, c - LAG)
                    elif not (isinstance(m, int) and m == 0):
                        down(m - 1, CS + c - LAG)

                def shared_rows(m):
                    pe.wait_ge(S["yt"], m + 1)
                    transposes(small_ps, y_t).then_inc(S["yr_ps"], 1)

                def turn_xn(b):
                    pe.wait_ge(S["xn"], b + 1)
                    need(pe, S["oa"], b - 1)
                    need(pe, S["xnT"], b)
                    transposes(turn_ps, xn).then_inc(S["xnT_ps"], 1)

                def logits(r, after):
                    pe.wait_ge(S["xf_lo"], r + 1)
                    need(pe, S["tanh_g"], after)
                    need(pe, S["place"], r)
                    hi, lo = xf_hi[:, ds(r * N, N)], xf_lo[:, ds(r * N, N)]
                    mm(kg_ps[0:E, :], wr_lo[:, :], hi, start=True, stop=False)
                    mm(kg_ps[0:E, :], wr_hi[:, :], lo, start=False, stop=False)
                    mm(kg_ps[0:E, :], wr_hi[:, :], hi, start=False, stop=True).then_inc(S["lgt_ps"], 1)

                def ranks(r):
                    pe.wait_ge(S["mask"], r + 1)
                    need(pe, S["takenb"], r)
                    rank, chosen = je(kg_ps[:, 0:J * E]), je(mask[:, :])
                    mm(rank, onesb[:, :], takenb[:, :].rearrange("p (o e) -> p o e", o=1).broadcast_to([P, J, E]),
                       start=True, stop=False, skip_group_check=True)
                    for j in range(J):
                        o = mm(rank, before[:, :], chosen[:, j:j + 1, :].broadcast_to([P, J, E]), start=False,
                               stop=(j == J - 1), skip_group_check=True)
                        if j < J - 1:
                            mm(rank[:, j + 1:J, :], identb[:, :],
                               chosen[:, j:j + 1, :].broadcast_to([P, J - 1 - j, E]),
                               start=False, stop=False, skip_group_check=True)
                    o.then_inc(S["rank_ps"], 1)

                def logits_in_rows(r):
                    pe.wait_ge(S["lgt"], r + 1)
                    alone(pe)
                    for j in range(J):
                        o = nc.tensor.transpose(kg_ps[:, j * E:(j + 1) * E], lgt[:, j * P:(j + 1) * P],
                                                ident[0:E, 0:E])
                    o.then_inc(S["lg_ps"], 1)

                def step(h, i, q):
                    attend, project, route, share, ahead, moments, routed = stages(i)
                    n, r, m, c = i - 1, i - 2, h - 1, 4 * q
                    later = not (isinstance(m, int) and m == 0)
                    late = isinstance(i, int) and i >= B
                    if attend:
                        pe.wait_ge(S["xnT"], i + 1)
                        need(pe, S["tanh_g"], i)
                        need(pe, S["place"], r)
                        mm(kg_ps[:, :], wqkv[:, H:2 * H], xn_t[:, :], start=True, stop=True).then_inc(S["k_in"], 1)
                        need(pe, S["silu_q"], i)
                        mm(q_ps[:, :], wqkv[:, 0:H], xn_t[:, :], start=True, stop=True).then_inc(S["q_in"], 1)
                    if isinstance(i, int) and i == 2:
                        pe.wait_ge(S["s_lo_done"], 3)
                        pe.wait_ge(S["xf_lo"], 1)
                    if isinstance(i, int) and i == 1:
                        pe.wait_ge(S["setup_dve"], 8)
                    if late:
                        gate(m, c)
                        up(m, c)
                    if project:
                        pe.wait_ge(S["on"], n + 1)
                        need(pe, S["xf_lo"], n)
                        transposes(turn_ps, on).then_inc(S["onT_ps"], 1)
                    if share and not late:
                        gate(m, c)
                        up(m, c)
                    if late:
                        logits(r, B)
                    if attend:
                        pe.wait_ge(S["exp"], i + 1)
                        need(pe, S["kvn"], i)
                        if share and q == 1 and later:
                            pe.wait_ge(S["yr"], m)
                        if isinstance(i, int) and i == 0:
                            pe.wait_ge(S["wg_copied"], 1)
                            pe.wait_ge(S["bg_ready"], 1)
                        transposes(small_ps, ek_t).then_inc(S["ekT_ps"], 1)
                        mm(kg_ps[:, :], wg[:, :], xn_t[:, :], start=True, stop=True).then_inc(S["g_in"], 1)
                    if project:
                        pe.wait_ge(S["u"], n + 1)
                        for part in (bo_lo, bo_hi):
                            mm(oy_ps[:, :], ones_r[:, :], part[:, :].rearrange("p (o h) -> p o h", o=1)
                               .broadcast_to([1, J, H]), start=(part is bo_lo), stop=False, skip_group_check=True)
                        for j in range(J):
                            o = mm(tile_of(oy_ps, j), u[:, j * P:(j + 1) * P], wo_c[:, :],
                                   start=False, stop=(j == J - 1), skip_group_check=True)
                        o.then_inc(S["y_ps"], 1)
                    if attend:
                        pe.wait_ge(S["ek"], i + 1)
                        for j in range(J):
                            o = mm(small_ps[:, 0:H], tile_of(xn, j), tile_of(ek, j), start=(j == 0),
                                   stop=(j == J - 1))
                        o.then_inc(S["aT_ps"], 1)
                    if route and not late:
                        logits(r, i + 1)
                    if attend:
                        pe.wait_ge(S["aT"], i + 1)
                        mm(small_ps[:, 0:H], a_t[:, :], wqkv[:, 2 * H:3 * H], start=True, stop=True)\
                            .then_inc(S["kv_ps"], 1)
                    if share:
                        down_behind(m, c)
                    if late:
                        logits_in_rows(r)
                    if share:
                        gate(m, c + 1)
                        up(m, c + 1)
                    if route and not late:
                        logits_in_rows(r)
                    if late and not project:
                        ranks(r)
                    if share:
                        down_behind(m, c + 1)
                    if ahead:
                        turn_xn(i + 1)
                    if share:
                        gate(m, c + 2)
                        up(m, c + 2)
                    if attend:
                        pe.wait_ge(S["kvm"], i + 1)
                        pe.wait_ge(S["silu_q"], i + 1)
                        if project:
                            pe.wait_ge(S["res"], n + 1)
                        for j in range(J):
                            o = mm(tile_of(oy_ps, j), q_t[:, j * P:(j + 1) * P], kvm[:, :], start=True, stop=True)
                        o.then_inc(S["out_ps"], 1)
                    if share:
                        down_behind(m, c + 2)
                        gate(m, c + 3)
                    if late and project:
                        ranks(r)
                    if share:
                        up(m, c + 3)
                    if route and not late:
                        ranks(r)
                    if share:
                        if q == 0 and later:
                            need(pe, S["kvn"], i + 1 if attend else B)
                            shared_rows(m - 1)
                        down_behind(m, c + 3)
                    if project:
                        pe.wait_ge(S["xf"], n + 1)
                        pe.wait_ge(S["oa"], n + 1)
                        if ahead:
                            pe.wait_ge(S["xnT"], i + 2)
                        transposes(turn_ps, xf[1 - q]).then_inc(S["xfT_ps"], 1)

                pe.wait_ge(S["ident"], 7)
                turn_xn(0)
                pe.wait_ge(S["weights"], 12 * 16)
                mm(small_ps[:, 0:H], g1[:, :], g2[:, :], start=True, stop=True)
                mm(small_ps[:, H:H + 1], g2[:, :], bg1[:, :], start=True, stop=True).then_inc(S["wg_psum"], 1)
                steps(pe.Fori, step)
                for c in range(CS - LAG, CS):
                    down(SHARED_1 - 1, c)
                shared_rows(SHARED_1 - 1)

        with ExitStack() as c2:
            def sb2(name, shape, dt=F32):
                return c2.enter_context(nc.sbuf_tensor(name, shape, dt))

            UPB = CR
            UPE = NBLK * CR
            W = CR * P
            w_hi = [sb2(f"w_hi{q}", [P, 3 * W], F32R) for q in range(2)]
            w_lo = [sb2(f"w_lo{q}", [P, 3 * W], F32R) for q in range(2)]
            xg = [sb2(f"xg{q}", [P, N]) for q in range(2)]
            xt_hi = [sb2(f"xt_hi{q}", [P, N], F32R) for q in range(2)]
            xt_lo = [sb2(f"xt_lo{q}", [P, N], F32R) for q in range(2)]
            gated = sb2("gated", [P, N])
            hid = [sb2(f"hid{q}", [P, N]) for q in range(2)]
            h_hi = [sb2(f"h_hi{q}", [P, N], F32R) for q in range(RING)]
            h_lo = [sb2(f"h_lo{q}", [P, N], F32R) for q in range(RING)]
            y_t = sb2("y_t", [P, N])
            y_rows = [sb2(f"y_rows{q}", [P, N]) for q in range(2)]
            gate_ps, up_ps, y_ps, xt_ps, yr_ps = bank[0:2], bank[2:4], bank[4:6], bank[6], bank[7]

            names = ("r_whi r_wlo r_xt_ps r_xt_hi r_xt_lo r_gate r_up r_silu r_hid r_hhi r_hlo r_down "
                     "r_yt r_yr_ps r_yr").split()
            R = {n: sem(n) for n in names}
            x_in = [sem(f"r_x_in{q}") for q in range(2)]
            y_out = [sem(f"r_y_out{q}") for q in range(2)]

            PAIR = 2 * NBLK
            assert PAIR % 2 == 0 and NBLK * CR % RING == 0

            def size(k):
                return BLOCKS[k % NBLK][1]

            block = c2.enter_context(nc.Block())

            @block.sync
            def _(sp):
                def load_w(e):
                    for dst, src in expert_loads(e):
                        sp.dma_start(dst, src).then_inc(w_in, 16)

                def slot_rows(t, e, k):
                    a, n = BLOCKS[k % NBLK]
                    return t[ds(e * CAP + a, n)].rearrange("(p j) h -> p (j h)", p=P)

                def load_x(e, k):
                    sp.dma_start(xg[k % 2][:, 0:size(k)], slot_rows(slot_x, e, k)).then_inc(x_in[k % 2], 16)

                def store_y(m, k, cold):
                    sp.wait_ge(R["r_yr"], m * PAIR + k + 1)
                    sp.dma_start(slot_rows(slot_y, m * 2 + k // NBLK, k), y_rows[k % 2][:, 0:size(k)])\
                      .then_inc(y_out[k % 2], 16)

                def pair(m, first, last):
                    for k in range(PAIR):
                        nxt = k + 2
                        if not (last and nxt >= PAIR):
                            sp.wait_ge(R["r_xt_ps"], m * PAIR + k + 1)
                            load_x(m * 2 + nxt // NBLK, nxt)
                        if k >= 3:
                            store_y(m, k - 3, first)
                        elif not first:
                            store_y(m - 1, PAIR + k - 3, first)
                        if k % NBLK == 0 and not (last and k >= NBLK):
                            sp.wait_ge(R["r_wlo"], m * 2 + k // NBLK + 1)
                            load_w(m * 2 + k // NBLK + 1)

                M = E // 2
                load_x(0, 0)
                load_x(0, 1)
                pair(0, True, False)
                with sp.Fori(1, M - 1) as m:
                    pair(m, False, False)
                pair(M - 1, False, True)
                for k in range(PAIR - 3, PAIR):
                    store_y(M - 1, k, False)
                for q in range(2):
                    sp.wait_ge(y_out[q], 16 * E * NBLK // 2)

            def unit(m, c):
                return m * (2 * UPE) + c

            @block.scalar
            def _(act):
                def split_w(m, q, warm):
                    act.wait_ge(w_centred, m * 2 + q + 1)
                    if warm:
                        act.wait_ge(R["r_down"], unit(m - 1, (q + 1) * UPE))
                    nc.scalar.activation(w_hi[q][:, :], raw[:, :], ACT.Copy).then_inc(R["r_whi"], 1)

                def split_x(m, k, warm):
                    b = m * PAIR + k
                    act.wait_ge(R["r_xt_ps"], b + 1)
                    if warm or k >= 2:
                        act.wait_ge(R["r_up"], unit(m, (k - 1) * CR))
                    nc.scalar.activation(xt_hi[k % 2][:, 0:size(k)], xt_ps[:, 0:size(k)],
                                         ACT.Copy).then_inc(R["r_xt_hi"], 1)

                def silu(m, c, warm):
                    act.wait_ge(R["r_gate"], unit(m, c) + 1)
                    if warm or c >= 1:
                        act.wait_ge(R["r_hid"], unit(m, c))
                    n = size(c // CR)
                    nc.scalar.activation(gated[:, 0:n], gate_ps[c % 2][:, 0:n], ACT.Silu).then_inc(R["r_silu"], 1)

                def high(m, c, warm):
                    act.wait_ge(R["r_hid"], unit(m, c) + 1)
                    if warm or c >= RING:
                        act.wait_ge(R["r_down"], unit(m, c) - RING + 1)
                    n = size(c % (2 * UPE) // CR)
                    nc.scalar.activation(h_hi[c % RING][:, 0:n], hid[c % 2][:, 0:n], ACT.Copy).then_inc(R["r_hhi"], 1)

                def y_copy(m, k, warm):
                    b = m * PAIR + k
                    act.wait_ge(R["r_down"], b * CR + CR)
                    if warm or k >= 1:
                        act.wait_ge(R["r_yr_ps"], b)
                    n = size(k)
                    nc.scalar.activation(y_t[:, 0:n], y_ps[k % 2][:, 0:n], ACT.Copy).then_inc(R["r_yt"], 1)

                def pair(m, first, last):
                    for c in range(2 * UPE):
                        k = c // CR
                        silu(m, c, not first)
                        if not (first and c < 1):
                            if c >= 1:
                                high(m, c - 1, not first)
                            else:
                                high(m - 1, 2 * UPE - 1, True)
                        if c % CR == 1 and not (last and k == PAIR - 1):
                            if k + 1 < PAIR:
                                split_x(m, k + 1, not first)
                            else:
                                split_x(m + 1, 0, True)
                        if c % CR == 3 and not (first and k == 0):
                            if k >= 1:
                                y_copy(m, k - 1, not first or k >= 3)
                            else:
                                y_copy(m - 1, PAIR - 1, True)
                        if c % UPE == UPE // 2:
                            q = c // UPE
                            if q == 0:
                                split_w(m, 1, not first)
                            elif not last:
                                split_w(m + 1, 0, True)

                M = E // 2
                split_w(0, 0, False)
                split_x(0, 0, False)
                pair(0, True, False)
                with act.Fori(1, M - 1) as m:
                    pair(m, False, False)
                pair(M - 1, False, True)
                high(M - 1, 2 * UPE - 1, True)
                y_copy(M - 1, PAIR - 1, True)

            @block.gpsimd
            def _(g):
                def low(m, c, warm):
                    g.wait_ge(R["r_hhi"], unit(m, c) + 1)
                    if warm or c >= RING:
                        g.wait_ge(R["r_down"], unit(m, c) - RING + 1)
                    n = size(c // CR)
                    g.tensor_tensor(h_lo[c % RING][:, 0:n], hid[c % 2][:, 0:n],
                                    h_hi[c % RING][:, 0:n].bitcast(F32), ALU.subtract).then_inc(R["r_hlo"], 1)

                for c in range(2 * UPE):
                    low(0, c, False)
                with g.Fori(1, E // 2) as m:
                    for c in range(2 * UPE):
                        low(m, c, True)

            @block.vector
            def _(v):
                def split_w(m, q, warm):
                    v.wait_ge(R["r_whi"], m * 2 + q + 1)
                    v.tensor_tensor(w_lo[q][:, :], raw[:, :], w_hi[q][:, :].bitcast(F32),
                                    ALU.subtract).then_inc(R["r_wlo"], 1)

                def split_x(m, k):
                    b = m * PAIR + k
                    v.wait_ge(R["r_xt_hi"], b + 1)
                    v.tensor_tensor(xt_lo[k % 2][:, 0:size(k)], xt_ps[:, 0:size(k)],
                                    xt_hi[k % 2][:, 0:size(k)].bitcast(F32), ALU.subtract).then_inc(R["r_xt_lo"], 1)

                def hidden(m, c, warm):
                    v.wait_ge(R["r_silu"], unit(m, c) + 1)
                    v.wait_ge(R["r_up"], unit(m, c) + 1)
                    if warm or c >= 2:
                        v.wait_ge(R["r_hlo"], unit(m, c) - 1)
                    n = size(c // CR)
                    v.tensor_tensor(hid[c % 2][:, 0:n], gated[:, 0:n], up_ps[c % 2][:, 0:n],
                                    ALU.mult).then_inc(R["r_hid"], 1)

                def y_copy(m, k, warm):
                    b = m * PAIR + k
                    v.wait_ge(R["r_yr_ps"], b + 1)
                    if warm or k >= 2:
                        v.wait_ge(y_out[k % 2], (m * (PAIR // 2) + k // 2) * 16)
                    n = size(k)
                    v.tensor_copy(y_rows[k % 2][:, 0:n], yr_ps[:, 0:n]).then_inc(R["r_yr"], 1)

                def pair(m, first, last):
                    for c in range(2 * UPE):
                        k = c // CR
                        hidden(m, c, not first)
                        if c % CR == 1 and not (last and k == PAIR - 1):
                            if k + 1 < PAIR:
                                split_x(m, k + 1)
                            else:
                                split_x(m + 1, 0)
                        if c % CR == 2 and not (first and k < 2):
                            if k >= 2:
                                y_copy(m, k - 2, not first)
                            else:
                                y_copy(m - 1, PAIR - 2 + k, True)
                        if c % UPE in (CR - 1, UPE // 2):
                            work = (lambda m, q: centre_rd(v, m * 2 + q)) if c % UPE == CR - 1 else lambda m, q: split_w(m, q, True)
                            if c < UPE:
                                work(m, 1)
                            elif not last:
                                work(m + 1, 0)

                M = E // 2
                split_w(0, 0, False)
                split_x(0, 0)
                pair(0, True, False)
                with v.Fori(1, M - 1) as m:
                    pair(m, False, False)
                pair(M - 1, False, True)
                y_copy(M - 1, PAIR - 2, True)
                y_copy(M - 1, PAIR - 1, True)

            @block.tensor
            def _(pe):
                mm = nc.tensor.matmul

                def x_in_t(m, k, warm):
                    n = size(k)
                    half = m * (PAIR // 2) + k // 2
                    pe.wait_ge(x_in[k % 2], half * 16 + 16)
                    if warm or k >= 1:
                        pe.wait_ge(R["r_xt_lo"], m * PAIR + k)
                    for j in range(n // P):
                        o = nc.tensor.transpose(xt_ps[:, j * P:(j + 1) * P], xg[k % 2][:, j * P:(j + 1) * P],
                                                ident[:, :])
                    o.then_inc(R["r_xt_ps"], 1)

                def product(dst, q, wa, a_hi, a_lo, start, stop):
                    mm(dst, w_lo[q][:, wa:wa + P], a_hi, start=start, stop=False)
                    mm(dst, w_hi[q][:, wa:wa + P], a_lo, start=False, stop=False)
                    return mm(dst, w_hi[q][:, wa:wa + P], a_hi, start=False, stop=stop)

                def gate_up(m, c, warm):
                    k, q = c // CR, c // UPE
                    n = size(k)
                    if c % CR == 0:
                        pe.wait_ge(R["r_xt_lo"], m * PAIR + k + 1)
                    if c % UPE == 0:
                        pe.wait_ge(R["r_wlo"], m * 2 + q + 1)
                    if warm or c >= 2:
                        pe.wait_ge(R["r_silu"], unit(m, c) - 1)
                    a = (xt_hi[k % 2][:, 0:n], xt_lo[k % 2][:, 0:n])
                    wa = (c % CR) * P
                    product(gate_ps[c % 2][:, 0:n], q, wa, *a, True, True).then_inc(R["r_gate"], 1)
                    if warm or c >= 2:
                        pe.wait_ge(R["r_hid"], unit(m, c) - 1)
                    product(up_ps[c % 2][:, 0:n], q, W + wa, *a, True, True).then_inc(R["r_up"], 1)

                def down(m, c, warm):
                    k, q = c // CR, c // UPE
                    n = size(k)
                    pe.wait_ge(R["r_hlo"], unit(m, c) + 1)
                    if c % CR == 0 and (warm or k >= 2):
                        pe.wait_ge(R["r_yt"], m * PAIR + k - 1)
                    product(y_ps[k % 2][:, 0:n], q, 2 * W + (c % CR) * P, h_hi[c % RING][:, 0:n],
                            h_lo[c % RING][:, 0:n], c % CR == 0, c % CR == CR - 1).then_inc(R["r_down"], 1)

                def y_in_rows(m, k, warm):
                    b = m * PAIR + k
                    pe.wait_ge(R["r_yt"], b + 1)
                    if warm or k >= 1:
                        pe.wait_ge(R["r_yr"], b)
                    for j in range(size(k) // P):
                        o = nc.tensor.transpose(yr_ps[:, j * P:(j + 1) * P], y_t[:, j * P:(j + 1) * P],
                                                ident[:, :])
                    o.then_inc(R["r_yr_ps"], 1)

                def pair(m, first, last):
                    U = 2 * UPE
                    for c in range(U):
                        k = c // CR
                        gate_up(m, c, not first)
                        if c % CR == 0 and not (last and k == PAIR - 1):
                            if k + 1 < PAIR:
                                x_in_t(m, k + 1, True)
                            else:
                                x_in_t(m + 1, 0, True)
                        if c >= LAG:
                            down(m, c - LAG, not first)
                        elif not first:
                            down(m - 1, U + c - LAG, True)
                        if c % CR == 1 and not (first and k < 2):
                            if k >= 2:
                                y_in_rows(m, k - 2, True)
                            else:
                                y_in_rows(m - 1, PAIR - 2 + k, True)

                M = E // 2
                x_in_t(0, 0, False)
                pair(0, True, False)
                with pe.Fori(1, M - 1) as m:
                    pair(m, False, False)
                pair(M - 1, False, True)
                for c in range(2 * UPE - LAG, 2 * UPE):
                    down(M - 1, c, True)
                y_in_rows(M - 1, PAIR - 2, True)
                y_in_rows(M - 1, PAIR - 1, True)

        with ExitStack() as c3:
            def sb3(name, shape, dt=F32):
                return c3.enter_context(nc.sbuf_tensor(name, shape, dt))

            HB = B // 2
            gated = [sb3(f"t_gated{q}", [P, N]) for q in range(2)]
            hid = [sb3(f"t_hid{q}", [P, N]) for q in range(2)]
            h_hi = [sb3(f"t_h_hi{q}", [P, N], F32R) for q in range(RING)]
            h_lo = [sb3(f"t_h_lo{q}", [P, N], F32R) for q in range(RING)]
            y_t = sb3("t_y_t", [P, N])
            KEPT, FRESH = 0, 1
            routed = [[sb3(f"routed{w}{k}", [P, N]) for k in range(K)] for w in range(2)]
            idx = [sb3(f"idx{w}", [P, K * J], U32) for w in range(2)]
            z = [sb3(f"z{w}", [P, N]) for w in range(2)]
            squares = sb3("t_squares", [P, N])
            ssq = [sb3(f"ssq{w}", [P, J]) for w in range(2)]
            ve = sb3("t_ve", [P, 2 * J])
            rs = sb3("t_rs", [P, 2 * J])
            fin = [sb3(f"fin{w}", [P, N]) for w in range(2)]
            gate_ps, up_ps, y_ps, yr_ps = bank[0:2], bank[2:4], bank[4], bank[6]

            names = ("t_ones t_gate t_up t_silu t_hid t_hhi t_hlo t_down "
                     "t_yt t_yr_ps t_ve t_rs").split()
            Q = {n: sem(n) for n in names}
            idx_set, gathered, z_first, z_done, ssq_done, fin_done, stored = (
                [sem(f"t_{n}{w}") for w in range(2)]
                for n in "idx gathered z_first z_done ssq fin stored".split())
            GATHERS = 16 * K * J
            tile_of = lambda t, j: t[:, j * H:(j + 1) * H]
            batch = (lambda g: g, lambda g: g + HB)

            block = c3.enter_context(nc.Block())

            @block.sync
            def _(sp):
                with sp.Fori(0, HB) as g:
                    for w in range(2):
                        sp.wait_ge(fin_done[w], g + 1)
                        sp.dma_start(out[ds(batch[w](g), 1)].rearrange("b (p j) h -> p (b j h)", p=P), fin[w][:, :])\
                          .then_inc(stored[w], 16)
                for w in range(2):
                    sp.wait_ge(stored[w], 16 * HB)

            @block.scalar
            def _(act):
                def copy(dst, src):
                    return nc.scalar.activation(dst, src, ACT.Copy)

                def silu(g, c):
                    act.wait_ge(Q["t_gate"], g * CS + c + 1)
                    need(act, Q["t_hid"], g * CS + c - 1)
                    nc.scalar.activation(gated[c % 2][:, :], gate_ps[c % 2][:, :], ACT.Silu).then_inc(Q["t_silu"], 1)

                def high(g, c):
                    act.wait_ge(Q["t_hid"], g * CS + c + 1)
                    need(act, Q["t_down"], g * CS + c - RING + 1)
                    copy(h_hi[c % RING][:, :], hid[c % 2][:, :]).then_inc(Q["t_hhi"], 1)

                def y_copy(g):
                    act.wait_ge(Q["t_down"], g * CS + CS)
                    need(act, Q["t_yr_ps"], g)
                    copy(y_t[:, :], y_ps[:, :]).then_inc(Q["t_yt"], 1)

                def squares_of(w, g):
                    act.wait_ge(z_done[w], g + 1)
                    for j in range(J):
                        o = nc.scalar.activation(tile_of(squares, j), tile_of(z[w], j), ACT.Square,
                                                 accum_out=ssq[w][:, j:j + 1])
                    o.then_inc(ssq_done[w], 1)

                def step(g, first):
                    for c in range(CS):
                        silu(g, c)
                        if c >= 1:
                            high(g, c - 1)
                        elif not first:
                            high(g - 1, CS - 1)
                        if c == LAG - 1 and not first:
                            y_copy(g - 1)
                        if c == 1 and not first:
                            squares_of(KEPT, g - 1)
                        if c == CS - 2 and not first:
                            squares_of(FRESH, g - 1)

                step(0, True)
                step(1, False)
                with act.Fori(2, HB) as g:
                    step(g, False)
                high(HB - 1, CS - 1)
                squares_of(KEPT, HB - 1)
                y_copy(HB - 1)
                squares_of(FRESH, HB - 1)

            @block.gpsimd
            def _(gp):
                def gather(w, g, cs):
                    for c in cs:
                        gp.indirect_dma_start(out=tile_of(routed[w][c // J], c % J), out_offset=None, in_=slot_y,
                                              in_offset=bass.IndirectOffsetOnAxis(ap=idx[w][:, c:c + 1], axis=0),
                                              bounds_check=SLOTS, oob_is_err=False).then_inc(gathered[w], 16)

                def powers(n, part=slice(0, 2 * J)):
                    gp.wait_ge(Q["t_ve"], n)
                    gp.tensor_tensor(rs[:, part], ve[:, part], mhalf[:, part], ALU.pow).then_inc(Q["t_rs"], 1)

                def step(g, first):
                    for w in range(2):
                        gp.wait_ge(idx_set[w], g + 1)
                        if not first:
                            gp.wait_ge(z_done[w], g)
                        alone(gp)
                        gather(w, g, range(0, 2))
                        if w == KEPT and not first:
                            powers(g)
                        gather(w, g, range(2, K * J))

                step(0, True)
                with gp.Fori(1, HB) as g:
                    step(g, False)
                powers(HB)
                powers(HB + 1, slice(FRESH * J, FRESH * J + J))

            @block.vector
            def _(v):
                def index(w, g):
                    need(v, gathered[w], g * GATHERS)
                    v.tensor_copy(idx[w][:, :], slots[:, ds(batch[w](g) * K * J, K * J)]).then_inc(idx_set[w], 1)

                def hidden(g, c):
                    v.wait_ge(Q["t_silu"], g * CS + c + 1)
                    v.wait_ge(Q["t_up"], g * CS + c + 1)
                    need(v, Q["t_hlo"], g * CS + c - 1)
                    v.tensor_tensor(hid[c % 2][:, :], gated[c % 2][:, :], up_ps[c % 2][:, :],
                                    ALU.mult).then_inc(Q["t_hid"], 1)

                def low(g, c):
                    v.wait_ge(Q["t_hhi"], g * CS + c + 1)
                    need(v, Q["t_down"], g * CS + c - RING + 1)
                    v.tensor_tensor(h_lo[c % RING][:, :], hid[c % 2][:, :], h_hi[c % RING][:, :].bitcast(F32),
                                    ALU.subtract).then_inc(Q["t_hlo"], 1)

                def mix_first(w, g):
                    v.wait_ge(gathered[w], g * GATHERS + GATHERS)
                    if w == FRESH:
                        v.wait_ge(Q["t_yr_ps"], g + 1)
                    need(v, fin_done[w], g)
                    for j in range(J):
                        part = tile_of(yr_ps, j) if w == FRESH else shared[:, ds(g * N + j * H, H)]
                        o = v.scalar_tensor_tensor(out=tile_of(z[w], j), in0=tile_of(routed[w][0], j),
                                                   scalar=wts[:, ds(batch[w](g) * K * J + j, 1)], in1=part,
                                                   op0=ALU.mult, op1=ALU.add)
                    o.then_inc(z_first[w], 1)

                def mix_second(w, g):
                    v.wait_ge(z_first[w], g + 1)
                    alone(v)
                    for j in range(J):
                        o = v.scalar_tensor_tensor(out=tile_of(z[w], j), in0=tile_of(routed[w][1], j),
                                                   scalar=wts[:, ds(batch[w](g) * K * J + J + j, 1)],
                                                   in1=tile_of(z[w], j), op0=ALU.mult, op1=ALU.add)
                    o.then_inc(z_done[w], 1)

                def variance(w, g):
                    v.wait_ge(ssq_done[w], g + 1)
                    return v.tensor_scalar(ve[:, w * J:(w + 1) * J], ssq[w][:, :], 1.0 / H, LN_EPS, ALU.mult, ALU.add)

                def final(w, g, powers):
                    v.wait_ge(Q["t_rs"], powers)
                    need(v, stored[w], g * 16)
                    alone(v)
                    for j in range(J):
                        o = v.scalar_tensor_tensor(out=tile_of(fin[w], j), in0=tile_of(z[w], j),
                                                   scalar=rs[:, w * J + j:w * J + j + 1],
                                                   in1=res[:, ds(batch[w](g) * N + j * H, H)],
                                                   op0=ALU.mult, op1=ALU.add)
                    o.then_inc(fin_done[w], 1)

                def step(g, first, second, last):
                    for c in range(CS):
                        hidden(g, c)
                        if c >= 1:
                            low(g, c - 1)
                        elif not first:
                            low(g - 1, CS - 1)
                        if c == 0 and first:
                            index(FRESH, g)
                        if c == 1 and not first:
                            o = variance(KEPT, g - 1)
                            if not second:
                                o = variance(FRESH, g - 2)
                            o.then_inc(Q["t_ve"], 1)
                        if c == 3 and not first:
                            index(FRESH, g)
                            if not second:
                                final(FRESH, g - 2, g)
                            mix_first(FRESH, g - 1)
                        if c == 4 and not first:
                            mix_second(FRESH, g - 1)
                        if c == 5 and not first:
                            final(KEPT, g - 1, g)
                        if c == CS - 2:
                            mix_first(KEPT, g)
                            if not last:
                                index(KEPT, g + 1)
                        if c == CS - 1:
                            mix_second(KEPT, g)

                index(KEPT, 0)
                v.memset(ve[:, :], 1.0).then_inc(Q["t_ones"], 1)
                step(0, True, False, False)
                step(1, False, True, False)
                with v.Fori(2, HB - 1) as g:
                    step(g, False, False, False)
                step(HB - 1, False, False, True)
                low(HB - 1, CS - 1)
                variance(KEPT, HB - 1)
                variance(FRESH, HB - 2).then_inc(Q["t_ve"], 1)
                final(FRESH, HB - 2, HB)
                mix_first(FRESH, HB - 1)
                mix_second(FRESH, HB - 1)
                final(KEPT, HB - 1, HB)
                variance(FRESH, HB - 1).then_inc(Q["t_ve"], 1)
                final(FRESH, HB - 1, HB + 1)

            @block.tensor
            def _(pe):
                mm = nc.tensor.matmul

                def product(dst, wa, a_hi, a_lo, start, stop):
                    mm(dst, s_lo[:, wa:wa + P], a_hi, start=start, stop=False)
                    mm(dst, s_hi[:, wa:wa + P], a_lo, start=False, stop=False)
                    return mm(dst, s_hi[:, wa:wa + P], a_hi, start=False, stop=stop)

                def gate_up(g, c):
                    b = batch[FRESH](g)
                    need(pe, Q["t_silu"], g * CS + c - 1)
                    a = (xf_hi[:, ds(b * N, N)], xf_lo[:, ds(b * N, N)])
                    product(gate_ps[c % 2][:, :], c * P, *a, True, True).then_inc(Q["t_gate"], 1)
                    need(pe, Q["t_hid"], g * CS + c - 1)
                    product(up_ps[c % 2][:, :], IS + c * P, *a, True, True).then_inc(Q["t_up"], 1)

                def down(g, c):
                    pe.wait_ge(Q["t_hlo"], g * CS + c + 1)
                    if c == 0:
                        need(pe, Q["t_yt"], g)
                    product(y_ps[:, :], 2 * IS + c * P, h_hi[c % RING][:, :], h_lo[c % RING][:, :],
                            c == 0, c == CS - 1).then_inc(Q["t_down"], 1)

                def y_in_rows(g):
                    pe.wait_ge(Q["t_yt"], g + 1)
                    need(pe, z_first[FRESH], g)
                    for j in range(J):
                        o = nc.tensor.transpose(yr_ps[:, j * P:(j + 1) * P], y_t[:, j * P:(j + 1) * P], ident[:, :])
                    o.then_inc(Q["t_yr_ps"], 1)

                def step(g, first):
                    for c in range(CS):
                        gate_up(g, c)
                        if c >= LAG:
                            down(g, c - LAG)
                        elif not first:
                            down(g - 1, CS + c - LAG)
                        if c == LAG and not first:
                            y_in_rows(g - 1)

                step(0, True)
                step(1, False)
                with pe.Fori(2, HB) as g:
                    step(g, False)
                for c in range(CS - LAG, CS):
                    down(HB - 1, c)
                y_in_rows(HB - 1)


def kernel(**inputs):
    import numpy as np
    import concourse.bacc as bacc
    from concourse.bass_utils import run_bass_kernel_spmd

    a = {n: np.ascontiguousarray(v) for n, v in inputs.items()}
    arrays = {
        "x": a["L0_attn_x"],
        "w_qkv_t": np.ascontiguousarray(a["L0_attn_w_qkv"].T),
        "b_qkv": a["L0_attn_b_qkv"],
        "b_qkv_t": np.ascontiguousarray(a["L0_attn_b_qkv"].reshape(3, H).T),
        "w_g1": a["L0_attn_w_g1"],
        "b_g1": a["L0_attn_b_g1"],
        "w_g2_t": np.ascontiguousarray(a["L0_attn_w_g2"].T),
        "b_g2": a["L0_attn_b_g2"],
        "w_out_t": np.ascontiguousarray(a["L0_attn_w_out"].T),
        "b_out": a["L0_attn_b_out"],
        "ln_g": a["L0_attn_ln_g"],
        "ln_b": a["L0_attn_ln_b"],
        "router_t": np.ascontiguousarray(a["L0_ffn_router_w"].T),
        "rg": a["L0_ffn_rg"],
        "ru": a["L0_ffn_ru"],
        "rd": a["L0_ffn_rd"],
        "sg": a["L0_ffn_sg"],
        "su": a["L0_ffn_su"],
        "sd": a["L0_ffn_sd"],
    }
    nc = bacc.Bacc("TRN2", target_bir_lowering=False, num_devices=1)
    args = [nc.dram_tensor(n, v.shape, F32, kind="ExternalInput").ap() for n, v in arrays.items()]
    out = nc.dram_tensor("out", arrays["x"].shape, F32, kind="ExternalOutput").ap()
    build(nc, *args, out)
    r = run_bass_kernel_spmd(nc, [arrays], core_ids=[0])
    return r.results[0]["out"]
```
